# Optimizing a Trainium2 kernel written in Bass

```python
import numpy as np
import jax
import jax.numpy as jnp

def _softmax(x, axis=-1):
    return jax.nn.softmax(x, axis=axis)

def _gelu(x):
    return jax.nn.gelu(x, approximate=True)

def _silu(x):
    return jax.nn.silu(x)

def _sigmoid(x):
    return jax.nn.sigmoid(x)

def _layernorm(x, axis=-1, eps=1e-05):
    m = jnp.mean(x, axis=axis, keepdims=True)
    v = jnp.var(x, axis=axis, keepdims=True)
    return (x - m) / jnp.sqrt(v + eps)

def _scatter_add(tgt, idx, src, axis=0):
    return tgt.at[idx].add(src)

def _segment_sum(src, seg, n):
    return jax.ops.segment_sum(src, seg, n)
kernel_name = 'mk_xattn_ffn_d1_seqx_r8_8bc891'

def setup_inputs(seed: int=0):
    np.random.seed(seed)
    _w = jnp.asarray

    def _rec_inputs():
        import jax
        import jax.numpy as jnp
        _rk = jax.random.key(seed)
        x = -0.0002928 + 1 * jax.random.normal(jax.random.fold_in(_rk, 1), (128, 64, 128), jnp.float32)
        _lenS = 64 - jax.random.randint(jax.random.fold_in(_rk, 7), (128,), 0, max(1, 64 // 4) + 1, jnp.int32)
        _lenS2 = 64 - jax.random.randint(jax.random.fold_in(_rk, 8), (128,), 0, max(1, 64 // 4) + 1, jnp.int32)
        _ctx_1024P = jax.random.normal(jax.random.fold_in(_rk, 11), (128, 16, 128), jnp.float32)
        _ctx_1024c = jax.random.dirichlet(jax.random.fold_in(_rk, 511), 0.3 * jnp.ones((16,), jnp.float32), (128, 64))
        _ctx_1024t = jnp.einsum('bsk,bkd->bsd', _ctx_1024c, _ctx_1024P)
        _ctx_1024t = _ctx_1024t * jax.lax.rsqrt(jnp.mean(jnp.square(_ctx_1024t)) + 1e-12) * 0.953939
        ctx_1024 = -1.39393e-06 + 0.999914 * (_ctx_1024t + 0.3 * jax.random.normal(jax.random.fold_in(_rk, 611), (128, 64, 128), jnp.float32))
        fside_BxSx4_0 = jax.random.uniform(jax.random.fold_in(_rk, 12), (128, 64, 4), jnp.float32, 0.0, 0.999884)
        return (x, ctx_1024, fside_BxSx4_0)
    x, ctx_1024, fside_BxSx4_0 = _rec_inputs()

    def _L0_xattn_setup():
        import jax, jax.numpy as jnp
        import numpy as np
        D_MODEL = 128
        H = 16
        D_K = 64
        D_V = 64
        D_G = D_MODEL // H
        WAVE_LEN = 1000.0
        B = 8
        N = 64

        def box_relational_embedding(boxes, dim_g=D_G):
            x_min, y_min, x_max, y_max = jnp.split(boxes, 4, axis=-1)
            cx = (x_min + x_max) * 0.5
            cy = (y_min + y_max) * 0.5
            w = x_max - x_min + 1.0
            h = y_max - y_min + 1.0
            delta_x = jnp.log(jnp.clip(jnp.abs((cx - jnp.swapaxes(cx, 1, 2)) / w), 0.001, None))
            delta_y = jnp.log(jnp.clip(jnp.abs((cy - jnp.swapaxes(cy, 1, 2)) / h), 0.001, None))
            delta_w = jnp.log(w / jnp.swapaxes(w, 1, 2))
            delta_h = jnp.log(h / jnp.swapaxes(h, 1, 2))
            pos = jnp.stack([delta_x, delta_y, delta_w, delta_h], axis=-1)
            n_freq = dim_g // 8
            feat_range = jnp.arange(n_freq, dtype=jnp.float32)
            dim_mat = 1.0 / WAVE_LEN ** (feat_range / n_freq)
            mul = (100.0 * pos)[..., None] * dim_mat
            b, n = (pos.shape[0], pos.shape[1])
            mul = mul.reshape(b, n, n, 4 * n_freq)
            return jnp.concatenate([jnp.sin(mul), jnp.cos(mul)], axis=-1)
        key = jax.random.key(seed)
        ks = jax.random.split(key, 12)
        s = 0.02
        inp = {'queries': jax.random.normal(ks[0], (B, N, D_MODEL), jnp.float32), 'keys': jax.random.normal(ks[1], (B, N, D_MODEL), jnp.float32), 'values': jax.random.normal(ks[2], (B, N, D_MODEL), jnp.float32), 'boxes': jax.random.uniform(ks[3], (B, N, 4), jnp.float32), 'Wq': jax.random.normal(ks[4], (H * D_K, D_MODEL), jnp.float32) * s, 'bq': jnp.zeros((H * D_K,), jnp.float32), 'Wk': jax.random.normal(ks[5], (H * D_K, D_MODEL), jnp.float32) * s, 'bk': jnp.zeros((H * D_K,), jnp.float32), 'Wv': jax.random.normal(ks[6], (H * D_V, D_MODEL), jnp.float32) * s, 'bv': jnp.zeros((H * D_V,), jnp.float32), 'Wo': jax.random.normal(ks[7], (D_MODEL, H * D_V), jnp.float32) * s, 'bo': jnp.zeros((D_MODEL,), jnp.float32), 'Wg': jax.random.normal(ks[8], (H, D_G), jnp.float32) * s, 'bg': jnp.zeros((H,), jnp.float32)}
        return inp
    _L0_xattn_all = _L0_xattn_setup()
    _L0_xattn_in = {k: v for k, v in _L0_xattn_all.items() if k in ('Wq', 'bq', 'Wk', 'bk', 'Wv', 'bv', 'Wo', 'bo', 'Wg', 'bg')}
    del _L0_xattn_all

    def _L0_ffn_setup():
        import jax, jax.numpy as jnp
        import numpy as np
        H = 128
        I = 4 * H
        E = 8
        K = 2
        B, S = (2, 128)
        STD = 0.02 / np.sqrt(H)
        key = jax.random.key(seed)
        ks = jax.random.split(key, 8)
        x = jax.random.normal(ks[0], (B, S, H), dtype=jnp.float32)
        gate_w = jax.random.normal(ks[1], (H, E), dtype=jnp.float32) * STD
        bias = jnp.zeros((E,), dtype=jnp.float32)
        up_w = jax.random.normal(ks[2], (E, H, I), dtype=jnp.float32) * STD
        up_b = jnp.zeros((E, I), dtype=jnp.float32)
        down_w = jax.random.normal(ks[3], (E, I, H), dtype=jnp.float32) * STD
        down_b = jnp.zeros((E, H), dtype=jnp.float32)
        sw_up = jax.random.normal(ks[4], (H, I), dtype=jnp.float32) * STD
        sb_up = jnp.zeros((I,), dtype=jnp.float32)
        sw_down = jax.random.normal(ks[5], (I, H), dtype=jnp.float32) * STD
        sb_down = jnp.zeros((H,), dtype=jnp.float32)
        return {'x': x, 'gate_w': gate_w, 'bias': bias, 'up_w': up_w, 'up_b': up_b, 'down_w': down_w, 'down_b': down_b, 'sw_up': sw_up, 'sb_up': sb_up, 'sw_down': sw_down, 'sb_down': sb_down}
    _L0_ffn_all = _L0_ffn_setup()
    _L0_ffn_in = {k: v for k, v in _L0_ffn_all.items() if k in ('gate_w', 'bias', 'up_w', 'up_b', 'down_w', 'down_b', 'sw_up', 'sb_up', 'sw_down', 'sb_down')}
    del _L0_ffn_all
    return {'x': x, 'ctx_1024': ctx_1024, 'fside_BxSx4_0': fside_BxSx4_0, 'L0_xattn_Wq': _L0_xattn_in['Wq'], 'L0_xattn_bq': _L0_xattn_in['bq'], 'L0_xattn_Wk': _L0_xattn_in['Wk'], 'L0_xattn_bk': _L0_xattn_in['bk'], 'L0_xattn_Wv': _L0_xattn_in['Wv'], 'L0_xattn_bv': _L0_xattn_in['bv'], 'L0_xattn_Wo': _L0_xattn_in['Wo'], 'L0_xattn_bo': _L0_xattn_in['bo'], 'L0_xattn_Wg': _L0_xattn_in['Wg'], 'L0_xattn_bg': _L0_xattn_in['bg'], 'L0_ffn_gate_w': _L0_ffn_in['gate_w'], 'L0_ffn_bias': _L0_ffn_in['bias'], 'L0_ffn_up_w': _L0_ffn_in['up_w'], 'L0_ffn_up_b': _L0_ffn_in['up_b'], 'L0_ffn_down_w': _L0_ffn_in['down_w'], 'L0_ffn_down_b': _L0_ffn_in['down_b'], 'L0_ffn_sw_up': _L0_ffn_in['sw_up'], 'L0_ffn_sb_up': _L0_ffn_in['sb_up'], 'L0_ffn_sw_down': _L0_ffn_in['sw_down'], 'L0_ffn_sb_down': _L0_ffn_in['sb_down']}

def reference(x, ctx_1024, fside_BxSx4_0, L0_xattn_Wq, L0_xattn_bq, L0_xattn_Wk, L0_xattn_bk, L0_xattn_Wv, L0_xattn_bv, L0_xattn_Wo, L0_xattn_bo, L0_xattn_Wg, L0_xattn_bg, L0_ffn_gate_w, L0_ffn_bias, L0_ffn_up_w, L0_ffn_up_b, L0_ffn_down_w, L0_ffn_down_b, L0_ffn_sw_up, L0_ffn_sb_up, L0_ffn_sw_down, L0_ffn_sb_down):
    import jax
    import jax.numpy as jnp

    def _L0_xattn_ref(queries, keys, values, boxes, Wq, bq, Wk, bk, Wv, bv, Wo, bo, Wg, bg):
        import jax, jax.numpy as jnp
        import numpy as np
        D_MODEL = 128
        H = 16
        D_K = 64
        D_V = 64
        D_G = D_MODEL // H
        WAVE_LEN = 1000.0
        B = 8
        N = 64

        def box_relational_embedding(boxes, dim_g=D_G):
            x_min, y_min, x_max, y_max = jnp.split(boxes, 4, axis=-1)
            cx = (x_min + x_max) * 0.5
            cy = (y_min + y_max) * 0.5
            w = x_max - x_min + 1.0
            h = y_max - y_min + 1.0
            delta_x = jnp.log(jnp.clip(jnp.abs((cx - jnp.swapaxes(cx, 1, 2)) / w), 0.001, None))
            delta_y = jnp.log(jnp.clip(jnp.abs((cy - jnp.swapaxes(cy, 1, 2)) / h), 0.001, None))
            delta_w = jnp.log(w / jnp.swapaxes(w, 1, 2))
            delta_h = jnp.log(h / jnp.swapaxes(h, 1, 2))
            pos = jnp.stack([delta_x, delta_y, delta_w, delta_h], axis=-1)
            n_freq = dim_g // 8
            feat_range = jnp.arange(n_freq, dtype=jnp.float32)
            dim_mat = 1.0 / WAVE_LEN ** (feat_range / n_freq)
            mul = (100.0 * pos)[..., None] * dim_mat
            b, n = (pos.shape[0], pos.shape[1])
            mul = mul.reshape(b, n, n, 4 * n_freq)
            return jnp.concatenate([jnp.sin(mul), jnp.cos(mul)], axis=-1)
        b, nq, _ = queries.shape
        nk = keys.shape[1]
        emb = box_relational_embedding(boxes)
        g = jax.nn.relu(jnp.einsum('bnmd,hd->bhnm', emb, Wg) + bg[None, :, None, None])
        q = (queries @ Wq.T + bq).reshape(b, nq, H, D_K).transpose(0, 2, 1, 3)
        k = (keys @ Wk.T + bk).reshape(b, nk, H, D_K).transpose(0, 2, 1, 3)
        v = (values @ Wv.T + bv).reshape(b, nk, H, D_V).transpose(0, 2, 1, 3)
        a = jnp.einsum('bhqd,bhkd->bhqk', q, k) / jnp.sqrt(jnp.float32(D_K))
        mn = jax.nn.softmax(jnp.log(jnp.clip(g, 1e-06, None)) + a, axis=-1)
        out = jnp.einsum('bhqk,bhkd->bqhd', mn, v).reshape(b, nq, H * D_V)
        return out @ Wo.T + bo

    def _L0_ffn_ref(x, gate_w, bias, up_w, up_b, down_w, down_b, sw_up, sb_up, sw_down, sb_down):
        import jax, jax.numpy as jnp
        import numpy as np
        H = 128
        I = 4 * H
        E = 8
        K = 2
        B, S = (2, 128)
        STD = 0.02 / np.sqrt(H)
        b, s, h = x.shape
        xf = x.reshape(-1, h)
        T = xf.shape[0]
        scores = jax.nn.sigmoid(xf @ gate_w + bias)
        top_scores, top_idx = jax.lax.top_k(scores, K)
        top_scores = top_scores / (jnp.sum(top_scores, axis=-1, keepdims=True) + 1e-06)
        w = jnp.zeros((T, E), dtype=xf.dtype).at[jnp.arange(T)[:, None], top_idx].add(top_scores)
        up = jnp.einsum('th,ehi->tei', xf, up_w) + up_b
        hact = jax.nn.gelu(up, approximate=False)
        eo = jnp.einsum('tei,eih->teh', hact, down_w) + down_b
        combined = jnp.einsum('teh,te->th', eo * 0.1, w)
        shared = (jax.nn.gelu(xf @ sw_up + sb_up, approximate=False) @ sw_down + sb_down) * 0.1
        out = (shared + combined).reshape(b, s, h)
        out = out / (jnp.max(jnp.abs(out), axis=-1, keepdims=True) + 1e-06)
        return out
    x = x + _L0_xattn_ref(_layernorm(x, axis=-1), ctx_1024, ctx_1024, fside_BxSx4_0, L0_xattn_Wq, L0_xattn_bq, L0_xattn_Wk, L0_xattn_bk, L0_xattn_Wv, L0_xattn_bv, L0_xattn_Wo, L0_xattn_bo, L0_xattn_Wg, L0_xattn_bg)
    x = x + _L0_ffn_ref(_layernorm(x, axis=-1), L0_ffn_gate_w, L0_ffn_bias, L0_ffn_up_w, L0_ffn_up_b, L0_ffn_down_w, L0_ffn_down_b, L0_ffn_sw_up, L0_ffn_sb_up, L0_ffn_sw_down, L0_ffn_sb_down)
    return x

_drawn_inputs = setup_inputs


def setup_inputs(seed=0):
    import zlib

    import numpy as np

    out = dict(_drawn_inputs(seed))
    spreads = {'L0_xattn_bq': (0.0, 0.8),
     'L0_xattn_bk': (0.0, 0.8),
     'L0_xattn_bv': (0.0, 0.1),
     'L0_xattn_bo': (0.0, 0.1),
     'L0_xattn_bg': (0.0, 0.1),
     'L0_ffn_bias': (0.0, 0.1),
     'L0_ffn_up_b': (0.0, 0.8),
     'L0_ffn_down_b': (0.0, 0.1),
     'L0_ffn_sb_up': (0.0, 0.8),
     'L0_ffn_sb_down': (0.0, 0.1)}
    factors = {'L0_xattn_Wq': 8.0,
     'L0_xattn_Wk': 8.0,
     'L0_ffn_up_w': 8.0,
     'L0_ffn_down_w': 8.0,
     'L0_ffn_sw_up': 8.0,
     'L0_ffn_sw_down': 7.167}
    for name, (base, spread) in spreads.items():
        noise = np.random.default_rng([zlib.crc32(name.encode()), seed]).standard_normal(out[name].shape)
        drawn = base * np.exp(spread * noise) if base else spread * noise
        out[name] = jnp.asarray(drawn.astype(out[name].dtype))
    for name, factor in factors.items():
        out[name] = (out[name] * factor).astype(out[name].dtype)
    return out
```

```python
from contextlib import ExitStack
from math import pi

import concourse.bass as bass
from concourse import mybir

F32 = mybir.dt.float32
BF16 = mybir.dt.bfloat16
I32 = mybir.dt.int32
ALU = mybir.AluOpType
ACT = mybir.ActivationFunctionType
X = mybir.AxisListType.X

P = 128
S = 64
H = 16
DK = 64
HP = H // 2
NB = 4
NF = 8
E = 8
FB = 4
HO = 6
LN_EPS = 1e-5
BANK = 512
ROUND = 1.5 * 2.0 ** 23
NO_SIGN = 0x7FFFFFFF
TURNS = 100.0 / (2 * pi)
SIN_SCALE = 6.283185


def run_pairs(eng, tiles, body):
    pairs = tiles // 2
    for t in range(4):
        body(t, t % 2, t // 2, t == 0, False)
    with eng.Fori(2, pairs - 1) as i:
        for u in range(2):
            body(i * 2 + u, u, i, False, False)
    for u in range(2):
        body(tiles - 2 + u, u, pairs - 1, False, u == 1)


def hold(eng, mark):
    eng.sem_inc(mark, 1)


def at(t, size):
    return slice(t * size, (t + 1) * size) if isinstance(t, int) else bass.ds(t * size, size)


def setup_block(nc, ctx, w, d):
    ld = ctx.enter_context(nc.semaphore("weights_loaded"))
    brd = ctx.enter_context(nc.semaphore("bias_rows_loaded"))
    hi = ctx.enter_context(nc.semaphore("high_parts"))
    lo = ctx.enter_context(nc.semaphore("low_parts"))
    cst = ctx.enter_context(nc.semaphore("constants_set"))
    spread = ctx.enter_context(nc.semaphore("value_bias_spread"))
    prod = ctx.enter_context(nc.semaphore("value_bias_projected"))
    step = ctx.enter_context(nc.semaphore("bias_split_steps"))
    with ExitStack() as c:
        raw = c.enter_context(nc.sbuf_tensor("raw_weights", [P, 4, H * DK], F32))
        nb = 2 * H * DK + 16 * H
        braw = c.enter_context(nc.sbuf_tensor("raw_bias_rows", [P, nb], F32))
        bpart = c.enter_context(nc.sbuf_tensor("bias_part", [P, nb], BF16))
        bvs = c.enter_context(nc.sbuf_tensor("value_bias_spread_sb", [P, HP, P], F32))
        bvc = c.enter_context(nc.sbuf_tensor("value_bias_cols", [P, HP], F32))
        bob = c.enter_context(nc.sbuf_tensor("out_bias_rows", [P, P], F32))
        yb = c.enter_context(nc.psum_tensor("bias_psum", [P, P], F32))
        block = c.enter_context(nc.Block())

        @block.sync
        def _(sp):
            for n, name in enumerate(("wq", "wk", "wv", "wo")):
                sp.dma_start(raw[:, n, :], d[name]).then_inc(ld, 16)
            sp.dma_start(bvc[:, :], d["bv"]).then_inc(ld, 16)
            sp.dma_start(bob[:, :], d["bo"].partition_broadcast(P)).then_inc(ld, 16)
            sp.dma_start(w["ident"][:, :], d["ident"]).then_inc(ld, 16)
            sp.dma_start(w["kron"][:, :], d["kron"]).then_inc(ld, 16)
            sp.dma_start(braw[:, :], d["bias_rows"].partition_broadcast(P)).then_inc(brd, 16)
            sp.wait_ge(ld, 16 * 8)

        @block.scalar
        def _(act):
            act.wait_ge(ld, 16 * 8)
            for n in range(4):
                act.activation(w["split"][:, n, 0, :], raw[:, n, :], ACT.Copy).then_inc(hi, 1)

        @block.gpsimd
        def _(pool):
            for name in ("qbd", "pbd"):
                pool.memset(w[name][:, :, :], 0.0).then_inc(cst, 1)
            pool.memset(w["v"][:, :, DK:DK + 1], 1.0).then_inc(cst, 1)
            pool.memset(w["ones"][:, :], 1.0).then_inc(cst, 1)
            pool.memset(w["minus_half"][:, :], -0.5).then_inc(cst, 1)
            pool.memset(w["quarter"][:, :], pi / 2).then_inc(cst, 1)
            pool.wait_ge(cst, 6)

        @block.vector
        def _(dve):
            dve.memset(w["brows"][:, :], 0.0).then_inc(step, 1)
            dve.wait_ge(brd, 16)
            for n, row in enumerate((0, 32, 64)):
                dve.wait_ge(step, 1 + 3 * n)
                dve.tensor_copy(bpart[:, :], braw[:, :]).then_inc(step, 1)
                dve.wait_ge(step, 2 + 3 * n)
                dve.tensor_copy(w["brows"][row:row + 1, :], bpart[row:row + 1, :]).then_inc(step, 1)
                dve.tensor_tensor(braw[:, :], braw[:, :], bpart[:, :], ALU.subtract).then_inc(step, 1)
            dve.wait_ge(ld, 16 * 8)
            for n in range(4):
                dve.wait_ge(hi, n + 1)
                dve.tensor_tensor(w["split"][:, n, 1, :], raw[:, n, :], w["split"][:, n, 0, :],
                                  ALU.subtract).then_inc(lo, 1)
            for j in range(HP):
                dve.tensor_copy(bvs[:, j, :], bvc[:, j:j + 1].to_broadcast([P, P])).then_inc(spread, 1)
            dve.wait_ge(prod, 1)
            dve.tensor_tensor(w["ybias"][:, :], yb[:, :], bob[:, :], ALU.add).then_inc(lo, 1)
            dve.wait_ge(lo, 5)

        @block.tensor
        def _(pe):
            pe.wait_ge(spread, HP)
            for j in range(HP):
                mm = pe.matmul(yb[:, :], bvs[:, j, :], raw[:, 3, j * P:(j + 1) * P],
                               start=(j == 0), stop=(j == HP - 1))
            mm.then_inc(prod, 1)


def relations_block(nc, ctx, w, d, ft, mtab, T):
    G = min(16, T // 2)
    NG = T // G

    def sem(n):
        return ctx.enter_context(nc.semaphore(n))

    boxes_ld, own_step, own_ready, tab_st = sem("boxes_loaded"), sem("own_steps"), sem("own_ready"), sem("table_stored")
    keys_ld = [sem("key_boxes_loaded0"), sem("key_boxes_loaded1")]
    dif_s, siz_s, sca_s, clip_s, log_s = sem("differences"), sem("size_ratios"), sem("scaled"), sem("clipped"), sem("logs")
    rnd_s, frc_s, sin_s, cos_s, turn_s = sem("rounding"), sem("fractions"), sem("sines"), sem("cosines"), sem("turned")
    abs_s = sem("absolute")
    out_s = [sem("turned_out_dve"), sem("turned_out_act")]
    st_s = [sem("features_stored0"), sem("features_stored1")]
    with ExitStack() as c:
        def sb(n, s):
            return c.enter_context(nc.sbuf_tensor(n, s, F32))

        box = sb("boxes", [P, T, NB])
        cen, size, rsz = sb("centres", [P, T, 2]), sb("box_sizes", [P, T, 2]), sb("inverse_sizes", [P, T, 2])
        mrow = sb("centre_and_inverse", [P, T, NB])
        keys = sb("key_side", [P, 2, G, S * NB])
        dist = sb("distances", [P, 2, G, NB, S])
        whole, frac, afrac = sb("whole_turns", [P, G, NB, S]), sb("part_turns", [P, G, NB, S]), sb("abs_part", [P, G, NB, S])
        feat = sb("features_sb", [P, G, S, NF])
        fto = sb("turned_features", [P, 2, BANK])
        ps = c.enter_context(nc.psum_tensor("turn_psum", [P, 2, BANK], F32))
        block = c.enter_context(nc.Block())

        def flat(x):
            return x.rearrange("p g c m -> p (g c m)")

        def tile_pairs(eng, g, body):
            if g == 0:
                for u in range(2):
                    body(u, u, 0, True)
            with eng.Fori(1 if g == 0 else 0, G // 2) as i:
                for u in range(2):
                    body(i * 2 + u, u, i + g * (G // 2), False)

        @block.sync
        def _(sp):
            sp.dma_start(box[:, :, :], d["boxes"].rearrange("(t p) c -> p t c", p=P)).then_inc(boxes_ld, 16)
            sp.wait_ge(own_ready, 1)
            sp.dma_start(mtab.rearrange("b (m c) -> (b m) c", c=NB).rearrange("(t p) c -> p t c", p=P),
                         mrow[:, :, :]).then_inc(tab_st, 16)
            sp.wait_ge(tab_st, 16)

            def load(g):
                if g >= 2:
                    sp.wait_ge(dif_s, g - 1)
                    sp.wait_ge(siz_s, g - 1)
                for b in range(2):
                    src = mtab[g * 2 * G:(g + 1) * 2 * G, :].rearrange("(t b) n -> b t n", b=2)[b]
                    sp.dma_start(keys[b * S:(b + 1) * S, g % 2, :, :], src.partition_broadcast(S)).then_inc(keys_ld[g % 2], 16)

            def store(k, u, n, first):
                sp.wait_ge(out_s[u], n + 1)
                sp.dma_start(ft[at(n * 2 + u, 1)].rearrange("t p n -> (t p) n"), fto[:, u, :]).then_inc(st_s[u], 16)

            load(0)
            for g in range(NG):
                if g + 1 < NG:
                    load(g + 1)
                tile_pairs(sp, g, store)
            for u in range(2):
                sp.wait_ge(st_s[u], 16 * (T // 2))

        @block.vector
        def _(dve):
            dve.wait_ge(boxes_ld, 16)
            dve.tensor_tensor(cen[:, :, :], box[:, :, 0:2], box[:, :, 2:4], ALU.add).then_inc(own_step, 1)
            dve.tensor_tensor(size[:, :, :], box[:, :, 2:4], box[:, :, 0:2], ALU.subtract).then_inc(own_step, 1)
            dve.wait_ge(own_step, 2)
            dve.tensor_scalar(cen[:, :, :], cen[:, :, :], 0.5, None, ALU.mult).then_inc(own_step, 1)
            dve.tensor_scalar(size[:, :, :], size[:, :, :], 1.0, None, ALU.add).then_inc(own_step, 1)
            dve.wait_ge(own_step, 4)
            dve.reciprocal(rsz[:, :, :], size[:, :, :]).then_inc(own_step, 1)
            dve.tensor_copy(mrow[:, :, 0:2], cen[:, :, :]).then_inc(own_step, 1)
            dve.wait_ge(own_step, 6)
            dve.tensor_copy(mrow[:, :, 2:4], rsz[:, :, :]).then_inc(own_ready, 1)

            def copy_out(k, u, n, first):
                if u:
                    return
                dve.wait_ge(turn_s, n * 2 + 1)
                if not first:
                    dve.wait_ge(st_s[0], n * 16)
                dve.tensor_copy(fto[:, 0, :], ps[:, 0, :]).then_inc(out_s[0], 1)

            for g in range(NG):
                u = g % 2
                own_c = cen[:, g * G:(g + 1) * G, :].unsqueeze(3).to_broadcast([P, G, 2, S])
                dve.wait_ge(keys_ld[u], 32 * (g // 2 + 1))
                dve.tensor_tensor(dist[:, u, :, 0:2, :], keys[:, u, :, :].rearrange("p g (m c) -> p g c m", c=NB)[:, :, 0:2, :],
                                  own_c, ALU.subtract).then_inc(dif_s, 1)
                dve.wait_ge(sca_s, g + 1)
                shift = dist[:, u, :, 0:2, :]
                dve.tensor_scalar(shift.bitcast(I32), shift.bitcast(I32), NO_SIGN, None, ALU.bitwise_and).then_inc(abs_s, 1)
                dve.wait_ge(abs_s, g + 1)
                dve.tensor_scalar(shift, shift, 1e-3, None, ALU.max).then_inc(clip_s, 1)
                dve.wait_ge(log_s, g + 1)
                L, W, Fr, A = flat(dist[:, u]), flat(whole[:, :, :, :]), flat(frac[:, :, :, :]), flat(afrac[:, :, :, :])
                dve.tensor_scalar(W, L, TURNS, ROUND, ALU.mult, ALU.add).then_inc(rnd_s, 1)
                dve.wait_ge(rnd_s, 2 * g + 1)
                dve.tensor_scalar(W, W, ROUND, None, ALU.subtract).then_inc(rnd_s, 1)
                dve.wait_ge(rnd_s, 2 * g + 2)
                if g >= 1:
                    dve.wait_ge(cos_s, g)
                dve.scalar_tensor_tensor(Fr, L, TURNS, W, ALU.mult, ALU.subtract).then_inc(frc_s, 1)
                dve.wait_ge(frc_s, 2 * g + 1)
                dve.tensor_scalar(A.bitcast(I32), Fr.bitcast(I32), NO_SIGN, None, ALU.bitwise_and).then_inc(frc_s, 1)
                tile_pairs(dve, g, copy_out)

        @block.gpsimd
        def _(pool):
            pool.wait_ge(own_ready, 1)
            for g in range(NG):
                u = g % 2
                tiles = slice(g * G, (g + 1) * G)
                pool.wait_ge(keys_ld[u], 32 * (g // 2 + 1))
                if g >= 2:
                    pool.wait_ge(frc_s, 2 * (g - 2) + 1)
                pool.tensor_tensor(dist[:, u, :, 2:4, :], keys[:, u, :, :].rearrange("p g (m c) -> p g c m", c=NB)[:, :, 2:4, :],
                                   size[:, tiles, :].unsqueeze(3).to_broadcast([P, G, 2, S]), ALU.mult).then_inc(siz_s, 1)
                pool.wait_ge(dif_s, g + 1)
                pool.tensor_tensor(dist[:, u, :, 0:2, :], dist[:, u, :, 0:2, :],
                                   rsz[:, tiles, :].unsqueeze(3).to_broadcast([P, G, 2, S]), ALU.mult).then_inc(sca_s, 1)

        @block.scalar
        def _(act):
            def copy_out(k, u, n, first):
                if not u:
                    return
                act.wait_ge(turn_s, n * 2 + 2)
                if not first:
                    act.wait_ge(st_s[1], n * 16)
                act.activation(fto[:, 1, :], ps[:, 1, :], ACT.Copy).then_inc(out_s[1], 1)

            for g in range(NG):
                act.wait_ge(clip_s, g + 1)
                act.wait_ge(siz_s, g + 1)
                act.activation(flat(dist[:, g % 2]), flat(dist[:, g % 2]), ACT.Ln).then_inc(log_s, 1)
                fv = feat[:, :, :, :].rearrange("p g m f -> p g f m")
                if g >= 1:
                    act.wait_ge(turn_s, g * G)
                act.wait_ge(frc_s, 2 * g + 1)
                act.activation(fv[:, :, 0:NB, :], frac[:, :, :, :], ACT.Sin, scale=SIN_SCALE).then_inc(sin_s, 1)
                act.wait_ge(frc_s, 2 * g + 2)
                act.activation(fv[:, :, NB:NF, :], afrac[:, :, :, :], ACT.Sin, bias=w["quarter"][:, 0:1],
                               scale=-SIN_SCALE).then_inc(cos_s, 1)
                tile_pairs(act, g, copy_out)

        @block.tensor
        def _(pe):
            def turn(g, k, wait_out):
                u, n = k % 2, k // 2 + g * (G // 2)
                if wait_out:
                    pe.wait_ge(out_s[u], n)
                row = feat[:, k, :, :].rearrange("p m f -> p (m f)")
                for q in range(NB):
                    mm = pe.transpose(ps[:, u, q * P:(q + 1) * P], row[:, q * P:(q + 1) * P], w["ident"][:, :])
                mm.then_inc(turn_s, 1)

            pe.wait_ge(cos_s, 1)
            for k in range(G):
                turn(0, k, k >= 2)
            with pe.Fori(1, NG) as g:
                pe.wait_ge(cos_s, g + 1)
                for k in range(G):
                    turn(g, k, True)


def attention_block(nc, ctx, w, d, ft, x2d, T):
    sem = lambda n: ctx.enter_context(nc.semaphore(n))
    ch_s = sem("ctx_high")
    held_dve, held_pool = sem("held_dve"), sem("held_pool")
    x_ld, c_ld, f_ld = ([sem(f"{n}_loaded{u}") for u in range(2)] for n in ("x", "ctx", "features"))
    x2_st = [sem("x2_stored0"), sem("x2_stored1")]
    stats, rstd, xn_s, xb_s, c_s = sem("ln_stats"), sem("ln_rstd"), sem("x_normed"), sem("x_biased"), sem("ctx_split")
    xT_s, xh_s, xl_s = sem("x_turned"), sem("xT_high"), sem("xT_low")
    q_s, k_s, v_s = sem("q_done"), sem("k_done"), sem("v_done")
    qa, qd, ka, kd, va = sem("q_out_act"), sem("q_out_dve"), sem("k_out_act"), sem("k_out_dve"), sem("v_out")
    sc_s, g_s, mx_s, sub_s, exp_s, p_s = sem("scores_done"), sem("gates_done"), sem("row_max"), sem("shifted"), sem("exps"), sem("probs")
    pT_s, pa, pd = sem("probs_turned"), sem("probs_out_act"), sem("probs_out_dve")
    o_s, rs_s, on_s, oT_s, oh_s, ol_s, y_s, x2_s = (sem(n) for n in (
        "heads_done", "sums_inverted", "heads_normed", "heads_turned", "headsT_high", "headsT_low", "attn_out", "x2_ready"))
    with ExitStack() as c:
        sb = lambda n, s, dt=F32: c.enter_context(nc.sbuf_tensor(n, s, dt))
        xt, xn, xb = sb("x_tile", [P, 2, P]), sb("x_norm", [P, 2, P]), sb("x_plus_bias", [P, 2, P])
        ct, cT = sb("ctxT_tile", [P, 2, P]), sb("ctxT_parts", [P, 2, 2, P], BF16)
        xT = sb("xT_parts", [P, 2, P], BF16)
        fts = sb("feature_tile", [P, 2, BANK])
        st6, mv, var, rs = sb("bn", [P, 2, 6]), sb("mean_var", [P, 2, 2]), sb("var_eps", [P, 2, 1]), sb("rstd", [P, 2, 1])
        kT = sb("kT", [P, H, S])
        z, mx = sb("logits", [P, H, S]), sb("row_maximum", [P, H])
        inv, on = sb("inverse_sums", [P, H]), sb("heads_out", [P, H, DK])
        oT = sb("headsT_parts", [P, 2, HP, P], BF16)
        x2 = sb("x2_tile", [P, 2, P])
        ps = c.enter_context(nc.psum_tensor("attn_psum", [P, 8, BANK], F32))
        flat = ps[:, :, :].rearrange("p b n -> p (b n)")
        SC = flat[:, 0:2 * BANK].rearrange("p (h k) -> p h k", k=S)
        GA = flat[:, 2 * BANK:4 * BANK]
        XQ = flat[:, 4 * BANK:6 * BANK].rearrange("p (j n) -> p j n", n=P)
        YT = flat[:, 6 * BANK:8 * BANK].rearrange("p (j n) -> p j n", n=P)
        AO = ps[:, 3, 0:P]
        qbd, pbd, v, split = w["qbd"], w["pbd"], w["v"], w["split"]
        block = c.enter_context(nc.Block())

        @block.sync
        def _(sp):
            def loads(t, u, wait_free):
                if wait_free:
                    sp.wait_ge(xb_s, t - 1)
                    sp.wait_ge(xn_s, t - 1)
                    sp.wait_ge(c_s, t - 1)
                sp.dma_start(xt[:, u, :], d["x"][at(t, P), :]).then_inc(x_ld[u], 16)
                sp.dma_start(ct[:, u, :], d["ctxT"][:, at(t, P)]).then_inc(c_ld[u], 16)
                if wait_free:
                    sp.wait_ge(g_s, t - 1)
                sp.dma_start(fts[:, u, :], ft[at(t, 1)].rearrange("t p n -> (t p) n")).then_inc(f_ld[u], 16)

            def body(t, u, i, first, last):
                if not first:
                    sp.wait_ge(x2_s, t)
                    sp.dma_start(x2d[at(t - 1, P), :], x2[:, 1 - u, :]).then_inc(x2_st[1 - u], 16)
                if not (isinstance(t, int) and t + 2 >= T):
                    loads(t + 2, u, True)

            loads(0, 0, False)
            loads(1, 1, False)
            run_pairs(sp, T, body)
            sp.wait_ge(x2_s, T)
            sp.dma_start(x2d[at(T - 1, P), :], x2[:, 1, :]).then_inc(x2_st[1], 16)
            for u in range(2):
                sp.wait_ge(x2_st[u], 16 * (T // 2))

        @block.gpsimd
        def _(pool):
            def prepare(t, u, i):
                pool.wait_ge(stats, 2 * t + 2)
                hold(pool, held_pool)
                pool.tensor_scalar(var[:, u, :], mv[:, u, 1:2], LN_EPS, None, ALU.add).then_inc(rstd, 1)
                pool.wait_ge(rstd, 2 * t + 1)
                pool.tensor_tensor(rs[:, u, :], var[:, u, :], w["minus_half"][:, :], ALU.pow).then_inc(rstd, 1)
                pool.wait_ge(rstd, 2 * t + 2)
                hold(pool, held_pool)
                pool.tensor_scalar(xn[:, u, :], xt[:, u, :], mv[:, u, 0:1], rs[:, u, :],
                                   ALU.subtract, ALU.mult).then_inc(xn_s, 1)
                pool.tensor_tensor(xb[:, u, :], xt[:, u, :], w["ybias"][:, :], ALU.add).then_inc(xb_s, 1)
                pool.wait_ge(c_ld[u], 16 * (i + 1))
                if not (isinstance(t, int) and t < 2):
                    pool.wait_ge(v_s, t - 1)
                hold(pool, held_pool)
                pool.tensor_copy(cT[:, u, 0, :], ct[:, u, :]).then_inc(ch_s, 1)
                pool.wait_ge(ch_s, t + 1)
                pool.tensor_tensor(cT[:, u, 1, :], ct[:, u, :], cT[:, u, 0, :], ALU.subtract).then_inc(c_s, 1)

            def body(t, u, i, first, last):
                if not last:
                    if not first:
                        pool.wait_ge(x2_s, t)
                        pool.wait_ge(xT_s, t)
                    prepare(t + 1, 1 - u, i + u)

            prepare(0, 0, 0)
            run_pairs(pool, T, body)

        @block.vector
        def _(dve):
            def norm_stats(t, u, i):
                dve.wait_ge(x_ld[u], 16 * (i + 1))
                dve.bn_stats(st6[:, u, :], xt[:, u, :]).then_inc(stats, 1)
                dve.wait_ge(stats, 2 * t + 1)
                hold(dve, held_dve)
                dve.bn_aggr(mv[:, u, :], st6[:, u, :]).then_inc(stats, 1)

            def low_xT(t):
                dve.wait_ge(xh_s, t + 1)
                dve.tensor_tensor(xT[:, 1, :], XQ[:, 0, :], xT[:, 0, :], ALU.subtract).then_inc(xl_s, 1)

            def q_out(t):
                dve.wait_ge(q_s, t + 1)
                for b in range(2):
                    ins = dve.tensor_copy(qbd[b * S:(b + 1) * S, 1:H:2, b * S:(b + 1) * S],
                                          XQ[S:P, :, b * S:(b + 1) * S])
                ins.then_inc(qd, 1)

            def k_out(t):
                dve.wait_ge(k_s, t + 1)
                for b in range(2):
                    ins = dve.tensor_copy(kT[b * S:(b + 1) * S, 1:H:2, :], XQ[S:P, :, b * S:(b + 1) * S])
                ins.then_inc(kd, 1)

            def low_oT(t):
                dve.wait_ge(oh_s, t + 1)
                dve.tensor_tensor(oT[:, 1, :, :], YT, oT[:, 0, :, :], ALU.subtract).then_inc(ol_s, 1)

            def add_out(t, u, i):
                dve.wait_ge(y_s, t + 1)
                dve.wait_ge(xb_s, t + 1)
                if not (isinstance(t, int) and t < 2):
                    dve.wait_ge(x2_st[u], 16 * i)
                dve.tensor_tensor(x2[:, u, :], AO, xb[:, u, :], ALU.add).then_inc(x2_s, 1)

            norm_stats(0, 0, 0)
            low_xT(0)
            q_out(0)
            k_out(0)

            def body(t, u, i, first, last):
                if not last:
                    if not first:
                        dve.wait_ge(xn_s, t)
                    norm_stats(t + 1, 1 - u, i + u)
                if not first:
                    low_oT(t - 1)
                dve.wait_ge(sc_s, t + 1)
                dve.tensor_reduce(mx[:, :], SC, X, ALU.max).then_inc(mx_s, 1)
                dve.wait_ge(mx_s, t + 1)
                dve.tensor_tensor(z[:, :, :], SC, mx[:, :].unsqueeze(2).to_broadcast([P, H, S]), ALU.subtract).then_inc(sub_s, 1)
                if not first:
                    add_out(t - 1, 1 - u, i - 1 + u)
                if not last:
                    low_xT(t + 1)
                dve.wait_ge(exp_s, t + 1)
                dve.wait_ge(g_s, t + 1)
                dve.scalar_tensor_tensor(z[:, :, :], GA.rearrange("p (m h) -> p h m", h=H), 1e-6, z[:, :, :],
                                         ALU.max, ALU.mult).then_inc(p_s, 1)
                if not last:
                    q_out(t + 1)
                dve.wait_ge(pT_s, t + 1)
                for b in range(2):
                    ins = dve.tensor_copy(pbd[b * S:(b + 1) * S, 1:H:2, b * S:(b + 1) * S], YT[S:P, :, b * S:(b + 1) * S])
                ins.then_inc(pd, 1)
                if not last:
                    k_out(t + 1)
                dve.wait_ge(o_s, t + 1)
                wide = ps[:, 0:2, 0:HO * (DK + 1)].rearrange("p b (h n) -> p b h n", n=DK + 1)
                rest = ps[:, 2, 0:(H - 2 * HO) * (DK + 1)].rearrange("p (h n) -> p h n", n=DK + 1)
                dve.reciprocal(inv[:, 0:2 * HO].rearrange("p (b h) -> p b h", b=2), wide[:, :, :, DK]).then_inc(rs_s, 1)
                dve.reciprocal(inv[:, 2 * HO:H], rest[:, :, DK]).then_inc(rs_s, 1)
                dve.wait_ge(rs_s, 2 * t + 2)
                dve.tensor_tensor(on[:, 0:2 * HO, :].rearrange("p (b h) n -> p b h n", b=2), wide[:, :, :, 0:DK],
                                  inv[:, 0:2 * HO].rearrange("p (b h) -> p b h", b=2).unsqueeze(3).to_broadcast([P, 2, HO, DK]),
                                  ALU.mult)
                dve.tensor_tensor(on[:, 2 * HO:H, :], rest[:, :, 0:DK],
                                  inv[:, 2 * HO:H].unsqueeze(2).to_broadcast([P, H - 2 * HO, DK]), ALU.mult).then_inc(on_s, 1)

            run_pairs(dve, T, body)
            low_oT(T - 1)
            add_out(T - 1, 1, T // 2 - 1)

        @block.scalar
        def _(act):
            def high_xT(t):
                act.wait_ge(xT_s, t + 1)
                act.activation(xT[:, 0, :], XQ[:, 0, :], ACT.Copy).then_inc(xh_s, 1)

            def out_half(done, out, src, dst, t, wide):
                act.wait_ge(done, t + 1)
                for b in range(2):
                    cols = slice(b * S, (b + 1) * S)
                    to = dst[b * S:(b + 1) * S, 0:H:2, cols if wide else slice(0, S)]
                    ins = act.activation(to, src[0:S, :, cols], ACT.Copy)
                ins.then_inc(out, 1)

            def v_out(t):
                act.wait_ge(v_s, t + 1)
                act.activation(v[:, :, 0:DK], XQ.rearrange("p j (e n) -> p (j e) n", e=2), ACT.Copy).then_inc(va, 1)

            def high_oT(t):
                act.wait_ge(oT_s, t + 1)
                act.activation(oT[:, 0, :, :], YT, ACT.Copy).then_inc(oh_s, 1)

            high_xT(0)
            out_half(q_s, qa, XQ, qbd, 0, True)
            out_half(k_s, ka, XQ, kT, 0, False)
            v_out(0)

            def body(t, u, i, first, last):
                act.wait_ge(sub_s, t + 1)
                act.activation(z[:, :, :], z[:, :, :], ACT.Exp, scale=DK ** -0.5).then_inc(exp_s, 1)
                if not last:
                    high_xT(t + 1)
                    out_half(q_s, qa, XQ, qbd, t + 1, True)
                out_half(pT_s, pa, YT, pbd, t, True)
                if not last:
                    out_half(k_s, ka, XQ, kT, t + 1, False)
                    v_out(t + 1)
                high_oT(t)

            run_pairs(act, T, body)

        @block.tensor
        def _(pe):
            def x_turn(t, u):
                pe.wait_ge(xn_s, t + 1)
                pe.transpose(XQ[:, 0, :], xn[:, u, :], w["ident"][:, :]).then_inc(xT_s, 1)

            def project(n, parts, done):
                for j in range(HP):
                    cols = slice(j * P, (j + 1) * P)
                    pe.matmul(XQ[:, j, :], w["brows"][:, n * H * DK + j * P:n * H * DK + (j + 1) * P], w["ones"][:, :], start=True, stop=False)
                    pe.matmul(XQ[:, j, :], split[:, n, 0, cols], parts[0], start=False, stop=False)
                    pe.matmul(XQ[:, j, :], split[:, n, 0, cols], parts[1], start=False, stop=False)
                    mm = pe.matmul(XQ[:, j, :], split[:, n, 1, cols], parts[0], start=False, stop=True)
                mm.then_inc(done, 1)

            def q_proj(t):
                pe.wait_ge(xl_s, t + 1)
                project(0, (xT[:, 0, :], xT[:, 1, :]), q_s)

            def k_proj(t, u):
                pe.wait_ge(c_s, t + 1)
                pe.wait_ge(qa, t + 1)
                pe.wait_ge(qd, t + 1)
                project(1, (cT[:, u, 0, :], cT[:, u, 1, :]), k_s)

            def v_proj(t, u):
                pe.wait_ge(ka, t + 1)
                pe.wait_ge(kd, t + 1)
                for half in range(2):
                    out = flat[:, (4 + half) * BANK:(5 + half) * BANK]
                    cols = slice(half * BANK, (half + 1) * BANK)
                    pe.matmul(out, cT[:, u, 0, :], split[:, 2, 0, cols], start=True, stop=False)
                    pe.matmul(out, cT[:, u, 0, :], split[:, 2, 1, cols], start=False, stop=False)
                    mm = pe.matmul(out, cT[:, u, 1, :], split[:, 2, 0, cols], start=False, stop=True)
                mm.then_inc(v_s, 1)

            def out_proj(t):
                pe.wait_ge(ol_s, t + 1)
                for j in range(HP):
                    cols = slice(j * P, (j + 1) * P)
                    pe.matmul(AO, oT[:, 0, j, :], split[:, 3, 0, cols], start=(j == 0), stop=False)
                    pe.matmul(AO, oT[:, 0, j, :], split[:, 3, 1, cols], start=False, stop=False)
                    mm = pe.matmul(AO, oT[:, 1, j, :], split[:, 3, 0, cols], start=False, stop=(j == HP - 1))
                mm.then_inc(y_s, 1)

            x_turn(0, 0)
            q_proj(0)
            k_proj(0, 0)
            v_proj(0, 0)

            def body(t, u, i, first, last):
                pe.wait_ge(qa, t + 1)
                pe.wait_ge(ka, t + 1)
                pe.wait_ge(kd, t + 1)
                if not first:
                    pe.wait_ge(on_s, t)
                for h in range(H):
                    mm = pe.matmul(SC[:, h, :], qbd[:, h, :], kT[:, h, :], start=True, stop=True)
                mm.then_inc(sc_s, 1)
                if not first:
                    out_proj(t - 1)
                pe.wait_ge(f_ld[u], 16 * (i + 1))
                for q in range(NB):
                    if q == 2 and not first:
                        pe.wait_ge(x2_s, t)
                    out = GA[:, q * 16 * H:(q + 1) * 16 * H]
                    pe.matmul(out, w["ones"][:, :], w["brows"][:, 2 * H * DK:], start=True, stop=False)
                    mm = pe.matmul(out, fts[:, u, q * P:(q + 1) * P], w["kron"][:, :], start=False, stop=True)
                mm.then_inc(g_s, 1)
                if not last:
                    pe.wait_ge(va, t + 1)
                    x_turn(t + 1, 1 - u)
                    q_proj(t + 1)
                pe.wait_ge(p_s, t + 1)
                if not first:
                    pe.wait_ge(ol_s, t)
                zf = z[:, :, :].rearrange("p h k -> p (h k)")
                for j in range(HP):
                    mm = pe.transpose(YT[:, j, :], zf[:, j * P:(j + 1) * P], w["ident"][:, :])
                mm.then_inc(pT_s, 1)
                if not last:
                    k_proj(t + 1, 1 - u)
                pe.wait_ge(pa, t + 1)
                pe.wait_ge(pd, t + 1)
                for h in range(H):
                    b, n = h // HO, (h % HO) * (DK + 1)
                    mm = pe.matmul(ps[:, b, n:n + DK + 1], pbd[:, h, :], v[:, h, :], start=True, stop=True)
                mm.then_inc(o_s, 1)
                if not last:
                    v_proj(t + 1, 1 - u)
                pe.wait_ge(on_s, t + 1)
                onf = on[:, :, :].rearrange("p h n -> p (h n)")
                for j in range(HP):
                    mm = pe.transpose(YT[:, j, :], onf[:, j * P:(j + 1) * P], w["ident"][:, :])
                mm.then_inc(oT_s, 1)

            run_pairs(pe, T, body)
            out_proj(T - 1)


def router_block(nc, ctx, w, d, x2d, xnTd, gate_all, T):
    def sem(n):
        return ctx.enter_context(nc.semaphore(n))

    ld = [sem("r_x2_loaded0"), sem("r_x2_loaded1")]
    st = [sem("r_turned_stored0"), sem("r_turned_stored1")]
    held_dve, held_pool = sem("r_held_dve"), sem("r_held_pool")
    cst, stats, rstd, xn_s, xT_s, xe_s, r_s, w_s, sig_s = (sem(n) for n in (
        "r_constants", "r_stats", "r_rstd", "r_normed", "r_turned", "r_turned_out", "r_scored", "r_steps", "r_sigmoid"))
    with ExitStack() as c:
        def sb(n, s):
            return c.enter_context(nc.sbuf_tensor(n, s, F32))

        x2, xn, xT = sb("r_x2", [P, 2, P]), sb("r_xn", [P, 2, P]), sb("r_xT", [P, 2, P])
        st6, mv, var, rs = sb("r_bn", [P, 2, 6]), sb("r_mv", [P, 2, 2]), sb("r_var", [P, 2, 1]), sb("r_rstd_sb", [P, 2, 1])
        gw, gb, number = sb("gate_weights", [P, E]), sb("gate_bias_sb", [P, E]), sb("expert_numbers", [P, E])
        score, left, hit, idx = (sb(n, [P, T, E]) for n in ("scores", "scores_left", "hits", "hit_numbers"))
        best, first, total = sb("best", [P, T, 2]), sb("first_hit", [P, T]), sb("score_sum", [P, T])
        ps = c.enter_context(nc.psum_tensor("r_psum", [P, 2, BANK], F32))
        pr = c.enter_context(nc.psum_tensor("r_scores_psum", [P, T, E], F32))
        block = c.enter_context(nc.Block())

        @block.sync
        def _(sp):
            sp.dma_start(gw[:, :], d["gate_w"]).then_inc(cst, 16)
            sp.dma_start(gb[:, :], d["gate_b"].partition_broadcast(P)).then_inc(cst, 16)
            sp.dma_start(number[:, :], d["numbers"].partition_broadcast(P)).then_inc(cst, 16)
            for t in range(2):
                sp.dma_start(x2[:, t, :], x2d[at(t, P), :]).then_inc(ld[t], 16)

            def body(t, u, i, first, last):
                sp.wait_ge(xe_s, t + 1)
                sp.dma_start(xnTd[at(t, 1)].rearrange("t p n -> (t p) n"), xT[:, u, :]).then_inc(st[u], 16)
                if not (isinstance(t, int) and t + 2 >= T):
                    sp.wait_ge(xn_s, t + 1)
                    sp.dma_start(x2[:, u, :], x2d[at(t + 2, P), :]).then_inc(ld[u], 16)

            run_pairs(sp, T, body)
            for u in range(2):
                sp.wait_ge(st[u], 16 * (T // 2))

        @block.vector
        def _(dve):
            def body(t, u, i, first, last):
                dve.wait_ge(ld[u], 16 * (i + 1))
                dve.bn_stats(st6[:, u, :], x2[:, u, :]).then_inc(stats, 1)
                dve.wait_ge(stats, 2 * t + 1)
                hold(dve, held_dve)
                dve.bn_aggr(mv[:, u, :], st6[:, u, :]).then_inc(stats, 1)
                dve.wait_ge(rstd, 2 * t + 2)
                if not (isinstance(t, int) and t < 2):
                    dve.wait_ge(xT_s, t - 1)
                dve.tensor_scalar(xn[:, u, :], x2[:, u, :], mv[:, u, 0:1], rs[:, u, :], ALU.subtract, ALU.mult).then_inc(xn_s, 1)

            run_pairs(dve, T, body)
            dve.wait_ge(r_s, T)
            dve.wait_ge(cst, 48)
            n = 0

            def step(ins):
                nonlocal n
                ins.then_inc(w_s, 1)
                n += 1
                dve.wait_ge(w_s, n)

            def over_experts(x):
                return x.unsqueeze(2).to_broadcast([P, T, E])

            per_expert = number[:, :].unsqueeze(1).to_broadcast([P, T, E])
            step(dve.tensor_tensor(score[:, :, :], pr[:, :, :], gb[:, :].unsqueeze(1).to_broadcast([P, T, E]), ALU.add))
            dve.wait_ge(sig_s, 1)
            src = score
            for k in range(2):
                step(dve.tensor_reduce(best[:, :, k], src[:, :, :], X, ALU.max))
                step(dve.tensor_tensor(hit[:, :, :], src[:, :, :], over_experts(best[:, :, k]), ALU.is_equal))
                step(dve.scalar_tensor_tensor(idx[:, :, :], hit[:, :, :], -float(E), per_expert, ALU.mult, ALU.add))
                step(dve.tensor_reduce(first[:, :], idx[:, :, :], X, ALU.min))
                step(dve.tensor_tensor(hit[:, :, :], idx[:, :, :], over_experts(first[:, :]), ALU.is_equal))
                out = gate_all if k == 0 else idx
                step(dve.tensor_tensor(out[:, :, :], hit[:, :, :], over_experts(best[:, :, k]), ALU.mult))
                if k == 0:
                    step(dve.scalar_tensor_tensor(left[:, :, :], hit[:, :, :], -4.0, score[:, :, :], ALU.mult, ALU.add))
                    src = left
            step(dve.tensor_tensor(gate_all[:, :, :], gate_all[:, :, :], idx[:, :, :], ALU.add))
            step(dve.tensor_tensor(total[:, :], best[:, :, 0], best[:, :, 1], ALU.add))
            step(dve.tensor_scalar(total[:, :], total[:, :], 1e-6, None, ALU.add))
            step(dve.reciprocal(total[:, :], total[:, :]))
            step(dve.tensor_tensor(gate_all[:, :, :], gate_all[:, :, :], over_experts(total[:, :]), ALU.mult))

        @block.gpsimd
        def _(pool):
            def body(t, u, i, first, last):
                pool.wait_ge(stats, 2 * t + 2)
                hold(pool, held_pool)
                pool.tensor_scalar(var[:, u, :], mv[:, u, 1:2], LN_EPS, None, ALU.add).then_inc(rstd, 1)
                pool.wait_ge(rstd, 2 * t + 1)
                pool.tensor_tensor(rs[:, u, :], var[:, u, :], w["minus_half"][:, :], ALU.pow).then_inc(rstd, 1)

            run_pairs(pool, T, body)

        @block.scalar
        def _(act):
            def body(t, u, i, first, last):
                act.wait_ge(xT_s, t + 1)
                if not (isinstance(t, int) and t < 2):
                    act.wait_ge(st[u], 16 * i)
                    act.wait_ge(r_s, t - 1)
                act.activation(xT[:, u, :], ps[:, u, 0:P], ACT.Copy).then_inc(xe_s, 1)

            run_pairs(act, T, body)
            act.wait_ge(w_s, 1)
            act.activation(score[:, :, :], score[:, :, :], ACT.Sigmoid).then_inc(sig_s, 1)

        @block.tensor
        def _(pe):
            pe.wait_ge(cst, 48)

            def body(t, u, i, first, last):
                pe.wait_ge(xn_s, t + 1)
                if not (isinstance(t, int) and t < 2):
                    pe.wait_ge(xe_s, t - 1)
                pe.transpose(ps[:, u, 0:P], xn[:, u, :], w["ident"][:, :]).then_inc(xT_s, 1)
                pe.wait_ge(xe_s, t + 1)
                pe.matmul(pr[:, t, :] if isinstance(t, int) else pr[:, bass.ds(t, 1), :].rearrange("p t e -> p (t e)"),
                          xT[:, u, :], gw[:, :], start=True, stop=True).then_inc(r_s, 1)

            run_pairs(pe, T, body)


def experts_block(nc, ctx, w, d, x2d, xnTd, gate_all, out, T):
    NE = E + 1
    def sem(n):
        return ctx.enter_context(nc.semaphore(n))

    cst = sem("e_weights")
    xl, x2l, st = ([sem(f"e_{n}{u}") for u in range(2)] for n in ("xT_loaded", "x2_loaded", "out_stored"))
    up_s, gl_s, dn_s, acc_s, fin = sem("e_up"), sem("e_gelu"), sem("e_down"), sem("e_added"), sem("e_final")
    step_s = sem("e_steps")
    with ExitStack() as c:
        def sb(n, s):
            return c.enter_context(nc.sbuf_tensor(n, s, F32))

        up, down = sb("up_sb", [P, NE, FB * P]), sb("down_sb", [P, NE, FB, P])
        ub, db = sb("up_bias", [P, NE, FB]), sb("down_bias", [P, NE, P])
        xT, x2 = sb("e_xT", [P, 2, P]), sb("e_x2", [P, 2, P])
        hid = sb("e_hidden", [P, 2, FB, P])
        acc, top, o = sb("e_acc", [P, P]), sb("e_top", [P, 1]), sb("e_out", [P, 2, P])
        ph = c.enter_context(nc.psum_tensor("e_up_psum", [P, 2, FB, P], F32))
        pd = c.enter_context(nc.psum_tensor("e_down_psum", [P, 2, BANK], F32))
        block = c.enter_context(nc.Block())

        @block.sync
        def _(sp):
            sp.dma_start(up[:, :, :], d["up"].rearrange("e p n -> p e n")).then_inc(cst, 16)
            for e in range(NE):
                sp.dma_start(down[:, e, :, :], d["down"][e].rearrange("(j p) n -> p j n", p=P)).then_inc(cst, 16)
            sp.dma_start(ub[:, :, :], d["up_b"]).then_inc(cst, 16)
            sp.dma_start(db[:, :, :], d["down_b"].partition_broadcast(P)).then_inc(cst, 16)
            for t in range(2):
                sp.dma_start(xT[:, t, :], xnTd[t]).then_inc(xl[t], 16)
                sp.dma_start(x2[:, t, :], x2d[at(t, P), :]).then_inc(x2l[t], 16)

            def body(t, u, i, first, last):
                sp.wait_ge(fin, t + 1)
                sp.dma_start(out[at(t, P), :], o[:, u, :]).then_inc(st[u], 16)
                if not (isinstance(t, int) and t + 2 >= T):
                    sp.wait_ge(up_s, NE * (t + 1))
                    sp.dma_start(xT[:, u, :], xnTd[at(t + 2, 1)].rearrange("t p n -> (t p) n")).then_inc(xl[u], 16)
                    sp.dma_start(x2[:, u, :], x2d[at(t + 2, P), :]).then_inc(x2l[u], 16)

            run_pairs(sp, T, body)
            for u in range(2):
                sp.wait_ge(st[u], 16 * (T // 2))

        def number(t, e):
            return NE * t + e

        def buf(u, e):
            return (u * NE + e) % 2

        @block.scalar
        def _(act):
            act.wait_ge(cst, 16 * (NE + 3))

            def body(t, u, i, first, last):
                for e in range(NE):
                    b = buf(u, e)
                    act.wait_ge(up_s, number(t, e) + 1)
                    if not first or e >= 2:
                        act.wait_ge(dn_s, number(t, e) - 1)
                    for j in range(FB):
                        ins = act.activation(hid[:, b, j, :], ph[:, b, j, :], ACT.Gelu, bias=ub[:, e, j:j + 1])
                    ins.then_inc(gl_s, 1)

            run_pairs(act, T, body)

        @block.vector
        def _(dve):
            dve.wait_ge(cst, 16 * (NE + 3))

            def body(t, u, i, first, last):
                def gate(e):
                    return gate_all[:, t, e:e + 1] if isinstance(t, int) else gate_all[:, bass.ds(t, 1), e:e + 1].rearrange("p t e -> p (t e)")

                n = 0
                steps = NE + 4

                def step(ins):
                    nonlocal n
                    ins.then_inc(step_s, 1)
                    n += 1
                    dve.wait_ge(step_s, steps * t + n)

                if not first:
                    dve.wait_ge(fin, t)
                step(dve.tensor_copy(acc[:, :], db[:, E, :]))
                for e in range(E):
                    step(dve.scalar_tensor_tensor(acc[:, :], db[:, e, :], gate(e), acc[:, :], ALU.mult, ALU.add))
                for e in range(NE):
                    dve.wait_ge(dn_s, number(t, e) + 1)
                    src = pd[:, buf(u, e), 0:P]
                    if e < E:
                        ins = dve.scalar_tensor_tensor(acc[:, :], src, gate(e), acc[:, :], ALU.mult, ALU.add)
                    else:
                        ins = dve.tensor_tensor(acc[:, :], src, acc[:, :], ALU.add)
                    ins.then_inc(acc_s, 1)
                    dve.wait_ge(acc_s, number(t, e) + 1)
                step(dve.tensor_scalar(acc[:, :], acc[:, :], 0.1, None, ALU.mult))
                step(dve.tensor_reduce(top[:, :], acc[:, :], X, ALU.max, apply_absolute_value=True))
                step(dve.tensor_scalar(top[:, :], top[:, :], 1e-6, None, ALU.add))
                step(dve.reciprocal(top[:, :], top[:, :]))
                dve.wait_ge(x2l[u], 16 * (i + 1))
                if not (isinstance(t, int) and t < 2):
                    dve.wait_ge(st[u], 16 * i)
                dve.scalar_tensor_tensor(o[:, u, :], acc[:, :], top[:, 0:1], x2[:, u, :], ALU.mult, ALU.add).then_inc(fin, 1)

            run_pairs(dve, T, body)

        @block.tensor
        def _(pe):
            pe.wait_ge(cst, 16 * (NE + 3))

            def down_proj(t, u, e):
                b = buf(u, e)
                pe.wait_ge(gl_s, number(t, e) + 1)
                if not (isinstance(t, int) and number(t, e) < 2):
                    pe.wait_ge(acc_s, number(t, e) - 1)
                for j in range(FB):
                    mm = pe.matmul(pd[:, b, 0:P], hid[:, b, j, :], down[:, e, j, :], start=(j == 0), stop=(j == FB - 1))
                mm.then_inc(dn_s, 1)

            def body(t, u, i, first, last):
                pe.wait_ge(xl[u], 16 * (i + 1))
                for e in range(NE):
                    b = buf(u, e)
                    if not first or e >= 2:
                        pe.wait_ge(gl_s, number(t, e) - 1)
                    for j in range(FB):
                        mm = pe.matmul(ph[:, b, j, :], up[:, e, j * P:(j + 1) * P], xT[:, u, :], start=True, stop=True)
                    mm.then_inc(up_s, 1)
                    if e >= 1:
                        down_proj(t, u, e - 1)
                down_proj(t, u, E)

            run_pairs(pe, T, body)


def build(nc, a, out, T):
    with ExitStack() as ctx:
        def keep(n, s, dt=F32):
            return ctx.enter_context(nc.sbuf_tensor(n, s, dt))

        w = {
            "ident": keep("identity_sb", [P, P]), "kron": keep("gate_weights_spread", [P, 16 * H]),
            "ones": keep("ones", [P, P], BF16), "minus_half": keep("minus_half", [P, 1]),
            "quarter": keep("quarter_turn", [P, 1]), "split": keep("projection_parts", [P, 4, 2, H * DK], BF16),
            "brows": keep("bias_parts", [P, 2 * H * DK + 16 * H], BF16), "ybias": keep("out_bias", [P, P]),
            "qbd": keep("q_block_diagonal", [P, H, P]), "pbd": keep("probs_block_diagonal", [P, H, P]),
            "v": keep("values_and_one", [P, H, DK + 1]),
        }
        gate_all = keep("gates", [P, T, E])

        def scratch(n, s):
            return nc.dram_tensor(n, s, F32).ap()

        ft, mtab = scratch("features_dram", [T, P, BANK]), scratch("key_table_dram", [2 * T, S * NB])
        x2d, xnTd = scratch("x2_dram", [T * P, P]), scratch("xnT_dram", [T, P, P])
        setup_block(nc, ctx, w, a)
        relations_block(nc, ctx, w, a, ft, mtab, T)
        attention_block(nc, ctx, w, a, ft, x2d, T)
        router_block(nc, ctx, w, a, x2d, xnTd, gate_all, T)
        experts_block(nc, ctx, w, a, x2d, xnTd, gate_all, out, T)


def kernel(**inputs):
    import numpy as np
    import concourse.bacc as bacc
    from concourse.bass_utils import run_bass_kernel_spmd as run

    g = {k.replace("L0_xattn_", "").replace("L0_ffn_", "f_"): np.asarray(v) for k, v in inputs.items()}
    tokens = g["x"].shape[0] * g["x"].shape[1]
    kron = np.zeros((16, NF, 16, H), np.float32)
    for m in range(16):
        kron[m, :, m, :] = g["Wg"].T
    bf = np.concatenate
    lay = {
        "x": g["x"].reshape(tokens, P), "ctxT": g["ctx_1024"].reshape(tokens, P).T,
        "boxes": g["fside_BxSx4_0"].reshape(tokens, NB),
        "wq": g["Wq"].T, "wk": g["Wk"].T, "wv": g["Wv"].T,
        "wo": g["Wo"].T.reshape(HP, P, P).transpose(1, 0, 2).reshape(P, H * DK),
        "bv": g["bv"].reshape(HP, P).T, "bo": g["bo"],
        "bias_rows": bf([g["bq"], g["bk"], np.tile(g["bg"], 16)]),
        "kron": kron.reshape(P, 16 * H), "ident": np.eye(P, dtype=np.float32),
        "gate_w": g["f_gate_w"], "gate_b": g["f_bias"], "numbers": np.arange(E, dtype=np.float32),
        "up": bf([g["f_up_w"], g["f_sw_up"][None]]), "down": bf([g["f_down_w"], g["f_sw_down"][None]]),
        "up_b": bf([g["f_up_b"], g["f_sb_up"][None]]).reshape(E + 1, FB, P).transpose(2, 0, 1),
        "down_b": bf([g["f_down_b"], g["f_sb_down"][None]]),
    }
    nc = bacc.Bacc("TRN2", target_bir_lowering=False, num_devices=1)
    arrays, a = {}, {}
    for n, v in lay.items():
        arrays["in_" + n] = np.ascontiguousarray(v)
        a[n] = nc.dram_tensor("in_" + n, v.shape, F32, kind="ExternalInput").ap()
    out = nc.dram_tensor("out", (tokens, P), F32, kind="ExternalOutput").ap()
    build(nc, a, out, tokens // P)
    r = run(nc, [arrays], core_ids=[0])
    return r.results[0]["out"].reshape(g["x"].shape)
```

```python
from contextlib import ExitStack
from math import pi

import concourse.bass as bass
from concourse import mybir

F32 = mybir.dt.float32
BF16 = mybir.dt.bfloat16
I32 = mybir.dt.int32
U32 = mybir.dt.uint32
ALU = mybir.AluOpType
ACT = mybir.ActivationFunctionType
X = mybir.AxisListType.X

P = 128
S = 64
H = 16
DK = 64
HP = H // 2
NB = 4
Q = 4
U = 2
NF = 8
E = 8
FB = 4
LN_EPS = 1e-5
ROW = P + 1
NOWHERE = 1 << 30
BANK = 512
ROUND = 1.5 * 2.0 ** 23
NO_SIGN = 0x7FFFFFFF
TURNS = 100.0 / (2 * pi)
SIN_SCALE = 6.283185


def run_tiles(eng, tiles, ways, body):
    turns, ahead = tiles // ways, max(1, 4 // ways)
    if turns <= ahead + 1:
        for t in range(tiles):
            body(t, t % ways, t // ways, t == 0, t == tiles - 1)
        return
    for t in range(ahead * ways):
        body(t, t % ways, t // ways, t == 0, False)
    with eng.Fori(ahead, turns - 1) as i:
        for u in range(ways):
            body(i * ways + u, u, i, False, False)
    for t in range(tiles - ways, tiles):
        body(t, t % ways, t // ways, False, t == tiles - 1)


def run_pairs(eng, tiles, body):
    run_tiles(eng, tiles, 2, body)


def hold(eng, mark):
    eng.sem_inc(mark, 1)


def at(t, size):
    return slice(t * size, (t + 1) * size) if isinstance(t, int) else bass.ds(t * size, size)


def tile_of(x, c, q):
    if isinstance(c, int):
        return x[:, c * Q + q, :]
    return x[:, bass.ds(c * Q + q, 1), :].rearrange("p t n -> p (t n)")


def setup_block(nc, ctx, w, d):
    ld = ctx.enter_context(nc.semaphore("weights_loaded"))
    brd = ctx.enter_context(nc.semaphore("bias_rows_loaded"))
    hi = ctx.enter_context(nc.semaphore("high_parts"))
    lo = ctx.enter_context(nc.semaphore("low_parts"))
    cst = ctx.enter_context(nc.semaphore("constants_set"))
    spread = ctx.enter_context(nc.semaphore("value_bias_spread"))
    prod = ctx.enter_context(nc.semaphore("value_bias_projected"))
    step = ctx.enter_context(nc.semaphore("bias_split_steps"))
    with ExitStack() as c:
        raw = c.enter_context(nc.sbuf_tensor("raw_weights", [P, 4, H * DK], F32))
        nb = 2 * H * DK + 16 * H
        braw = c.enter_context(nc.sbuf_tensor("raw_bias_rows", [P, nb], F32))
        bpart = c.enter_context(nc.sbuf_tensor("bias_part", [P, nb], BF16))
        bvs = c.enter_context(nc.sbuf_tensor("value_bias_spread_sb", [P, HP, P], F32))
        bvc = c.enter_context(nc.sbuf_tensor("value_bias_cols", [P, HP], F32))
        bob = c.enter_context(nc.sbuf_tensor("out_bias_rows", [P, P], F32))
        yb = c.enter_context(nc.psum_tensor("bias_psum", [P, P], F32))
        block = c.enter_context(nc.Block())

        @block.sync
        def _(sp):
            for n, name in enumerate(("wq", "wk", "wv", "wo")):
                sp.dma_start(raw[:, n, :], d[name]).then_inc(ld, 16)
            sp.dma_start(bvc[:, :], d["bv"]).then_inc(ld, 16)
            sp.dma_start(bob[:, :], d["bo"].partition_broadcast(P)).then_inc(ld, 16)
            sp.dma_start(w["ident"][:, :], d["ident"]).then_inc(ld, 16)
            sp.dma_start(w["kron"][:, :], d["kron"]).then_inc(ld, 16)
            sp.dma_start(braw[:, :], d["bias_rows"].partition_broadcast(P)).then_inc(brd, 16)
            sp.wait_ge(ld, 16 * 8)

        @block.scalar
        def _(act):
            act.wait_ge(ld, 16 * 8)
            for n in range(4):
                act.activation(w["split"][:, n, 0, :], raw[:, n, :], ACT.Copy).then_inc(hi, 1)

        @block.gpsimd
        def _(pool):
            for name in ("qbd", "pbd"):
                pool.memset(w[name][:, :, :], 0.0).then_inc(cst, 1)
            pool.memset(w["ones"][:, :], 1.0).then_inc(cst, 1)
            pool.memset(w["minus_half"][:, :], -0.5).then_inc(cst, 1)
            pool.memset(w["quarter"][:, :], pi / 2).then_inc(cst, 1)
            pool.wait_ge(cst, 5)

        @block.vector
        def _(dve):
            dve.memset(w["brows"][:, :], 0.0).then_inc(step, 1)
            dve.wait_ge(brd, 16)
            for n, row in enumerate((0, 32, 64)):
                dve.wait_ge(step, 1 + 3 * n)
                dve.tensor_copy(bpart[:, :], braw[:, :]).then_inc(step, 1)
                dve.wait_ge(step, 2 + 3 * n)
                dve.tensor_copy(w["brows"][row:row + 1, :], bpart[row:row + 1, :]).then_inc(step, 1)
                dve.tensor_tensor(braw[:, :], braw[:, :], bpart[:, :], ALU.subtract).then_inc(step, 1)
            dve.wait_ge(ld, 16 * 8)
            for n in range(4):
                dve.wait_ge(hi, n + 1)
                dve.tensor_tensor(w["split"][:, n, 1, :], raw[:, n, :], w["split"][:, n, 0, :],
                                  ALU.subtract).then_inc(lo, 1)
            for j in range(HP):
                dve.tensor_copy(bvs[:, j, :], bvc[:, j:j + 1].to_broadcast([P, P])).then_inc(spread, 1)
            dve.wait_ge(prod, 1)
            dve.tensor_tensor(w["ybias"][:, :], yb[:, :], bob[:, :], ALU.add).then_inc(lo, 1)
            dve.wait_ge(lo, 5)

        @block.tensor
        def _(pe):
            pe.wait_ge(spread, HP)
            for j in range(HP):
                mm = pe.matmul(yb[:, :], bvs[:, j, :], raw[:, 3, j * P:(j + 1) * P],
                               start=(j == 0), stop=(j == HP - 1))
            mm.then_inc(prod, 1)


def relations_block(nc, ctx, w, d, ft, mtab, T):
    G = min(16, T // 2)
    NG = T // G

    def sem(n):
        return ctx.enter_context(nc.semaphore(n))

    boxes_ld, own_step, own_ready, tab_st = sem("boxes_loaded"), sem("own_steps"), sem("own_ready"), sem("table_stored")
    keys_ld = [sem("key_boxes_loaded0"), sem("key_boxes_loaded1")]
    dif_s, siz_s, sca_s, clip_s, log_s = sem("differences"), sem("size_ratios"), sem("scaled"), sem("clipped"), sem("logs")
    rnd_s, frc_s, sin_s, cos_s, turn_s = sem("rounding"), sem("fractions"), sem("sines"), sem("cosines"), sem("turned")
    abs_s = sem("absolute")
    out_s = [sem("turned_out_dve"), sem("turned_out_act")]
    st_s = [sem("features_stored0"), sem("features_stored1")]
    with ExitStack() as c:
        def sb(n, s):
            return c.enter_context(nc.sbuf_tensor(n, s, F32))

        box = sb("boxes", [P, T, NB])
        cen, size, rsz = sb("centres", [P, T, 2]), sb("box_sizes", [P, T, 2]), sb("inverse_sizes", [P, T, 2])
        mrow = sb("centre_and_inverse", [P, T, NB])
        keys = sb("key_side", [P, 2, G, S * NB])
        dist = sb("distances", [P, 2, G, NB, S])
        whole, frac, afrac = sb("whole_turns", [P, G, NB, S]), sb("part_turns", [P, G, NB, S]), sb("abs_part", [P, G, NB, S])
        feat = sb("features_sb", [P, G, S, NF])
        fto = sb("turned_features", [P, 2, BANK])
        ps = c.enter_context(nc.psum_tensor("turn_psum", [P, 2, BANK], F32))
        block = c.enter_context(nc.Block())

        def flat(x):
            return x.rearrange("p g c m -> p (g c m)")

        def tile_pairs(eng, g, body):
            if g == 0:
                for u in range(2):
                    body(u, u, 0, True)
            with eng.Fori(1 if g == 0 else 0, G // 2) as i:
                for u in range(2):
                    body(i * 2 + u, u, i + g * (G // 2), False)

        @block.sync
        def _(sp):
            sp.dma_start(box[:, :, :], d["boxes"].rearrange("(t p) c -> p t c", p=P)).then_inc(boxes_ld, 16)
            sp.wait_ge(own_ready, 1)
            sp.dma_start(mtab.rearrange("b (m c) -> (b m) c", c=NB).rearrange("(t p) c -> p t c", p=P),
                         mrow[:, :, :]).then_inc(tab_st, 16)
            sp.wait_ge(tab_st, 16)

            def load(g):
                if g >= 2:
                    sp.wait_ge(dif_s, g - 1)
                    sp.wait_ge(siz_s, g - 1)
                for b in range(2):
                    src = mtab[g * 2 * G:(g + 1) * 2 * G, :].rearrange("(t b) n -> b t n", b=2)[b]
                    sp.dma_start(keys[b * S:(b + 1) * S, g % 2, :, :], src.partition_broadcast(S)).then_inc(keys_ld[g % 2], 16)

            def store(k, u, n, first):
                sp.wait_ge(out_s[u], n + 1)
                sp.dma_start(ft[at(n * 2 + u, 1)].rearrange("t p n -> (t p) n"), fto[:, u, :]).then_inc(st_s[u], 16)

            load(0)
            for g in range(NG):
                if g + 1 < NG:
                    load(g + 1)
                tile_pairs(sp, g, store)
            for u in range(2):
                sp.wait_ge(st_s[u], 16 * (T // 2))

        @block.vector
        def _(dve):
            dve.wait_ge(boxes_ld, 16)
            dve.tensor_tensor(cen[:, :, :], box[:, :, 0:2], box[:, :, 2:4], ALU.add).then_inc(own_step, 1)
            dve.tensor_tensor(size[:, :, :], box[:, :, 2:4], box[:, :, 0:2], ALU.subtract).then_inc(own_step, 1)
            dve.wait_ge(own_step, 2)
            dve.tensor_scalar(cen[:, :, :], cen[:, :, :], 0.5, None, ALU.mult).then_inc(own_step, 1)
            dve.tensor_scalar(size[:, :, :], size[:, :, :], 1.0, None, ALU.add).then_inc(own_step, 1)
            dve.wait_ge(own_step, 4)
            dve.reciprocal(rsz[:, :, :], size[:, :, :]).then_inc(own_step, 1)
            dve.tensor_copy(mrow[:, :, 0:2], cen[:, :, :]).then_inc(own_step, 1)
            dve.wait_ge(own_step, 6)
            dve.tensor_copy(mrow[:, :, 2:4], rsz[:, :, :]).then_inc(own_ready, 1)

            def copy_out(k, u, n, first):
                if u:
                    return
                dve.wait_ge(turn_s, n * 2 + 1)
                if not first:
                    dve.wait_ge(st_s[0], n * 16)
                dve.tensor_copy(fto[:, 0, :], ps[:, 0, :]).then_inc(out_s[0], 1)

            for g in range(NG):
                u = g % 2
                own_c = cen[:, g * G:(g + 1) * G, :].unsqueeze(3).to_broadcast([P, G, 2, S])
                dve.wait_ge(keys_ld[u], 32 * (g // 2 + 1))
                dve.tensor_tensor(dist[:, u, :, 0:2, :], keys[:, u, :, :].rearrange("p g (m c) -> p g c m", c=NB)[:, :, 0:2, :],
                                  own_c, ALU.subtract).then_inc(dif_s, 1)
                dve.wait_ge(sca_s, g + 1)
                shift = dist[:, u, :, 0:2, :]
                dve.tensor_scalar(shift.bitcast(I32), shift.bitcast(I32), NO_SIGN, None, ALU.bitwise_and).then_inc(abs_s, 1)
                dve.wait_ge(abs_s, g + 1)
                dve.tensor_scalar(shift, shift, 1e-3, None, ALU.max).then_inc(clip_s, 1)
                dve.wait_ge(log_s, g + 1)
                L, W, Fr, A = flat(dist[:, u]), flat(whole[:, :, :, :]), flat(frac[:, :, :, :]), flat(afrac[:, :, :, :])
                dve.tensor_scalar(W, L, TURNS, ROUND, ALU.mult, ALU.add).then_inc(rnd_s, 1)
                dve.wait_ge(rnd_s, 2 * g + 1)
                dve.tensor_scalar(W, W, ROUND, None, ALU.subtract).then_inc(rnd_s, 1)
                dve.wait_ge(rnd_s, 2 * g + 2)
                if g >= 1:
                    dve.wait_ge(cos_s, g)
                dve.scalar_tensor_tensor(Fr, L, TURNS, W, ALU.mult, ALU.subtract).then_inc(frc_s, 1)
                dve.wait_ge(frc_s, 2 * g + 1)
                dve.tensor_scalar(A.bitcast(I32), Fr.bitcast(I32), NO_SIGN, None, ALU.bitwise_and).then_inc(frc_s, 1)
                tile_pairs(dve, g, copy_out)

        @block.gpsimd
        def _(pool):
            pool.wait_ge(own_ready, 1)
            for g in range(NG):
                u = g % 2
                tiles = slice(g * G, (g + 1) * G)
                pool.wait_ge(keys_ld[u], 32 * (g // 2 + 1))
                if g >= 2:
                    pool.wait_ge(frc_s, 2 * (g - 2) + 1)
                pool.tensor_tensor(dist[:, u, :, 2:4, :], keys[:, u, :, :].rearrange("p g (m c) -> p g c m", c=NB)[:, :, 2:4, :],
                                   size[:, tiles, :].unsqueeze(3).to_broadcast([P, G, 2, S]), ALU.mult).then_inc(siz_s, 1)
                pool.wait_ge(dif_s, g + 1)
                pool.tensor_tensor(dist[:, u, :, 0:2, :], dist[:, u, :, 0:2, :],
                                   rsz[:, tiles, :].unsqueeze(3).to_broadcast([P, G, 2, S]), ALU.mult).then_inc(sca_s, 1)

        @block.scalar
        def _(act):
            def copy_out(k, u, n, first):
                if not u:
                    return
                act.wait_ge(turn_s, n * 2 + 2)
                if not first:
                    act.wait_ge(st_s[1], n * 16)
                act.activation(fto[:, 1, :], ps[:, 1, :], ACT.Copy).then_inc(out_s[1], 1)

            for g in range(NG):
                act.wait_ge(clip_s, g + 1)
                act.wait_ge(siz_s, g + 1)
                act.activation(flat(dist[:, g % 2]), flat(dist[:, g % 2]), ACT.Ln).then_inc(log_s, 1)
                fv = feat[:, :, :, :].rearrange("p g m f -> p g f m")
                if g >= 1:
                    act.wait_ge(turn_s, g * G)
                act.wait_ge(frc_s, 2 * g + 1)
                act.activation(fv[:, :, 0:NB, :], frac[:, :, :, :], ACT.Sin, scale=SIN_SCALE).then_inc(sin_s, 1)
                act.wait_ge(frc_s, 2 * g + 2)
                act.activation(fv[:, :, NB:NF, :], afrac[:, :, :, :], ACT.Sin, bias=w["quarter"][:, 0:1],
                               scale=-SIN_SCALE).then_inc(cos_s, 1)
                tile_pairs(act, g, copy_out)

        @block.tensor
        def _(pe):
            def turn(g, k, wait_out):
                u, n = k % 2, k // 2 + g * (G // 2)
                if wait_out:
                    pe.wait_ge(out_s[u], n)
                row = feat[:, k, :, :].rearrange("p m f -> p (m f)")
                for q in range(NB):
                    mm = pe.transpose(ps[:, u, q * P:(q + 1) * P], row[:, q * P:(q + 1) * P], w["ident"][:, :])
                mm.then_inc(turn_s, 1)

            pe.wait_ge(cos_s, 1)
            for k in range(G):
                turn(0, k, k >= 2)
            with pe.Fori(1, NG) as g:
                pe.wait_ge(cos_s, g + 1)
                for k in range(G):
                    turn(g, k, True)


def attention_block(nc, ctx, w, d, ft, x2d, T):
    sem = lambda n: ctx.enter_context(nc.semaphore(n))
    ch_s = sem("ctx_high")
    held_dve, held_pool = sem("held_dve"), sem("held_pool")
    x_ld, c_ld, f_ld = ([sem(f"{n}_loaded{u}") for u in range(2)] for n in ("x", "ctx", "features"))
    x2_st = [sem("x2_stored0"), sem("x2_stored1")]
    stats, rstd, xn_s, xb_s, c_s = sem("ln_stats"), sem("ln_rstd"), sem("x_normed"), sem("x_biased"), sem("ctx_split")
    xT_s, xh_s, xl_s = sem("x_turned"), sem("xT_high"), sem("xT_low")
    q_s, k_s, v_s = sem("q_done"), sem("k_done"), sem("v_done")
    qa, ka, kd, va = sem("q_out"), sem("k_out_act"), sem("k_out_dve"), sem("v_out")
    sc_s, g_s, mx_s, sub_s, exp_s, p_s = sem("scores_done"), sem("gates_done"), sem("row_max"), sem("shifted"), sem("exps"), sem("probs")
    pT_s, pa, pd = sem("probs_turned"), sem("probs_out_act"), sem("probs_out_dve")
    gated, summed, inverted = sem("exps_gated"), sem("exps_summed"), sem("sums_inverted")
    o_s, oh_s, ol_s, y_s, x2_s = (sem(n) for n in ("heads_done", "headsT_high", "headsT_low", "attn_out", "x2_ready"))
    with ExitStack() as c:
        sb = lambda n, s, dt=F32: c.enter_context(nc.sbuf_tensor(n, s, dt))
        xt, xn, xb = sb("x_tile", [P, 2, P]), sb("x_norm", [P, 2, P]), sb("x_plus_bias", [P, 2, P])
        ct, cT = sb("ctxT_tile", [P, 2, P]), sb("ctxT_parts", [P, 2, 2, P], BF16)
        xT = sb("xT_parts", [P, 2, P], BF16)
        fts = sb("feature_tile", [P, 2, BANK])
        st6, mv, var, rs = sb("bn", [P, 2, 6]), sb("mean_var", [P, 2, 2]), sb("var_eps", [P, 2, 1]), sb("rstd", [P, 2, 1])
        kT = sb("kT", [P, H, S])
        z, mx = sb("logits", [P, H, S]), sb("row_maximum", [P, H])
        total, inv = sb("exp_sums", [P, H]), sb("inverse_sums", [P, H])
        oT = sb("headsT_parts", [P, 2, HP, P], BF16)
        x2 = sb("x2_tile", [P, 2, P])
        ps = c.enter_context(nc.psum_tensor("attn_psum", [P, 8, BANK], F32))
        flat = ps[:, :, :].rearrange("p b n -> p (b n)")
        SC = flat[:, 0:2 * BANK].rearrange("p (h k) -> p h k", k=S)
        GA = flat[:, 2 * BANK:4 * BANK]
        XQ = flat[:, 4 * BANK:6 * BANK].rearrange("p (j n) -> p j n", n=P)
        YT = flat[:, 6 * BANK:8 * BANK].rearrange("p (j n) -> p j n", n=P)
        KP = flat[:, 0:2 * BANK].rearrange("p (j n) -> p j n", n=P)
        AO = ps[:, 6, 0:P]
        qbd, pbd, v, split = w["qbd"], w["pbd"], w["v"], w["split"]
        block = c.enter_context(nc.Block())

        @block.sync
        def _(sp):
            def loads(t, u, wait_free):
                if wait_free:
                    sp.wait_ge(xb_s, t - 1)
                    sp.wait_ge(xn_s, t - 1)
                    sp.wait_ge(c_s, t - 1)
                sp.dma_start(xt[:, u, :], d["x"][at(t, P), :]).then_inc(x_ld[u], 16)
                sp.dma_start(ct[:, u, :], d["ctxT"][:, at(t, P)]).then_inc(c_ld[u], 16)
                if wait_free:
                    sp.wait_ge(g_s, t - 1)
                sp.dma_start(fts[:, u, :], ft[at(t, 1)].rearrange("t p n -> (t p) n")).then_inc(f_ld[u], 16)

            def body(t, u, i, first, last):
                if not first:
                    sp.wait_ge(x2_s, t)
                    sp.dma_start(x2d[at(t - 1, P), :], x2[:, 1 - u, :]).then_inc(x2_st[1 - u], 16)
                if not (isinstance(t, int) and t + 2 >= T):
                    loads(t + 2, u, True)

            loads(0, 0, False)
            loads(1, 1, False)
            run_pairs(sp, T, body)
            sp.wait_ge(x2_s, T)
            sp.dma_start(x2d[at(T - 1, P), :], x2[:, 1, :]).then_inc(x2_st[1], 16)
            for u in range(2):
                sp.wait_ge(x2_st[u], 16 * (T // 2))

        @block.gpsimd
        def _(pool):
            def prepare(t, u, i):
                pool.wait_ge(stats, 2 * t + 2)
                hold(pool, held_pool)
                pool.tensor_scalar(var[:, u, :], mv[:, u, 1:2], LN_EPS, None, ALU.add).then_inc(rstd, 1)
                pool.wait_ge(rstd, 2 * t + 1)
                pool.tensor_tensor(rs[:, u, :], var[:, u, :], w["minus_half"][:, :], ALU.pow).then_inc(rstd, 1)
                pool.wait_ge(rstd, 2 * t + 2)
                hold(pool, held_pool)
                pool.tensor_scalar(xn[:, u, :], xt[:, u, :], mv[:, u, 0:1], rs[:, u, :],
                                   ALU.subtract, ALU.mult).then_inc(xn_s, 1)
                pool.wait_ge(c_ld[u], 16 * (i + 1))
                if not (isinstance(t, int) and t < 2):
                    pool.wait_ge(v_s, t - 1)
                hold(pool, held_pool)
                pool.tensor_copy(cT[:, u, 0, :], ct[:, u, :]).then_inc(ch_s, 1)
                pool.wait_ge(ch_s, t + 1)
                pool.tensor_tensor(cT[:, u, 1, :], ct[:, u, :], cT[:, u, 0, :], ALU.subtract).then_inc(c_s, 1)
                if not (isinstance(t, int) and t < 2):
                    pool.wait_ge(x2_s, t - 1)
                pool.tensor_tensor(xb[:, u, :], xt[:, u, :], w["ybias"][:, :], ALU.add).then_inc(xb_s, 1)

            def body(t, u, i, first, last):
                if not last:
                    if not first:
                        pool.wait_ge(xT_s, t)
                    prepare(t + 1, 1 - u, i + u)

            prepare(0, 0, 0)
            run_pairs(pool, T, body)

        @block.vector
        def _(dve):
            def norm_stats(t, u, i):
                dve.wait_ge(x_ld[u], 16 * (i + 1))
                dve.bn_stats(st6[:, u, :], xt[:, u, :]).then_inc(stats, 1)
                dve.wait_ge(stats, 2 * t + 1)
                hold(dve, held_dve)
                dve.bn_aggr(mv[:, u, :], st6[:, u, :]).then_inc(stats, 1)

            def low_xT(t):
                dve.wait_ge(xh_s, t + 1)
                dve.tensor_tensor(xT[:, 1, :], XQ[:, 0, :], xT[:, 0, :], ALU.subtract).then_inc(xl_s, 1)

            def k_out(t):
                dve.wait_ge(k_s, t + 1)
                for b in range(2):
                    ins = dve.tensor_copy(kT[b * S:(b + 1) * S, 1:H:2, :], KP[S:P, :, b * S:(b + 1) * S])
                ins.then_inc(kd, 1)

            def low_oT(t):
                dve.wait_ge(oh_s, t + 1)
                dve.tensor_tensor(oT[:, 1, :, :], YT, oT[:, 0, :, :], ALU.subtract).then_inc(ol_s, 1)

            def add_out(t, u, i):
                dve.wait_ge(y_s, t + 1)
                dve.wait_ge(xb_s, t + 1)
                if not (isinstance(t, int) and t < 2):
                    dve.wait_ge(x2_st[u], 16 * i)
                dve.tensor_tensor(x2[:, u, :], AO, xb[:, u, :], ALU.add).then_inc(x2_s, 1)

            norm_stats(0, 0, 0)
            low_xT(0)
            k_out(0)

            def body(t, u, i, first, last):
                if not last:
                    if not first:
                        dve.wait_ge(xn_s, t)
                    norm_stats(t + 1, 1 - u, i + u)
                if not first:
                    low_oT(t - 1)
                dve.wait_ge(sc_s, t + 1)
                dve.tensor_reduce(mx[:, :], SC, X, ALU.max).then_inc(mx_s, 1)
                dve.wait_ge(mx_s, t + 1)
                dve.tensor_tensor(z[:, :, :], SC, mx[:, :].unsqueeze(2).to_broadcast([P, H, S]), ALU.subtract).then_inc(sub_s, 1)
                if not last:
                    low_xT(t + 1)
                if not first:
                    add_out(t - 1, 1 - u, i - 1 + u)
                dve.wait_ge(exp_s, t + 1)
                dve.wait_ge(g_s, t + 1)
                dve.scalar_tensor_tensor(z[:, :, :], GA.rearrange("p (m h) -> p h m", h=H), 1e-6, z[:, :, :],
                                         ALU.max, ALU.mult).then_inc(gated, 1)
                dve.wait_ge(gated, t + 1)
                dve.tensor_reduce(total[:, :], z[:, :, :], X, ALU.add).then_inc(summed, 1)
                dve.wait_ge(summed, t + 1)
                dve.reciprocal(inv[:, :], total[:, :]).then_inc(inverted, 1)
                dve.wait_ge(inverted, t + 1)
                dve.tensor_tensor(z[:, :, :], z[:, :, :], inv[:, :].unsqueeze(2).to_broadcast([P, H, S]), ALU.mult).then_inc(p_s, 1)
                if not last:
                    k_out(t + 1)
                dve.wait_ge(pT_s, t + 1)
                for b in range(2):
                    ins = dve.tensor_copy(pbd[b * S:(b + 1) * S, 1:H:2, b * S:(b + 1) * S], YT[S:P, :, b * S:(b + 1) * S])
                ins.then_inc(pd, 1)

            run_pairs(dve, T, body)
            low_oT(T - 1)
            add_out(T - 1, 1, T // 2 - 1)

        @block.scalar
        def _(act):
            def high_xT(t):
                act.wait_ge(xT_s, t + 1)
                act.activation(xT[:, 0, :], XQ[:, 0, :], ACT.Copy).then_inc(xh_s, 1)

            def out_halves(done, out, src, dst, t, wide, halves):
                act.wait_ge(done, t + 1)
                for half in range(halves):
                    for b in range(2):
                        cols = slice(b * S, (b + 1) * S)
                        to = dst[b * S:(b + 1) * S, half:H:2, cols if wide else slice(0, S)]
                        ins = act.activation(to, src[half * S:(half + 1) * S, :, cols], ACT.Copy)
                ins.then_inc(out, 1)

            def v_out(t):
                act.wait_ge(v_s, t + 1)
                if not (isinstance(t, int) and t < 1):
                    act.wait_ge(o_s, t)
                act.activation(v[:, :, :], XQ.rearrange("p j (e n) -> p (j e) n", e=2), ACT.Copy).then_inc(va, 1)

            def high_oT(t):
                act.wait_ge(o_s, t + 1)
                act.activation(oT[:, 0, :, :], YT, ACT.Copy).then_inc(oh_s, 1)

            high_xT(0)
            out_halves(q_s, qa, XQ, qbd, 0, True, 2)
            out_halves(k_s, ka, KP, kT, 0, False, 1)
            v_out(0)

            def body(t, u, i, first, last):
                if not last:
                    high_xT(t + 1)
                act.wait_ge(sub_s, t + 1)
                act.activation(z[:, :, :], z[:, :, :], ACT.Exp, scale=DK ** -0.5).then_inc(exp_s, 1)
                if not last:
                    out_halves(q_s, qa, XQ, qbd, t + 1, True, 2)
                    out_halves(k_s, ka, KP, kT, t + 1, False, 1)
                out_halves(pT_s, pa, YT, pbd, t, True, 1)
                high_oT(t)
                if not last:
                    v_out(t + 1)

            run_pairs(act, T, body)

        @block.tensor
        def _(pe):
            def x_turn(t, u):
                pe.wait_ge(xn_s, t + 1)
                pe.transpose(XQ[:, 0, :], xn[:, u, :], w["ident"][:, :]).then_inc(xT_s, 1)

            def project(n, parts, done, out):
                for j in range(HP):
                    cols = slice(j * P, (j + 1) * P)
                    pe.matmul(out[:, j, :], w["brows"][:, n * H * DK + j * P:n * H * DK + (j + 1) * P], w["ones"][:, :], start=True, stop=False)
                    pe.matmul(out[:, j, :], split[:, n, 0, cols], parts[0], start=False, stop=False)
                    pe.matmul(out[:, j, :], split[:, n, 0, cols], parts[1], start=False, stop=False)
                    mm = pe.matmul(out[:, j, :], split[:, n, 1, cols], parts[0], start=False, stop=True)
                mm.then_inc(done, 1)

            def q_proj(t):
                pe.wait_ge(xl_s, t + 1)
                project(0, (xT[:, 0, :], xT[:, 1, :]), q_s, XQ)

            def k_proj(t, u):
                pe.wait_ge(c_s, t + 1)
                if not (isinstance(t, int) and t < 1):
                    pe.wait_ge(sub_s, t)
                project(1, (cT[:, u, 0, :], cT[:, u, 1, :]), k_s, KP)

            def v_proj(t, u):
                pe.wait_ge(qa, t + 1)
                for half in range(2):
                    out = flat[:, (4 + half) * BANK:(5 + half) * BANK]
                    cols = slice(half * BANK, (half + 1) * BANK)
                    pe.matmul(out, cT[:, u, 0, :], split[:, 2, 0, cols], start=True, stop=False)
                    pe.matmul(out, cT[:, u, 0, :], split[:, 2, 1, cols], start=False, stop=False)
                    mm = pe.matmul(out, cT[:, u, 1, :], split[:, 2, 0, cols], start=False, stop=True)
                mm.then_inc(v_s, 1)

            def out_proj(t):
                pe.wait_ge(ol_s, t + 1)
                for j in range(HP):
                    cols = slice(j * P, (j + 1) * P)
                    pe.matmul(AO, oT[:, 0, j, :], split[:, 3, 0, cols], start=(j == 0), stop=False)
                    pe.matmul(AO, oT[:, 0, j, :], split[:, 3, 1, cols], start=False, stop=False)
                    mm = pe.matmul(AO, oT[:, 1, j, :], split[:, 3, 0, cols], start=False, stop=(j == HP - 1))
                mm.then_inc(y_s, 1)

            x_turn(0, 0)
            q_proj(0)
            k_proj(0, 0)
            v_proj(0, 0)

            def body(t, u, i, first, last):
                pe.wait_ge(qa, t + 1)
                pe.wait_ge(ka, t + 1)
                pe.wait_ge(kd, t + 1)
                for h in range(H):
                    mm = pe.matmul(SC[:, h, :], qbd[:, h, :], kT[:, h, :], start=True, stop=True)
                mm.then_inc(sc_s, 1)
                if not first:
                    out_proj(t - 1)
                if not last:
                    pe.wait_ge(va, t + 1)
                    x_turn(t + 1, 1 - u)
                pe.wait_ge(f_ld[u], 16 * (i + 1))
                for q in range(NB):
                    out = GA[:, q * 16 * H:(q + 1) * 16 * H]
                    pe.matmul(out, w["ones"][:, :], w["brows"][:, 2 * H * DK:], start=True, stop=False)
                    mm = pe.matmul(out, fts[:, u, q * P:(q + 1) * P], w["kron"][:, :], start=False, stop=True)
                mm.then_inc(g_s, 1)
                if not last:
                    q_proj(t + 1)
                    k_proj(t + 1, 1 - u)
                pe.wait_ge(p_s, t + 1)
                if not first:
                    pe.wait_ge(x2_s, t)
                zf = z[:, :, :].rearrange("p h k -> p (h k)")
                for j in range(HP):
                    mm = pe.transpose(YT[:, j, :], zf[:, j * P:(j + 1) * P], w["ident"][:, :])
                mm.then_inc(pT_s, 1)
                if not last:
                    v_proj(t + 1, 1 - u)
                pe.wait_ge(pa, t + 1)
                pe.wait_ge(pd, t + 1)
                pe.wait_ge(va, t + 1)
                for h in range(H):
                    half = slice(h % 2 * DK, (h % 2 + 1) * DK)
                    mm = pe.matmul(YT[half, h // 2, :], v[:, h, :], pbd[:, h, :], start=True, stop=True)
                mm.then_inc(o_s, 1)

            run_pairs(pe, T, body)
            out_proj(T - 1)


def norm_block(nc, ctx, w, d, x2d, T):
    C = T // Q

    def sem(n):
        return ctx.enter_context(nc.semaphore(n))

    ld = [sem("n_x2_loaded0"), sem("n_x2_loaded1")]
    cst, stats, agg_s, var_s, rstd_s, xn_s = (sem(n) for n in (
        "n_constants", "n_stats", "n_means", "n_variance", "n_rstd", "n_normed"))
    xT_s, xe_s, xh_s, xl_s, pr_s, num_s, row_s = (sem(n) for n in (
        "n_turned", "n_turned_out", "n_high", "n_low", "n_scored", "n_logits_out", "n_rows_kept"))
    held_dve, held_pool = sem("n_held_dve"), sem("n_held_pool")
    rows, x2, xnT = w["rows"], w["x2"], w["xnT"]
    with ExitStack() as c_:
        def sb(n, s, dt=F32):
            return c_.enter_context(nc.sbuf_tensor(n, s, dt))

        st6, mv = sb("n_bn", [P, 2, Q, 6]), sb("n_mv", [P, 2, Q, 2])
        var, rs, xT = sb("n_var", [P, 2, Q]), sb("n_rs", [P, 2, Q]), sb("n_xT", [P, 2, Q * P])
        xn = sb("n_xn", [P, 2, Q, P])
        gw = sb("gate_weights", [P, E])
        ps = c_.enter_context(nc.psum_tensor("n_psum", [P, 2, Q * P], F32))
        pr = c_.enter_context(nc.psum_tensor("n_scores_psum", [P, T * E], F32))
        block = c_.enter_context(nc.Block())

        @block.sync
        def _(sp):
            sp.dma_start(gw[:, :], d["gate_w"]).then_inc(cst, 16)

            def body(c, u, i, first, last):
                if not (isinstance(c, int) and c < 2):
                    sp.wait_ge(ld[u], 16 * i)
                sp.dma_start(x2[:, at(c, Q), :],
                             x2d[at(c, Q * P), :].rearrange("(q p) n -> p q n", p=P)).then_inc(ld[u], 16)

            run_pairs(sp, C, body)

        @block.vector
        def _(dve):
            def statistics(c, u, i):
                dve.wait_ge(ld[u], 16 * (i + 1))
                if not (isinstance(c, int) and c < 2):
                    dve.wait_ge(xn_s, c - 1)
                for q in range(Q):
                    ins = dve.bn_stats(st6[:, u, q, :], tile_of(x2, c, q))
                ins.then_inc(stats, 1)
                dve.wait_ge(stats, c + 1)
                hold(dve, held_dve)
                for q in range(Q):
                    ins = dve.bn_aggr(mv[:, u, q, :], st6[:, u, q, :])
                ins.then_inc(agg_s, 1)

            def low(c, u):
                dve.wait_ge(xh_s, c + 1)
                cols = at(c, Q * P)
                dve.tensor_tensor(xnT[:, 1, cols], ps[:, u, :], xnT[:, 0, cols], ALU.subtract).then_inc(xl_s, 1)

            statistics(0, 0, 0)

            def body(c, u, i, first, last):
                if not last:
                    statistics(c + 1, 1 - u, i + u)
                dve.wait_ge(rstd_s, c + 1)
                if not (isinstance(c, int) and c < 2):
                    dve.wait_ge(xT_s, c - 1)
                    dve.wait_ge(row_s, c - 1)
                for q in range(Q):
                    ins = dve.tensor_scalar(xn[:, u, q, :], tile_of(x2, c, q), mv[:, u, q, 0:1], rs[:, u, q:q + 1],
                                            ALU.subtract, ALU.mult)
                ins.then_inc(xn_s, 1)
                if not first:
                    low(c - 1, 1 - u)

            run_pairs(dve, C, body)
            low(C - 1, 1)
            dve.wait_ge(pr_s, C)
            dve.tensor_copy(w["logits"].rearrange("p t e -> p (t e)"), pr[:, :]).then_inc(num_s, 1)
            dve.wait_ge(num_s, 1)

        @block.gpsimd
        def _(pool):
            def body(c, u, i, first, last):
                pool.wait_ge(agg_s, c + 1)
                if not (isinstance(c, int) and c < 2):
                    pool.wait_ge(xn_s, c - 1)
                hold(pool, held_pool)
                pool.tensor_scalar(var[:, u, :], mv[:, u, :, 1], LN_EPS, None, ALU.add).then_inc(var_s, 1)
                pool.wait_ge(var_s, c + 1)
                pool.tensor_tensor(rs[:, u, :], var[:, u, :], w["minus_half"][:, 0:1].to_broadcast([P, Q]),
                                   ALU.pow).then_inc(rstd_s, 1)
                if not first:
                    keep_rows(c - 1, 1 - u)

            def keep_rows(c, u):
                pool.wait_ge(xn_s, c + 1)
                hold(pool, held_pool)
                pool.tensor_copy(rows[:, at(c, Q), :], xn[:, u, :, :]).then_inc(row_s, 1)

            run_pairs(pool, C, body)
            keep_rows(C - 1, 1)
            pool.wait_ge(row_s, C)

        @block.scalar
        def _(act):
            def body(c, u, i, first, last):
                act.wait_ge(xT_s, c + 1)
                if not (isinstance(c, int) and c < 2):
                    act.wait_ge(pr_s, c - 1)
                act.activation(xT[:, u, :], ps[:, u, :], ACT.Copy).then_inc(xe_s, 1)
                act.activation(xnT[:, 0, at(c, Q * P)], ps[:, u, :], ACT.Copy).then_inc(xh_s, 1)

            run_pairs(act, C, body)

        @block.tensor
        def _(pe):
            def turn(c, u):
                pe.wait_ge(xn_s, c + 1)
                if not (isinstance(c, int) and c < 2):
                    pe.wait_ge(xl_s, c - 1)
                    pe.wait_ge(xe_s, c - 1)
                for q in range(Q):
                    mm = pe.transpose(ps[:, u, q * P:(q + 1) * P], xn[:, u, q, :], w["ident"][:, :])
                mm.then_inc(xT_s, 1)

            pe.wait_ge(cst, 16)
            turn(0, 0)

            def body(c, u, i, first, last):
                if not last:
                    turn(c + 1, 1 - u)
                pe.wait_ge(xe_s, c + 1)
                for q in range(Q):
                    cols = slice((c * Q + q) * E, (c * Q + q + 1) * E) if isinstance(c, int) else bass.ds(c * (Q * E) + q * E, E)
                    mm = pe.matmul(pr[:, cols], xT[:, u, q * P:(q + 1) * P], gw[:, :], start=True, stop=True)
                mm.then_inc(pr_s, 1)

            run_pairs(pe, C, body)


def dispatch_block(nc, ctx, w, d, gates, counts, T):
    CAP = (T + U) * P

    def sem(n):
        return ctx.enter_context(nc.semaphore(n))

    cst, step_s, sig_s, mask_s, rank_s, zero_s = (sem(n) for n in (
        "d_constants", "d_steps", "d_sigmoid", "d_mask", "d_ranked", "d_zeros"))
    with ExitStack() as c:
        def sb(n, s, dt=F32):
            return c.enter_context(nc.sbuf_tensor(n, s, dt))

        gb, below = sb("gate_bias", [P, E]), sb("expert_number_less_8", [P, E])
        z, score, rest = sb("d_z", [P, T, E]), sb("d_score", [P, T, E]), sb("d_rest", [P, T, E])
        best, number = sb("d_best", [P, 2, T]), sb("d_number", [P, 2, T])
        same, hot = sb("d_same", [P, T, E]), sb("d_hot", [P, 2, T, E])
        total, mask = sb("d_total", [P, T]), sb("d_mask_sb", [P, T, E], BF16)
        zeros, through, pos, dest = sb("d_zero_row", [P, T]), sb("d_through", [P, T, E]), sb("d_pos", [P, T, E]), sb("d_dest", [P, 2, T])
        before = sb("d_tokens_before", [P, P], BF16)
        pq = c.enter_context(nc.psum_tensor("d_rank_psum", [P, 2, T * E], F32))
        block = c.enter_context(nc.Block())

        @block.sync
        def _(sp):
            sp.dma_start(gb[:, :], d["gate_b"].partition_broadcast(P)).then_inc(cst, 16)
            sp.dma_start(below[:, :], d["numbers"].partition_broadcast(P)).then_inc(cst, 16)

        @block.gpsimd
        def _(pool):
            pool.memset(before[:, :], 1.0).then_inc(zero_s, 1)
            pool.wait_ge(zero_s, 1)
            pool.affine_select(out=before[:, :], in_=before[:, :], compare_op=ALU.is_gt, fill=0.0,
                               base=0, pattern=[[1, P]], channel_multiplier=-1).then_inc(zero_s, 1)
            pool.memset(zeros[:, :], 0.0).then_inc(zero_s, 1)

        @block.scalar
        def _(act):
            act.wait_ge(step_s, 1)
            act.activation(score[:, :, :], z[:, :, :], ACT.Sigmoid).then_inc(sig_s, 1)

        @block.vector
        def _(dve):
            n = 0

            def step(ins):
                nonlocal n
                ins.then_inc(step_s, 1)
                n += 1
                dve.wait_ge(step_s, n)

            def each(x):
                return x.unsqueeze(2).to_broadcast([P, T, E])

            def every(x):
                return x.unsqueeze(1).to_broadcast([P, T, E])

            dve.wait_ge(cst, 32)
            step(dve.tensor_tensor(z[:, :, :], w["logits"][:, :, :], every(gb[:, :]), ALU.add))
            dve.wait_ge(sig_s, 1)
            for k, left in enumerate((score, rest)):
                step(dve.tensor_reduce(best[:, k, :], left[:, :, :], X, ALU.max))
                step(dve.tensor_tensor(same[:, :, :], left[:, :, :], each(best[:, k, :]), ALU.is_equal))
                step(dve.tensor_tensor(same[:, :, :], same[:, :, :], every(below[:, :]), ALU.mult))
                step(dve.tensor_reduce(number[:, k, :], same[:, :, :], X, ALU.min))
                step(dve.tensor_tensor(hot[:, k, :, :], every(below[:, :]), each(number[:, k, :]), ALU.is_equal))
                if k == 0:
                    step(dve.scalar_tensor_tensor(rest[:, :, :], hot[:, 0, :, :], -4.0, score[:, :, :], ALU.mult, ALU.add))
            dve.tensor_tensor(mask[:, :, :], hot[:, 0, :, :], hot[:, 1, :, :], ALU.add).then_inc(mask_s, 1)
            step(dve.tensor_tensor(total[:, :], best[:, 0, :], best[:, 1, :], ALU.add))
            step(dve.tensor_scalar(total[:, :], total[:, :], 1e-6, None, ALU.add))
            step(dve.reciprocal(total[:, :], total[:, :]))
            for k in range(2):
                step(dve.tensor_tensor(gates[:, :, k], best[:, k, :], total[:, :], ALU.mult))
            dve.wait_ge(zero_s, 3)
            dve.wait_ge(rank_s, 1)
            ranks, sums = (pq[:, k, :].rearrange("p (t e) -> p t e", e=E) for k in range(2))
            for e in range(E):
                step(dve.tensor_tensor_scan(through[:, :, e], sums[:, :, e], zeros[:, :], float(e * CAP), ALU.add, ALU.add))
            step(dve.tensor_copy(counts[:, :], through[:, T - 1, :]))
            step(dve.tensor_tensor(through[:, :, :], through[:, :, :], sums, ALU.subtract))
            step(dve.tensor_tensor(pos[:, :, :], through[:, :, :], ranks, ALU.add))
            for k in range(2):
                step(dve.tensor_tensor(same[:, :, :], hot[:, k, :, :], pos[:, :, :], ALU.mult))
                step(dve.tensor_reduce(dest[:, k, :], same[:, :, :], X, ALU.add))
                step(dve.tensor_copy(w["dest"][:, k, :], dest[:, k, :]))

        @block.tensor
        def _(pe):
            pe.wait_ge(zero_s, 2)
            pe.wait_ge(mask_s, 1)
            flat = mask[:, :, :].rearrange("p t e -> p (t e)")
            pe.matmul(pq[:, 0, :], before[:, :], flat, start=True, stop=True)
            pe.matmul(pq[:, 1, :], w["ones"][:, :], flat, start=True, stop=True).then_inc(rank_s, 1)


def expert_weights_block(nc, ctx, w, d):
    def sem(n):
        return ctx.enter_context(nc.semaphore(n))

    ld, hi, lo = [sem("w_loaded0"), sem("w_loaded1")], sem("w_high"), sem("w_low")
    bias = sem("w_bias")
    NE = E + 1
    with ExitStack() as c:
        raw = c.enter_context(nc.sbuf_tensor("w_raw", [P, 2, 2 * FB * P], F32))
        block = c.enter_context(nc.Block())

        @block.sync
        def _(sp):
            sp.dma_start(w["up_bias"][:, :, :], d["up_b"]).then_inc(bias, 16)
            sp.dma_start(w["down_bias"][:, :, :], d["down_b"].partition_broadcast(P)).then_inc(bias, 16)
            for e in range(NE):
                if e >= 2:
                    sp.wait_ge(lo, e - 1)
                sp.dma_start(raw[:, e % 2, 0:FB * P], d["up"][e]).then_inc(ld[e % 2], 16)
                sp.dma_start(raw[:, e % 2, FB * P:].rearrange("p (j n) -> p j n", n=P),
                             d["down"][e].rearrange("(j p) n -> p j n", p=P)).then_inc(ld[e % 2], 16)
            sp.wait_ge(bias, 32)

        @block.scalar
        def _(act):
            for e in range(NE):
                act.wait_ge(ld[e % 2], 32 * (e // 2 + 1))
                act.activation(w["experts"][:, 0, e, :], raw[:, e % 2, :], ACT.Copy).then_inc(hi, 1)

        @block.vector
        def _(dve):
            for e in range(NE):
                dve.wait_ge(hi, e + 1)
                dve.tensor_tensor(w["experts"][:, 1, e, :], raw[:, e % 2, :], w["experts"][:, 0, e, :],
                                  ALU.subtract).then_inc(lo, 1)


def routed_block(nc, ctx, w, d, slots, counts, results, T):
    N = 2 * T // U + E
    WAYS = 8
    CAP = (T + U) * P
    def sem(n):
        return ctx.enter_context(nc.semaphore(n))

    ld, y_st = [sem(f"e_rows_loaded{q}") for q in range(WAYS)], [sem(f"e_results_stored{q}") for q in range(WAYS)]
    pad_s, padded, step_s, cst = sem("e_pads_made"), sem("e_pads_stored"), sem("e_table_steps"), sem("e_constants")
    xT_s, xh_s, xl_s, up_s, gl_s, hh_s, hl_s, dn_s, y_s = (sem(n) for n in (
        "e_turned", "e_high", "e_low", "e_up", "e_gelu", "e_hidden_high", "e_hidden_low", "e_down", "e_result"))
    id_s, held_pool = sem("e_numbers_copied"), sem("e_held_pool")
    with ExitStack() as c:
        def sb(n, s, dt=F32):
            return c.enter_context(nc.sbuf_tensor(n, s, dt))

        xr, xT = sb("e_rows", [P, WAYS, U, ROW]), sb("e_T", [P, 2, 2, U * P], BF16)
        hid, hidp = sb("e_hidden", [P, 2, FB, U * P]), sb("e_hidden_parts", [P, 4, 2, FB, U * P], BF16)
        y, idn = sb("e_y", [P, WAYS, U, P]), sb("e_numbers", [P, WAYS, U], I32)
        pad = sb("e_pad", [P, U, ROW])
        row_of, used, ti = sb("e_row_of", [1, E]), sb("e_used", [1, E]), sb("e_int", [1, E], I32)
        rows_i, cum = sb("e_first_free", [1, E], I32), sb("e_tiles_through", [1, E])
        num, zero8 = sb("e_tile_numbers", [1, N]), sb("e_zero", [1, E])
        past, exp_f, start_f = sb("e_past", [1, N, E]), sb("e_expert", [1, N]), sb("e_start", [1, N])
        tmp, real = sb("e_tmp", [1, N, E]), sb("e_real", [1, N])
        exp_i, start_i = sb("e_expert_int", [1, N], I32), sb("e_start_int", [1, N], I32)
        ps = c.enter_context(nc.psum_tensor("e_psum", [P, 2, BANK], F32))
        ph = c.enter_context(nc.psum_tensor("e_up_psum", [P, 2, FB, U * P], F32))
        pd = c.enter_context(nc.psum_tensor("e_down_psum", [P, 2, BANK], F32))
        block = c.enter_context(nc.Block())
        STEPS = 18

        def per_unit(x, t):
            return x[:, t:t + 1] if isinstance(t, int) else x[:, bass.ds(t, 1)]

        def unit_rows(rows):
            return slots[rows, :].rearrange("(p k) n -> p k n", k=U)

        @block.sync
        def _(sp):
            sp.dma_start(num[:, :], d["unit_numbers"].unsqueeze(0)).then_inc(cst, 16)
            sp.dma_start(zero8[:, :], d["bases"].unsqueeze(0)).then_inc(cst, 16)
            sp.wait_ge(pad_s, 2)
            sp.wait_ge(step_s, STEPS)
            for e in range(E):
                r = sp.value_load(rows_i[0:1, e:e + 1], min_val=e * CAP, max_val=e * CAP + T * P)
                sp.dma_start(unit_rows(bass.ds(r, U * P)), pad[:, :, :]).then_inc(padded, 16)
            sp.dma_start(unit_rows(slice(E * CAP, E * CAP + U * P)), pad[:, :, :]).then_inc(padded, 16)
            sp.wait_ge(padded, 16 * (E + 1))

            def load(t, q):
                r = sp.value_load(per_unit(start_i, t), min_val=0, max_val=E * CAP)
                sp.dma_start(xr[:, q, :, :], unit_rows(bass.ds(r, U * P))).then_inc(ld[q], 16)

            for t in range(WAYS):
                load(t, t)

            def body(t, q, i, first, last):
                if not (isinstance(t, int) and t + WAYS >= N):
                    sp.wait_ge(xT_s, t + 1)
                    sp.wait_ge(id_s, t + 1)
                    load(t + WAYS, q)

            run_tiles(sp, N, WAYS, body)

        @block.vector
        def _(dve):
            n = 0

            def step(ins):
                nonlocal n
                ins.then_inc(step_s, 1)
                n += 1
                dve.wait_ge(step_s, n)

            dve.memset(pad[:, :, :], 0.0).then_inc(pad_s, 1)
            dve.wait_ge(pad_s, 1)
            dve.memset(pad[:, :, P:P + 1].bitcast(I32), NOWHERE).then_inc(pad_s, 1)
            dve.wait_ge(cst, 32)
            own = counts[0:1, :]
            step(dve.tensor_copy(rows_i[:, :], own))
            step(dve.tensor_tensor(used[:, :], own, zero8[:, :], ALU.subtract))
            step(dve.tensor_scalar(used[:, :], used[:, :], float(U * P - 1), None, ALU.add))
            step(dve.tensor_copy(ti[:, :], used[:, :]))
            step(dve.tensor_scalar(ti[:, :], ti[:, :], 8, None, ALU.arith_shift_right))
            step(dve.tensor_copy(used[:, :], ti[:, :]))
            step(dve.tensor_scalar(row_of[:, :], used[:, :], 0.0, None, ALU.mult))
            step(dve.tensor_tensor_scan(cum[:, :], used[:, :], row_of[:, :], 0.0, ALU.add, ALU.add))
            step(dve.tensor_tensor(past[:, :, :], num[:, :].unsqueeze(2).to_broadcast([1, N, E]),
                                   cum[:, :].unsqueeze(1).to_broadcast([1, N, E]), ALU.is_ge))
            step(dve.tensor_reduce(exp_f[:, :], past[:, :, :], X, ALU.add))
            step(dve.tensor_tensor(tmp[:, :, :], past[:, :, :], used[:, :].unsqueeze(1).to_broadcast([1, N, E]), ALU.mult))
            step(dve.tensor_reduce(start_f[:, :], tmp[:, :, :], X, ALU.add))
            step(dve.tensor_tensor(start_f[:, :], num[:, :], start_f[:, :], ALU.subtract))
            step(dve.tensor_scalar(real[:, :], exp_f[:, :], float(E), float(U * P), ALU.is_lt, ALU.mult))
            step(dve.tensor_tensor(start_f[:, :], start_f[:, :], real[:, :], ALU.mult))
            step(dve.scalar_tensor_tensor(start_f[:, :], exp_f[:, :], float(CAP), start_f[:, :], ALU.mult, ALU.add))
            step(dve.tensor_copy(exp_i[:, :], exp_f[:, :]))
            step(dve.tensor_copy(start_i[:, :], start_f[:, :]))

            def x_parts(t, q, i):
                u = q % 2
                dve.wait_ge(ld[q], 16 * (i + 1))
                if not (isinstance(t, int) and t < WAYS):
                    dve.wait_ge(y_st[q], 16 * U * i)
                dve.tensor_copy(idn[:, q, :], xr[:, q, :, P].bitcast(I32)).then_inc(id_s, 1)
                dve.wait_ge(xh_s, t + 1)
                dve.tensor_tensor(xT[:, u, 1, :], ps[:, u, 0:U * P], xT[:, u, 0, :], ALU.subtract).then_inc(xl_s, 1)

            def result(t, q, i):
                e = dve.value_load(per_unit(exp_i, t), min_val=0, max_val=E)
                dve.wait_ge(dn_s, t + 1)
                dve.tensor_tensor(y[:, q, :, :], pd[:, q % 2, 0:U * P].rearrange("p (k n) -> p k n", n=P),
                                  w["down_bias"][:, bass.ds(e, 1), :].to_broadcast([P, U, P]),
                                  ALU.add).then_inc(y_s, 1)

            x_parts(0, 0, 0)

            def body(t, q, i, first, last):
                u = q % 2
                if not last:
                    x_parts(t + 1, (q + 1) % WAYS, i + (q == WAYS - 1))
                dve.wait_ge(gl_s, t + 1)
                if not (isinstance(t, int) and t < 4):
                    dve.wait_ge(dn_s, t - 3)
                dve.tensor_copy(hidp[:, q % 4, 0, :, :], hid[:, u, :, :]).then_inc(hh_s, 1)
                dve.wait_ge(hh_s, t + 1)
                dve.tensor_tensor(hidp[:, q % 4, 1, :, :], hid[:, u, :, :], hidp[:, q % 4, 0, :, :], ALU.subtract).then_inc(hl_s, 1)
                if not (isinstance(t, int) and t < 2):
                    result(t - 2, (q - 2) % WAYS, i - (q < 2))

            run_tiles(dve, N, WAYS, body)
            result(N - 2, WAYS - 2, N // WAYS - 1)
            result(N - 1, WAYS - 1, N // WAYS - 1)

        @block.gpsimd
        def _(pool):
            def body(t, q, i, first, last):
                pool.wait_ge(y_s, t + 1)
                hold(pool, held_pool)
                for k in range(U):
                    pool.indirect_dma_start(results, bass.IndirectOffsetOnAxis(idn[:, q, k:k + 1], 0), y[:, q, k, :], None,
                                            bounds_check=2 * T * P - 1, oob_is_err=False).then_inc(y_st[q], 16)

            run_tiles(pool, N, WAYS, body)
            for q in range(WAYS):
                pool.wait_ge(y_st[q], 16 * U * (N // WAYS))

        @block.scalar
        def _(act):
            act.wait_ge(step_s, STEPS)

            def high_x(t, u):
                act.wait_ge(xT_s, t + 1)
                if not (isinstance(t, int) and t < 2):
                    act.wait_ge(up_s, t - 1)
                act.activation(xT[:, u, 0, :], ps[:, u, 0:U * P], ACT.Copy).then_inc(xh_s, 1)

            high_x(0, 0)

            def body(t, q, i, first, last):
                u = q % 2
                if not last:
                    high_x(t + 1, 1 - u)
                e = act.value_load(per_unit(exp_i, t), min_val=0, max_val=E)
                act.wait_ge(up_s, t + 1)
                if not (isinstance(t, int) and t < 2):
                    act.wait_ge(hl_s, t - 1)
                for j in range(FB):
                    ins = act.activation(hid[:, u, j, :], ph[:, u, j, :], ACT.Gelu,
                                         bias=w["up_bias"][:, bass.ds(e, 1), j:j + 1].rearrange("p e j -> p (e j)"))
                ins.then_inc(gl_s, 1)

            run_tiles(act, N, WAYS, body)

        @block.tensor
        def _(pe):
            pe.wait_ge(step_s, STEPS)

            def turn(t, q, i):
                u = q % 2
                pe.wait_ge(ld[q], 16 * (i + 1))
                if not (isinstance(t, int) and t < 2):
                    pe.wait_ge(xl_s, t - 1)
                for k in range(U):
                    mm = pe.transpose(ps[:, u, k * P:(k + 1) * P], xr[:, q, k, 0:P], w["ident"][:, :])
                mm.then_inc(xT_s, 1)

            def expert(t):
                return pe.value_load(per_unit(exp_i, t), min_val=0, max_val=E)

            def part(k, e, n, size):
                return w["experts"][:, k, bass.ds(e, 1), n:n + size].rearrange("p e n -> p (e n)")

            def up_proj(t, u, e):
                pe.wait_ge(xl_s, t + 1)
                if not (isinstance(t, int) and t < 2):
                    pe.wait_ge(gl_s, t - 1)
                for j in range(FB):
                    pe.matmul(ph[:, u, j, :], part(0, e, j * P, P), xT[:, u, 0, :], start=True, stop=False)
                    pe.matmul(ph[:, u, j, :], part(0, e, j * P, P), xT[:, u, 1, :], start=False, stop=False)
                    mm = pe.matmul(ph[:, u, j, :], part(1, e, j * P, P), xT[:, u, 0, :], start=False, stop=True)
                mm.then_inc(up_s, 1)

            def down_proj(t, q, e):
                u = q % 2
                pe.wait_ge(hl_s, t + 1)
                if not (isinstance(t, int) and t < 2):
                    pe.wait_ge(y_s, t - 1)
                for k in range(U):
                    toks, own = slice(k * P, (k + 1) * P), pd[:, u, k * P:(k + 1) * P]
                    for j in range(FB):
                        hi, lo = (part(n, e, (FB + j) * P, P) for n in range(2))
                        pe.matmul(own, hidp[:, q % 4, 0, j, toks], hi, start=(j == 0), stop=False)
                        pe.matmul(own, hidp[:, q % 4, 0, j, toks], lo, start=False, stop=False)
                        mm = pe.matmul(own, hidp[:, q % 4, 1, j, toks], hi, start=False, stop=(j == FB - 1))
                mm.then_inc(dn_s, 1)

            turn(0, 0, 0)

            def body(t, q, i, first, last):
                u = q % 2
                if not last:
                    turn(t + 1, (q + 1) % WAYS, i + (q == WAYS - 1))
                up_proj(t, u, expert(t))
                if not (isinstance(t, int) and t < 2):
                    down_proj(t - 2, (q - 2) % WAYS, expert(t - 2))

            run_tiles(pe, N, WAYS, body)
            down_proj(N - 2, WAYS - 2, expert(N - 2))
            down_proj(N - 1, WAYS - 1, expert(N - 1))


def shared_block(nc, ctx, w, d, slots, T):
    C = T // Q

    def sem(n):
        return ctx.enter_context(nc.semaphore(n))

    sent = [sem("s_rows_sent0"), sem("s_rows_sent1")]
    up_s, gl_s, hh_s, hl_s, dn_s, out_s, num_s, row_s = (sem(n) for n in (
        "s_up", "s_gelu", "s_hidden_high", "s_hidden_low", "s_down", "s_out", "s_numbered", "s_rows_copied"))
    ids_s = sem("s_numbers_loaded")
    held_pool = sem("s_held_pool")
    rows, xnT = w["rows"], w["xnT"]
    with ExitStack() as c_:
        def sb(n, s, dt=F32):
            return c_.enter_context(nc.sbuf_tensor(n, s, dt))

        hid, hidp = sb("s_hidden", [P, FB, Q * P]), sb("s_hidden_parts", [P, 2, 2, FB, Q * P], BF16)
        ids, index = sb("s_numbers", [P, T, 2]), sb("s_index", [P, 2, 2, Q], I32)
        row = sb("s_rows", [P, 2, Q, 2, ROW])
        ph = c_.enter_context(nc.psum_tensor("s_up_psum", [P, FB, Q * P], F32))
        pd = c_.enter_context(nc.psum_tensor("s_down_psum", [P, 2, Q * P], F32))
        block = c_.enter_context(nc.Block())

        @block.sync
        def _(sp):
            sp.dma_start(ids[:, :, :], d["ids"]).then_inc(ids_s, 16)

        @block.gpsimd
        def _(pool):
            def body(c, u, i, first, last):
                pool.wait_ge(num_s, 2 * (c + 1))
                pool.wait_ge(row_s, c + 1)
                hold(pool, held_pool)
                for q in range(Q):
                    for k in range(2):
                        pool.indirect_dma_start(slots, bass.IndirectOffsetOnAxis(index[:, u, k, q:q + 1], 0),
                                                row[:, u, q, k, :], None).then_inc(sent[u], 16)

            run_pairs(pool, C, body)
            for u in range(2):
                pool.wait_ge(sent[u], 16 * Q * C)

        @block.scalar
        def _(act):
            def body(c, u, i, first, last):
                if not (isinstance(c, int) and c < 2):
                    act.wait_ge(sent[u], 16 * 2 * Q * i)
                for k in range(2):
                    ins = act.activation(row[:, u, :, k, 0:P], rows[:, at(c, Q), :], ACT.Copy)
                ins.then_inc(row_s, 1)
                for j in range(FB):
                    act.wait_ge(up_s, c * FB + j + 1)
                    if not first:
                        act.wait_ge(hl_s, (c - 1) * FB + j + 1)
                    act.activation(hid[:, j, :], ph[:, j, :], ACT.Gelu, bias=w["up_bias"][:, E, j:j + 1]).then_inc(gl_s, 1)

            run_pairs(act, C, body)

        @block.vector
        def _(dve):
            def result(c, u):
                dve.wait_ge(dn_s, c + 1)
                dve.tensor_tensor(w["shared"][:, at(c, Q), :], pd[:, u, :].rearrange("p (q n) -> p q n", n=P),
                                  w["down_bias"][:, E:E + 1, :].to_broadcast([P, Q, P]), ALU.add).then_inc(out_s, 1)

            dve.wait_ge(ids_s, 16)

            def body(c, u, i, first, last):
                if not (isinstance(c, int) and c < 2):
                    dve.wait_ge(sent[u], 16 * 2 * Q * i)
                dve.tensor_copy(index[:, u, :, :], w["dest"][:, :, at(c, Q)]).then_inc(num_s, 1)
                dve.tensor_copy(row[:, u, :, :, P].bitcast(I32), ids[:, at(c, Q), :]).then_inc(num_s, 1)
                for j in range(FB):
                    dve.wait_ge(gl_s, c * FB + j + 1)
                    if j == 0 and not (isinstance(c, int) and c < 2):
                        dve.wait_ge(dn_s, c - 1)
                    dve.tensor_copy(hidp[:, u, 0, j, :], hid[:, j, :]).then_inc(hh_s, 1)
                    dve.wait_ge(hh_s, c * FB + j + 1)
                    dve.tensor_tensor(hidp[:, u, 1, j, :], hid[:, j, :], hidp[:, u, 0, j, :], ALU.subtract).then_inc(hl_s, 1)
                if not first:
                    result(c - 1, 1 - u)

            run_pairs(dve, C, body)
            result(C - 1, 1)

        @block.tensor
        def _(pe):
            def down_proj(c, u):
                pe.wait_ge(hl_s, (c + 1) * FB)
                if not (isinstance(c, int) and c < 2):
                    pe.wait_ge(out_s, c - 1)
                for q in range(Q):
                    toks, own = slice(q * P, (q + 1) * P), pd[:, u, q * P:(q + 1) * P]
                    for j in range(FB):
                        cols = slice((FB + j) * P, (FB + j + 1) * P)
                        hi, lo = w["experts"][:, 0, E, cols], w["experts"][:, 1, E, cols]
                        pe.matmul(own, hidp[:, u, 0, j, toks], hi, start=(j == 0), stop=False)
                        pe.matmul(own, hidp[:, u, 0, j, toks], lo, start=False, stop=False)
                        mm = pe.matmul(own, hidp[:, u, 1, j, toks], hi, start=False, stop=(j == FB - 1))
                mm.then_inc(dn_s, 1)

            def body(c, u, i, first, last):
                toks = at(c, Q * P)
                for j in range(FB):
                    cols = slice(j * P, (j + 1) * P)
                    hi, lo = w["experts"][:, 0, E, cols], w["experts"][:, 1, E, cols]
                    if not first:
                        pe.wait_ge(gl_s, (c - 1) * FB + j + 1)
                    pe.matmul(ph[:, j, :], hi, xnT[:, 0, toks], start=True, stop=False)
                    pe.matmul(ph[:, j, :], hi, xnT[:, 1, toks], start=False, stop=False)
                    pe.matmul(ph[:, j, :], lo, xnT[:, 0, toks], start=False, stop=True).then_inc(up_s, 1)
                if not first:
                    down_proj(c - 1, 1 - u)

            run_pairs(pe, C, body)
            down_proj(C - 1, 1)


def combine_block(nc, ctx, w, d, results, gates, out, T):
    C = T // Q

    def sem(n):
        return ctx.enter_context(nc.semaphore(n))

    ld, st = ([sem(f"c_{n}{u}") for u in range(2)] for n in ("results_loaded", "out_stored"))
    a_s, b_s, top_s, fin = (sem(n) for n in ("c_first_added", "c_second_added", "c_top_steps", "c_final"))
    with ExitStack() as c_:
        def sb(n, s, dt=F32):
            return c_.enter_context(nc.sbuf_tensor(n, s, dt))

        res, acc = sb("c_results", [P, 2, Q, 2, P]), sb("c_acc", [P, 2, Q, P])
        top, o = sb("c_top", [P, 2, Q]), sb("c_out", [P, 2, Q, P])
        block = c_.enter_context(nc.Block())

        def tiles(x, c):
            return x[at(c, Q * P)]

        @block.sync
        def _(sp):
            def load(c, u):
                sp.dma_start(res[:, u, :, :, :], tiles(results.rearrange("(n k) d -> n k d", k=2), c)
                             .rearrange("(q p) k n -> p q k n", p=P)).then_inc(ld[u], 16)

            load(0, 0)
            load(1, 1)

            def body(c, u, i, first, last):
                if not (isinstance(c, int) and c + 2 >= C):
                    sp.wait_ge(b_s, c + 1)
                    load(c + 2, u)
                sp.wait_ge(fin, c + 1)
                sp.dma_start(tiles(out, c).rearrange("(q p) n -> p q n", p=P), o[:, u, :, :]).then_inc(st[u], 16)

            run_pairs(sp, C, body)
            for u in range(2):
                sp.wait_ge(st[u], 16 * (C // 2))

        @block.vector
        def _(dve):
            def finish(c, u, i):
                if not (isinstance(c, int) and c < 2):
                    dve.wait_ge(st[u], 16 * i)
                dve.wait_ge(top_s, 3 * (c + 1))
                for q in range(Q):
                    ins = dve.scalar_tensor_tensor(o[:, u, q, :], acc[:, u, q, :], top[:, u, q:q + 1], tile_of(w["x2"], c, q),
                                                   ALU.mult, ALU.add)
                ins.then_inc(fin, 1)

            def body(c, u, i, first, last):
                def gate(q, k):
                    if isinstance(c, int):
                        return gates[:, c * Q + q, k:k + 1]
                    return gates[:, bass.ds(c * Q + q, 1), k:k + 1].rearrange("p t k -> p (t k)")

                dve.wait_ge(ld[u], 16 * (i + 1))
                if not (isinstance(c, int) and c < 2):
                    dve.wait_ge(fin, c - 1)
                for q in range(Q):
                    ins = dve.scalar_tensor_tensor(acc[:, u, q, :], res[:, u, q, 0, :], gate(q, 0), tile_of(w["shared"], c, q), ALU.mult, ALU.add)
                ins.then_inc(a_s, 1)
                dve.wait_ge(a_s, c + 1)
                for q in range(Q):
                    ins = dve.scalar_tensor_tensor(acc[:, u, q, :], res[:, u, q, 1, :], gate(q, 1), acc[:, u, q, :], ALU.mult, ALU.add)
                ins.then_inc(b_s, 1)
                dve.wait_ge(b_s, c + 1)
                dve.tensor_reduce(top[:, u, :], acc[:, u, :, :], X, ALU.max, apply_absolute_value=True).then_inc(top_s, 1)
                if not first:
                    finish(c - 1, 1 - u, i - 1 + u)
                dve.wait_ge(top_s, 3 * c + 1)
                dve.tensor_scalar(top[:, u, :], top[:, u, :], 1e-5, None, ALU.add).then_inc(top_s, 1)
                dve.wait_ge(top_s, 3 * c + 2)
                dve.reciprocal(top[:, u, :], top[:, u, :]).then_inc(top_s, 1)

            run_pairs(dve, C, body)
            finish(C - 1, 1, C // 2 - 1)


def build(nc, a, out, T):
    with ExitStack() as ctx:
        def keep(n, s, dt=F32, stack=ctx):
            return stack.enter_context(nc.sbuf_tensor(n, s, dt))

        def scratch(n, s, dt=F32):
            return nc.dram_tensor(n, s, dt).ap()

        ft, mtab = scratch("features_dram", [T, P, BANK]), scratch("key_table_dram", [2 * T, S * NB])
        x2d = scratch("x2_dram", [T * P, P])
        slots = scratch("slots_dram", [(E * (T + U) + U) * P, ROW])
        results = scratch("results_dram", [2 * T * P, P])
        w = {
            "ident": keep("identity_sb", [P, P]), "ones": keep("ones", [P, P], BF16),
            "minus_half": keep("minus_half", [P, 1]), "quarter": keep("quarter_turn", [P, 1]),
        }
        gates, counts = keep("gates", [P, T, 2]), keep("rows_through", [P, E])
        with ExitStack() as attention:
            def keep_for_attention(n, s, dt=F32):
                return keep(n, s, dt, attention)

            w["kron"] = keep_for_attention("gate_weights_spread", [P, 16 * H])
            w["split"] = keep_for_attention("projection_parts", [P, 4, 2, H * DK], BF16)
            w["brows"] = keep_for_attention("bias_parts", [P, 2 * H * DK + 16 * H], BF16)
            w["ybias"] = keep_for_attention("out_bias", [P, P])
            w["qbd"] = keep_for_attention("q_block_diagonal", [P, H, P])
            w["pbd"] = keep_for_attention("probs_block_diagonal", [P, H, P])
            w["v"] = keep_for_attention("values", [P, H, DK])
            setup_block(nc, ctx, w, a)
            relations_block(nc, ctx, w, a, ft, mtab, T)
            attention_block(nc, ctx, w, a, ft, x2d, T)
        w["experts"] = keep("expert_parts", [P, 2, E + 1, 2 * FB * P], BF16)
        w["up_bias"], w["down_bias"] = keep("up_biases", [P, E + 1, FB]), keep("down_biases", [P, E + 1, P])
        w["x2"], w["shared"] = keep("x2_sb", [P, T, P]), keep("shared_results", [P, T, P])
        with ExitStack() as dispatch:
            w["rows"] = keep("normed_rows", [P, T, P], F32, dispatch)
            w["xnT"] = keep("normed_turned", [P, 2, T * P], BF16, dispatch)
            w["logits"] = keep("expert_logits", [P, T, E], F32, dispatch)
            w["dest"] = keep("rows_to_fill", [P, 2, T], I32, dispatch)
            expert_weights_block(nc, ctx, w, a)
            norm_block(nc, ctx, w, a, x2d, T)
            dispatch_block(nc, ctx, w, a, gates, counts, T)
            shared_block(nc, ctx, w, a, slots, T)
        routed_block(nc, ctx, w, a, slots, counts, results, T)
        combine_block(nc, ctx, w, a, results, gates, out, T)


def kernel(**inputs):
    import numpy as np
    import concourse.bacc as bacc
    from concourse.bass_utils import run_bass_kernel_spmd as run

    g = {k.replace("L0_xattn_", "").replace("L0_ffn_", "f_"): np.asarray(v) for k, v in inputs.items()}
    tokens = g["x"].shape[0] * g["x"].shape[1]
    kron = np.zeros((16, NF, 16, H), np.float32)
    for m in range(16):
        kron[m, :, m, :] = g["Wg"].T
    bf = np.concatenate
    lay = {
        "x": g["x"].reshape(tokens, P), "ctxT": g["ctx_1024"].reshape(tokens, P).T,
        "boxes": g["fside_BxSx4_0"].reshape(tokens, NB),
        "wq": g["Wq"].T, "wk": g["Wk"].T, "wv": g["Wv"].T,
        "wo": g["Wo"].T.reshape(HP, P, P).transpose(1, 0, 2).reshape(P, H * DK),
        "bv": g["bv"].reshape(HP, P).T, "bo": g["bo"],
        "bias_rows": bf([g["bq"], g["bk"], np.tile(g["bg"], 16)]),
        "kron": kron.reshape(P, 16 * H), "ident": np.eye(P, dtype=np.float32),
        "gate_w": g["f_gate_w"], "gate_b": g["f_bias"], "numbers": np.arange(E, dtype=np.float32) - E,
        "bases": np.arange(E, dtype=np.float32) * (tokens + U * P),
        "ids": (2 * (np.arange(tokens // P)[None, :, None] * P + np.arange(P)[:, None, None]) + np.arange(2)).astype(np.float32),
        "unit_numbers": np.arange(2 * tokens // P // U + E, dtype=np.float32),
        "up": bf([g["f_up_w"], g["f_sw_up"][None]]), "down": bf([g["f_down_w"], g["f_sw_down"][None]]),
        "up_b": bf([g["f_up_b"], g["f_sb_up"][None]]).reshape(E + 1, FB, P).transpose(2, 0, 1),
        "down_b": bf([g["f_down_b"], g["f_sb_down"][None]]),
    }
    nc = bacc.Bacc("TRN2", target_bir_lowering=False, num_devices=1)
    arrays, a = {}, {}
    for n, v in lay.items():
        arrays["in_" + n] = np.ascontiguousarray(v)
        a[n] = nc.dram_tensor("in_" + n, v.shape, F32, kind="ExternalInput").ap()
    out = nc.dram_tensor("out", (tokens, P), F32, kind="ExternalOutput").ap()
    build(nc, a, out, tokens // P)
    r = run(nc, [arrays], core_ids=[0])
    return r.results[0]["out"].reshape(g["x"].shape)
```

```python
from contextlib import ExitStack
from math import pi

import concourse.bass as bass
from concourse import mybir

F32 = mybir.dt.float32
BF16 = mybir.dt.bfloat16
I32 = mybir.dt.int32
ALU = mybir.AluOpType
ACT = mybir.ActivationFunctionType
X = mybir.AxisListType.X

P = 128
S = 64
H = 16
DK = 64
HP = H // 2
NB = 4
Q = 4
U = 2
NF = 8
E = 8
FB = 4
LN_EPS = 1e-5
ROW = P + 1
NOWHERE = 1 << 30
BANK = 512
ROUND = 1.5 * 2.0 ** 23
NO_SIGN = 0x7FFFFFFF
TURNS = 100.0 / (2 * pi)
SIN_SCALE = 6.283185


def run_tiles(eng, tiles, ways, body):
    turns, ahead = tiles // ways, max(1, 4 // ways)
    if turns <= ahead + 1:
        for t in range(tiles):
            body(t, t % ways, t // ways, t == 0, t == tiles - 1)
        return
    for t in range(ahead * ways):
        body(t, t % ways, t // ways, t == 0, False)
    with eng.Fori(ahead, turns - 1) as i:
        for u in range(ways):
            body(i * ways + u, u, i, False, False)
    for t in range(tiles - ways, tiles):
        body(t, t % ways, t // ways, False, t == tiles - 1)


def run_pairs(eng, tiles, body):
    run_tiles(eng, tiles, 2, body)


def hold(eng, mark):
    eng.sem_inc(mark, 1)


def at(t, size):
    return slice(t * size, (t + 1) * size) if isinstance(t, int) else bass.ds(t * size, size)


def tile_of(x, c, q):
    if isinstance(c, int):
        return x[:, c * Q + q, :]
    return x[:, bass.ds(c * Q + q, 1), :].rearrange("p t n -> p (t n)")


def setup_block(nc, ctx, w, d, mtab, T):
    ld = ctx.enter_context(nc.semaphore("weights_loaded"))
    brd = ctx.enter_context(nc.semaphore("bias_rows_loaded"))
    hi = ctx.enter_context(nc.semaphore("high_parts"))
    lo = ctx.enter_context(nc.semaphore("low_parts"))
    cst = ctx.enter_context(nc.semaphore("constants_set"))
    spread = ctx.enter_context(nc.semaphore("value_bias_spread"))
    prod = ctx.enter_context(nc.semaphore("value_bias_projected"))
    step = ctx.enter_context(nc.semaphore("bias_split_steps"))
    boxes_ld, own_step, own_ready, tab_st = (ctx.enter_context(nc.semaphore(n)) for n in (
        "boxes_loaded", "own_steps", "own_ready", "table_stored"))
    cen, size, rsz = w["centres"], w["sizes"], w["inverse_sizes"]
    with ExitStack() as c:
        raw = c.enter_context(nc.sbuf_tensor("raw_weights", [P, 4, H * DK], F32))
        nb = 2 * H * DK + 16 * H
        braw = c.enter_context(nc.sbuf_tensor("raw_bias_rows", [P, nb], F32))
        bpart = c.enter_context(nc.sbuf_tensor("bias_part", [P, nb], BF16))
        bvs = c.enter_context(nc.sbuf_tensor("value_bias_spread_sb", [P, HP, P], F32))
        bvc = c.enter_context(nc.sbuf_tensor("value_bias_cols", [P, HP], F32))
        bob = c.enter_context(nc.sbuf_tensor("out_bias_rows", [P, P], F32))
        box, mrow = (c.enter_context(nc.sbuf_tensor(n, [P, T, NB], F32)) for n in ("boxes", "centre_and_inverse"))
        yb = c.enter_context(nc.psum_tensor("bias_psum", [P, P], F32))
        block = c.enter_context(nc.Block())

        @block.sync
        def _(sp):
            sp.dma_start(box[:, :, :], d["boxes"].rearrange("(t p) c -> p t c", p=P)).then_inc(boxes_ld, 16)
            for n, name in enumerate(("wq", "wk", "wv", "wo")):
                sp.dma_start(raw[:, n, :], d[name]).then_inc(ld, 16)
            sp.dma_start(bvc[:, :], d["bv"]).then_inc(ld, 16)
            sp.dma_start(bob[:, :], d["bo"].partition_broadcast(P)).then_inc(ld, 16)
            sp.dma_start(w["ident"][:, :], d["ident"]).then_inc(ld, 16)
            sp.dma_start(w["kron"][:, :], d["kron"]).then_inc(ld, 16)
            sp.dma_start(braw[:, :], d["bias_rows"].partition_broadcast(P)).then_inc(brd, 16)
            sp.wait_ge(own_ready, 1)
            sp.dma_start(mtab.rearrange("b (m c) -> (b m) c", c=NB).rearrange("(t p) c -> p t c", p=P),
                         mrow[:, :, :]).then_inc(tab_st, 16)
            sp.wait_ge(tab_st, 16)
            sp.wait_ge(ld, 16 * 8)

        @block.scalar
        def _(act):
            act.wait_ge(ld, 16 * 8)
            for n in range(4):
                act.activation(w["split"][:, n, 0, :], raw[:, n, :], ACT.Copy).then_inc(hi, 1)

        @block.gpsimd
        def _(pool):
            for name in ("qbd", "pbd"):
                pool.memset(w[name][:, :, :], 0.0).then_inc(cst, 1)
            pool.memset(w["ones"][:, :], 1.0).then_inc(cst, 1)
            pool.memset(w["minus_half"][:, :], -0.5).then_inc(cst, 1)
            pool.memset(w["quarter"][:, :], pi / 2).then_inc(cst, 1)
            pool.wait_ge(cst, 5)

        @block.vector
        def _(dve):
            dve.memset(w["brows"][:, :], 0.0).then_inc(step, 1)
            dve.wait_ge(boxes_ld, 16)
            dve.tensor_tensor(cen[:, :, :], box[:, :, 0:2], box[:, :, 2:4], ALU.add).then_inc(own_step, 1)
            dve.tensor_tensor(size[:, :, :], box[:, :, 2:4], box[:, :, 0:2], ALU.subtract).then_inc(own_step, 1)
            dve.wait_ge(own_step, 2)
            dve.tensor_scalar(cen[:, :, :], cen[:, :, :], 0.5, None, ALU.mult).then_inc(own_step, 1)
            dve.tensor_scalar(size[:, :, :], size[:, :, :], 1.0, None, ALU.add).then_inc(own_step, 1)
            dve.wait_ge(own_step, 4)
            dve.reciprocal(rsz[:, :, :], size[:, :, :]).then_inc(own_step, 1)
            dve.tensor_copy(mrow[:, :, 0:2], cen[:, :, :]).then_inc(own_step, 1)
            dve.wait_ge(own_step, 6)
            dve.tensor_copy(mrow[:, :, 2:4], rsz[:, :, :]).then_inc(own_ready, 1)
            dve.wait_ge(ld, 16 * 8)
            for j in range(HP):
                dve.tensor_copy(bvs[:, j, :], bvc[:, j:j + 1].to_broadcast([P, P])).then_inc(spread, 1)
            for n in range(4):
                dve.wait_ge(hi, n + 1)
                dve.tensor_tensor(w["split"][:, n, 1, :], raw[:, n, :], w["split"][:, n, 0, :],
                                  ALU.subtract).then_inc(lo, 1)
            dve.wait_ge(brd, 16)
            for n, row in enumerate((0, 32, 64)):
                dve.wait_ge(step, 1 + 3 * n)
                dve.tensor_copy(bpart[:, :], braw[:, :]).then_inc(step, 1)
                dve.wait_ge(step, 2 + 3 * n)
                dve.tensor_copy(w["brows"][row:row + 1, :], bpart[row:row + 1, :]).then_inc(step, 1)
                if n < 2:
                    dve.tensor_tensor(braw[:, :], braw[:, :], bpart[:, :], ALU.subtract).then_inc(step, 1)
            dve.wait_ge(prod, 1)
            dve.tensor_tensor(w["ybias"][:, :], yb[:, :], bob[:, :], ALU.add).then_inc(lo, 1)
            dve.wait_ge(lo, 5)

        @block.tensor
        def _(pe):
            pe.wait_ge(spread, HP)
            for j in range(HP):
                mm = pe.matmul(yb[:, :], bvs[:, j, :], raw[:, 3, j * P:(j + 1) * P],
                               start=(j == 0), stop=(j == HP - 1))
            mm.then_inc(prod, 1)


def relations_block(nc, ctx, w, d, ft, mtab, T):
    G = 8
    NG, HG = T // G, G // 2

    def sem(n):
        return ctx.enter_context(nc.semaphore(n))

    keys_ld = [sem("key_boxes_loaded0"), sem("key_boxes_loaded1")]
    dif_s, siz_s, sca_s, clip_s, log_s = sem("differences"), sem("size_ratios"), sem("scaled"), sem("clipped"), sem("logs")
    rnd_s, frc_s, sin_s, cos_s, turn_s = sem("rounding"), sem("fractions"), sem("sines"), sem("cosines"), sem("turned")
    abs_s = sem("absolute")
    out_s = [sem("turned_out_dve"), sem("turned_out_act")]
    st_s = [[sem(f"features_stored{e}{u}") for u in range(2)] for e in range(2)]
    with ExitStack() as c:
        def sb(n, s, dt=F32):
            return c.enter_context(nc.sbuf_tensor(n, s, dt))

        cen, size, rsz = w["centres"], w["sizes"], w["inverse_sizes"]
        keys = sb("key_side", [P, 2, G, S * NB])
        dist = sb("distances", [P, 2, G, NB, S])
        whole, frac, afrac = sb("whole_turns", [P, G, NB, S]), sb("part_turns", [P, 2, G, NB, S]), sb("abs_part", [P, 2, G, NB, S])
        feat = sb("features_sb", [P, 2, G, S, NF])
        fto = sb("turned_features", [P, 2, G, BANK])
        ps = c.enter_context(nc.psum_tensor("turn_psum", [P, G, BANK], F32))
        block = c.enter_context(nc.Block())

        def flat(x):
            return x.rearrange("p g c m -> p (g c m)")

        def early(g, n):
            return isinstance(g, int) and g < n

        def steps(eng, body):
            run_pairs(eng, NG + 2, lambda s, u, i, first, last: body(s, u, i))

        def enters(s):
            return not (isinstance(s, int) and s >= NG)

        def halfway(s):
            return not isinstance(s, int) or 1 <= s <= NG

        def leaves(s):
            return not early(s, 2)

        @block.sync
        def _(sp):
            def load(g, u):
                if not early(g, 2):
                    sp.wait_ge(dif_s, g - 1)
                    sp.wait_ge(siz_s, g - 1)
                for b in range(2):
                    src = mtab[at(g, 2 * G), :].rearrange("(t b) n -> b t n", b=2)[b]
                    sp.dma_start(keys[b * S:(b + 1) * S, u, :, :], src.partition_broadcast(S)).then_inc(keys_ld[u], 16)

            def body(s, u, i):
                if enters(s):
                    load(s, u)

            steps(sp, body)
            for e in range(2):
                for u in range(2):
                    sp.wait_ge(st_s[e][u], 16 * (NG // 2))

        @block.vector
        def _(dve):
            def body(s, u, i):
                if enters(s):
                    dve.wait_ge(keys_ld[u], 32 * (i + 1))
                    dve.tensor_tensor(dist[:, u, :, 0:2, :], keys[:, u, :, :].rearrange("p g (m c) -> p g c m", c=NB)[:, :, 0:2, :],
                                      cen[:, at(s, G), :].unsqueeze(3).to_broadcast([P, G, 2, S]), ALU.subtract).then_inc(dif_s, 1)
                g, v = s - 1, 1 - u
                L, W, Fr, A = flat(dist[:, v]), flat(whole[:, :, :, :]), flat(frac[:, v]), flat(afrac[:, v])
                if halfway(s):
                    dve.wait_ge(log_s, s)
                    dve.tensor_scalar(W, L, TURNS, ROUND, ALU.mult, ALU.add).then_inc(rnd_s, 1)
                    dve.wait_ge(rnd_s, 2 * g + 1)
                    dve.tensor_scalar(W, W, ROUND, None, ALU.subtract).then_inc(rnd_s, 1)
                if enters(s):
                    dve.wait_ge(sca_s, s + 1)
                    shift = dist[:, u, :, 0:2, :]
                    dve.tensor_scalar(shift.bitcast(I32), shift.bitcast(I32), NO_SIGN, None, ALU.bitwise_and).then_inc(abs_s, 1)
                    dve.wait_ge(abs_s, s + 1)
                    dve.tensor_scalar(shift, shift, 1e-3, None, ALU.max).then_inc(clip_s, 1)
                if halfway(s):
                    dve.wait_ge(rnd_s, 2 * g + 2)
                    if not early(g, 2):
                        dve.wait_ge(sin_s, g - 1)
                        dve.wait_ge(cos_s, g - 1)
                    dve.scalar_tensor_tensor(Fr, L, TURNS, W, ALU.mult, ALU.subtract).then_inc(frc_s, 1)
                    dve.wait_ge(frc_s, 2 * g + 1)
                    dve.tensor_scalar(A.bitcast(I32), Fr.bitcast(I32), NO_SIGN, None, ALU.bitwise_and).then_inc(frc_s, 1)
                if leaves(s):
                    if not early(s, 4):
                        dve.wait_ge(st_s[0][u], 16 * (i - 1))
                    for k in range(0, G, 2):
                        dve.wait_ge(turn_s, G * (s - 2) + k + 1)
                        dve.tensor_copy(fto[:, u, k, :], ps[:, k, :]).then_inc(out_s[0], 1)

            steps(dve, body)

        @block.gpsimd
        def _(pool):
            def body(s, u, i):
                if not enters(s):
                    return
                pool.wait_ge(keys_ld[u], 32 * (i + 1))
                if not early(s, 2):
                    pool.wait_ge(frc_s, 2 * s - 3)
                pool.tensor_tensor(dist[:, u, :, 2:4, :], keys[:, u, :, :].rearrange("p g (m c) -> p g c m", c=NB)[:, :, 2:4, :],
                                   size[:, at(s, G), :].unsqueeze(3).to_broadcast([P, G, 2, S]), ALU.mult).then_inc(siz_s, 1)
                pool.wait_ge(dif_s, s + 1)
                pool.tensor_tensor(dist[:, u, :, 0:2, :], dist[:, u, :, 0:2, :],
                                   rsz[:, at(s, G), :].unsqueeze(3).to_broadcast([P, G, 2, S]), ALU.mult).then_inc(sca_s, 1)

            steps(pool, body)

        @block.scalar
        def _(act):
            def store(g, u):
                for e in range(2):
                    act.wait_ge(out_s[e], HG * (g + 1))
                    act.dma_start(ft[at(g, G)].rearrange("(k e) p n -> e p k n", e=2)[e],
                                  fto[:, u, e:G:2, :]).then_inc(st_s[e][u], 16)

            def body(s, u, i):
                if not early(s, 3):
                    store(s - 3, 1 - u)
                if enters(s):
                    act.wait_ge(clip_s, s + 1)
                    act.wait_ge(siz_s, s + 1)
                    act.activation(flat(dist[:, u]), flat(dist[:, u]), ACT.Ln).then_inc(log_s, 1)
                if leaves(s):
                    if not early(s, 4):
                        act.wait_ge(st_s[1][u], 16 * (i - 1))
                    for k in range(1, G, 2):
                        act.wait_ge(turn_s, G * (s - 2) + k + 1)
                        act.activation(fto[:, u, k, :], ps[:, k, :], ACT.Copy).then_inc(out_s[1], 1)
                if halfway(s):
                    g, v = s - 1, 1 - u
                    fv = feat[:, v].rearrange("p g m f -> p g f m")
                    if not early(g, 2):
                        act.wait_ge(turn_s, G * (g - 1))
                    act.wait_ge(frc_s, 2 * g + 1)
                    act.activation(fv[:, :, 0:NB, :], frac[:, v], ACT.Sin, scale=SIN_SCALE).then_inc(sin_s, 1)
                    act.wait_ge(frc_s, 2 * g + 2)
                    act.activation(fv[:, :, NB:NF, :], afrac[:, v], ACT.Sin, bias=w["quarter"][:, 0:1],
                                   scale=-SIN_SCALE).then_inc(cos_s, 1)

            steps(act, body)
            store(NG - 1, 1)

        @block.tensor
        def _(pe):
            def turn(g, u, i, first, last):
                pe.wait_ge(sin_s, g + 1)
                pe.wait_ge(cos_s, g + 1)
                for k in range(G):
                    if not early(g, 1) and k < 2:
                        pe.wait_ge(out_s[k], HG * g)
                    row = feat[:, u, k, :, :].rearrange("p m f -> p (m f)")
                    for q in range(NB):
                        mm = pe.transpose(ps[:, k, q * P:(q + 1) * P], row[:, q * P:(q + 1) * P], w["ident"][:, :])
                    mm.then_inc(turn_s, 1)

            run_pairs(pe, NG, turn)


def attention_block(nc, ctx, w, d, ft, x2d, T):
    def sem(n):
        return ctx.enter_context(nc.semaphore(n))

    ch_s = sem("ctx_high")
    x_ld, c_ld, f_ld = ([sem(f"{n}_loaded{u}") for u in range(2)] for n in ("x", "ctx", "features"))
    x2_st = [sem("x2_stored0"), sem("x2_stored1")]
    stats, rstd, xn_s, xb_s, c_s = sem("ln_stats"), sem("ln_rstd"), sem("x_normed"), sem("x_biased"), sem("ctx_split")
    xT_s, xh_s, xl_s = sem("x_turned"), sem("xT_high"), sem("xT_low")
    q_s, k_s, v_s = sem("q_done"), sem("k_done"), sem("v_done")
    qa, ka, kd, va = sem("q_out"), sem("k_out_act"), sem("k_out_dve"), sem("v_out")
    sc_s, g_s, mx_s, sub_s, exp_s, p_s = sem("scores_done"), sem("gates_done"), sem("row_max"), sem("shifted"), sem("exps"), sem("probs")
    pT_s, pa, pd = sem("probs_turned"), sem("probs_out_act"), sem("probs_out_dve")
    gated, summed, inverted = sem("exps_gated"), sem("exps_summed"), sem("sums_inverted")
    o_s, oh_s, ol_s, y_s, x2_s = (sem(n) for n in ("heads_done", "headsT_high", "headsT_low", "attn_out", "x2_ready"))
    with ExitStack() as c:
        def sb(n, s, dt=F32):
            return c.enter_context(nc.sbuf_tensor(n, s, dt))

        xt, xn, xb = sb("x_tile", [P, 2, P]), sb("x_norm", [P, 2, P]), sb("x_plus_bias", [P, 2, P])
        ct, cT = sb("ctxT_tile", [P, 2, P]), sb("ctxT_parts", [P, 2, 2, P], BF16)
        xT = sb("xT_parts", [P, 2, P], BF16)
        fts = sb("feature_tile", [P, 2, BANK])
        st6, mv, var, rs = sb("bn", [P, 2, 6]), sb("mean_var", [P, 2, 2]), sb("var_eps", [P, 2, 1]), sb("rstd", [P, 2, 1])
        kT = sb("kT", [P, H, S])
        z, mx = sb("logits", [P, H, S]), sb("row_maximum", [P, H])
        total, inv = sb("exp_sums", [P, H]), sb("inverse_sums", [P, H])
        oT = sb("headsT_parts", [P, 2, HP, P], BF16)
        x2 = sb("x2_tile", [P, 2, P])
        ps = c.enter_context(nc.psum_tensor("attn_psum", [P, 8, BANK], F32))
        flat = ps[:, :, :].rearrange("p b n -> p (b n)")
        SC = flat[:, 0:2 * BANK].rearrange("p (h k) -> p h k", k=S)
        GA = flat[:, 2 * BANK:4 * BANK]
        XQ = flat[:, 4 * BANK:6 * BANK].rearrange("p (j n) -> p j n", n=P)
        YT = flat[:, 6 * BANK:8 * BANK].rearrange("p (j n) -> p j n", n=P)
        KP = flat[:, 0:2 * BANK].rearrange("p (j n) -> p j n", n=P)
        AO = ps[:, 3, 0:P]
        qbd, pbd, v, split = w["qbd"], w["pbd"], w["v"], w["split"]
        block = c.enter_context(nc.Block())

        @block.sync
        def _(sp):
            def loads(t, u, wait_free):
                if wait_free:
                    sp.wait_ge(xb_s, t - 1)
                    sp.wait_ge(xn_s, t - 1)
                    sp.wait_ge(c_s, t - 1)
                sp.dma_start(xt[:, u, :], d["x"][at(t, P), :]).then_inc(x_ld[u], 16)
                sp.dma_start(ct[:, u, :], d["ctxT"][:, at(t, P)]).then_inc(c_ld[u], 16)
                if wait_free:
                    sp.wait_ge(g_s, t - 1)
                sp.dma_start(fts[:, u, :], ft[at(t, 1)].rearrange("t p n -> (t p) n")).then_inc(f_ld[u], 16)

            def body(t, u, i, first, last):
                if not (isinstance(t, int) and t + 2 >= T):
                    loads(t + 2, u, True)
                if not first:
                    sp.wait_ge(x2_s, t)
                    sp.dma_start(x2d[at(t - 1, P), :], x2[:, 1 - u, :]).then_inc(x2_st[1 - u], 16)

            loads(0, 0, False)
            loads(1, 1, False)
            run_pairs(sp, T, body)
            sp.wait_ge(x2_s, T)
            sp.dma_start(x2d[at(T - 1, P), :], x2[:, 1, :]).then_inc(x2_st[1], 16)
            for u in range(2):
                sp.wait_ge(x2_st[u], 16 * (T // 2))

        @block.gpsimd
        def _(pool):
            def prepare(t, u, i):
                pool.wait_ge(stats, 2 * t + 2)
                hold(pool, w["held_pool"])
                pool.tensor_scalar(var[:, u, :], mv[:, u, 1:2], LN_EPS, None, ALU.add).then_inc(rstd, 1)
                pool.wait_ge(rstd, 2 * t + 1)
                pool.tensor_tensor(rs[:, u, :], var[:, u, :], w["minus_half"][:, :], ALU.pow).then_inc(rstd, 1)
                pool.wait_ge(rstd, 2 * t + 2)
                hold(pool, w["held_pool"])
                pool.tensor_scalar(xn[:, u, :], xt[:, u, :], mv[:, u, 0:1], rs[:, u, :],
                                   ALU.subtract, ALU.mult).then_inc(xn_s, 1)
                pool.wait_ge(c_ld[u], 16 * (i + 1))
                if not (isinstance(t, int) and t < 2):
                    pool.wait_ge(v_s, t - 1)
                hold(pool, w["held_pool"])
                pool.tensor_copy(cT[:, u, 0, :], ct[:, u, :]).then_inc(ch_s, 1)
                pool.wait_ge(ch_s, t + 1)
                pool.tensor_tensor(cT[:, u, 1, :], ct[:, u, :], cT[:, u, 0, :], ALU.subtract).then_inc(c_s, 1)
                if not (isinstance(t, int) and t < 2):
                    pool.wait_ge(x2_s, t - 1)
                pool.tensor_tensor(xb[:, u, :], xt[:, u, :], w["ybias"][:, :], ALU.add).then_inc(xb_s, 1)

            def body(t, u, i, first, last):
                if not last:
                    if not first:
                        pool.wait_ge(xT_s, t)
                    prepare(t + 1, 1 - u, i + u)

            prepare(0, 0, 0)
            run_pairs(pool, T, body)

        @block.vector
        def _(dve):
            def norm_stats(t, u, i):
                dve.wait_ge(x_ld[u], 16 * (i + 1))
                dve.bn_stats(st6[:, u, :], xt[:, u, :]).then_inc(stats, 1)
                dve.wait_ge(stats, 2 * t + 1)
                hold(dve, w["held_dve"])
                dve.bn_aggr(mv[:, u, :], st6[:, u, :]).then_inc(stats, 1)

            def low_xT(t):
                dve.wait_ge(xh_s, t + 1)
                dve.tensor_tensor(xT[:, 1, :], XQ[:, 0, :], xT[:, 0, :], ALU.subtract).then_inc(xl_s, 1)

            def k_out(t):
                dve.wait_ge(k_s, t + 1)
                for b in range(2):
                    ins = dve.tensor_copy(kT[b * S:(b + 1) * S, 1:H:2, :], KP[S:P, :, b * S:(b + 1) * S])
                ins.then_inc(kd, 1)

            def low_oT(t):
                dve.wait_ge(oh_s, t + 1)
                dve.tensor_tensor(oT[:, 1, :, :], YT, oT[:, 0, :, :], ALU.subtract).then_inc(ol_s, 1)

            def add_out(t, u, i):
                dve.wait_ge(y_s, t + 1)
                dve.wait_ge(xb_s, t + 1)
                if not (isinstance(t, int) and t < 2):
                    dve.wait_ge(x2_st[u], 16 * i)
                dve.tensor_tensor(x2[:, u, :], AO, xb[:, u, :], ALU.add).then_inc(x2_s, 1)

            norm_stats(0, 0, 0)
            low_xT(0)
            k_out(0)

            def body(t, u, i, first, last):
                if not last:
                    if not first:
                        dve.wait_ge(xn_s, t)
                    norm_stats(t + 1, 1 - u, i + u)
                if not first:
                    low_oT(t - 1)
                for half in range(2):
                    heads = slice(half * HP, (half + 1) * HP)
                    dve.wait_ge(sc_s, 2 * t + 1 + half)
                    dve.tensor_reduce(mx[:, heads], SC[:, heads, :], X, ALU.max).then_inc(mx_s, 1)
                dve.wait_ge(mx_s, 2 * t + 2)
                dve.tensor_tensor(z[:, :, :], SC, mx[:, :].unsqueeze(2).to_broadcast([P, H, S]), ALU.subtract).then_inc(sub_s, 1)
                if not last:
                    low_xT(t + 1)
                dve.wait_ge(exp_s, t + 1)
                dve.wait_ge(g_s, t + 1)
                dve.scalar_tensor_tensor(z[:, :, :], GA.rearrange("p (m h) -> p h m", h=H), 1e-6, z[:, :, :],
                                         ALU.max, ALU.mult).then_inc(gated, 1)
                dve.wait_ge(gated, t + 1)
                dve.tensor_reduce(total[:, :], z[:, :, :], X, ALU.add).then_inc(summed, 1)
                dve.wait_ge(summed, t + 1)
                dve.reciprocal(inv[:, :], total[:, :]).then_inc(inverted, 1)
                dve.wait_ge(inverted, t + 1)
                for half in range(2):
                    heads = slice(half * HP, (half + 1) * HP)
                    dve.tensor_tensor(z[:, heads, :], z[:, heads, :], inv[:, heads].unsqueeze(2).to_broadcast([P, HP, S]),
                                      ALU.mult).then_inc(p_s, 1)
                if not last:
                    k_out(t + 1)
                dve.wait_ge(pT_s, t + 1)
                for b in range(2):
                    ins = dve.tensor_copy(pbd[b * S:(b + 1) * S, 1:H:2, b * S:(b + 1) * S], YT[S:P, :, b * S:(b + 1) * S])
                ins.then_inc(pd, 1)
                if not first:
                    add_out(t - 1, 1 - u, i - 1 + u)

            run_pairs(dve, T, body)
            low_oT(T - 1)
            add_out(T - 1, 1, T // 2 - 1)

        @block.scalar
        def _(act):
            def high_xT(t):
                act.wait_ge(xT_s, t + 1)
                act.activation(xT[:, 0, :], XQ[:, 0, :], ACT.Copy).then_inc(xh_s, 1)

            def out_halves(done, out, src, dst, t, halves):
                act.wait_ge(done, t + 1)
                for half in range(halves):
                    for b in range(2):
                        cols = slice(b * S, (b + 1) * S)
                        to = dst[b * S:(b + 1) * S, half:H:2, cols]
                        ins = act.activation(to, src[half * S:(half + 1) * S, :, cols], ACT.Copy)
                ins.then_inc(out, 1)

            def k_out(t):
                act.wait_ge(k_s, t + 1)
                for b in range(2):
                    ins = act.activation(kT[b * S:(b + 1) * S, 0:H:2, :], KP[0:S, :, b * S:(b + 1) * S], ACT.Copy)
                ins.then_inc(ka, 1)

            def v_out(t):
                act.wait_ge(v_s, t + 1)
                if not (isinstance(t, int) and t < 1):
                    act.wait_ge(o_s, t)
                act.activation(v[:, :, :], XQ.rearrange("p j (e n) -> p (j e) n", e=2), ACT.Copy).then_inc(va, 1)

            def high_oT(t):
                act.wait_ge(o_s, t + 1)
                act.activation(oT[:, 0, :, :], YT, ACT.Copy).then_inc(oh_s, 1)

            high_xT(0)
            out_halves(q_s, qa, XQ, qbd, 0, 2)
            k_out(0)
            v_out(0)

            def body(t, u, i, first, last):
                if not last:
                    high_xT(t + 1)
                act.wait_ge(sub_s, t + 1)
                act.activation(z[:, :, :], z[:, :, :], ACT.Exp, scale=DK ** -0.5).then_inc(exp_s, 1)
                if not last:
                    out_halves(q_s, qa, XQ, qbd, t + 1, 2)
                    k_out(t + 1)
                out_halves(pT_s, pa, YT, pbd, t, 1)
                high_oT(t)
                if not last:
                    v_out(t + 1)

            run_pairs(act, T, body)

        @block.tensor
        def _(pe):
            def x_turn(t, u):
                pe.wait_ge(xn_s, t + 1)
                pe.transpose(XQ[:, 0, :], xn[:, u, :], w["ident"][:, :]).then_inc(xT_s, 1)

            def project(n, parts, done, out):
                for j in range(HP):
                    cols = slice(j * P, (j + 1) * P)
                    pe.matmul(out[:, j, :], w["brows"][:, n * H * DK + j * P:n * H * DK + (j + 1) * P], w["ones"][:, :], start=True, stop=False)
                    pe.matmul(out[:, j, :], split[:, n, 0, cols], parts[0], start=False, stop=False)
                    pe.matmul(out[:, j, :], split[:, n, 0, cols], parts[1], start=False, stop=False)
                    mm = pe.matmul(out[:, j, :], split[:, n, 1, cols], parts[0], start=False, stop=True)
                mm.then_inc(done, 1)

            def q_proj(t):
                pe.wait_ge(xl_s, t + 1)
                project(0, (xT[:, 0, :], xT[:, 1, :]), q_s, XQ)

            def k_proj(t, u):
                pe.wait_ge(c_s, t + 1)
                if not (isinstance(t, int) and t < 1):
                    pe.wait_ge(sub_s, t)
                project(1, (cT[:, u, 0, :], cT[:, u, 1, :]), k_s, KP)

            def v_proj(t, u):
                pe.wait_ge(qa, t + 1)
                for half in range(2):
                    out = flat[:, (4 + half) * BANK:(5 + half) * BANK]
                    cols = slice(half * BANK, (half + 1) * BANK)
                    pe.matmul(out, cT[:, u, 0, :], split[:, 2, 0, cols], start=True, stop=False)
                    pe.matmul(out, cT[:, u, 0, :], split[:, 2, 1, cols], start=False, stop=False)
                    mm = pe.matmul(out, cT[:, u, 1, :], split[:, 2, 0, cols], start=False, stop=True)
                mm.then_inc(v_s, 1)

            def out_proj(t):
                pe.wait_ge(ol_s, t + 1)
                for j in range(HP):
                    cols = slice(j * P, (j + 1) * P)
                    pe.matmul(AO, oT[:, 0, j, :], split[:, 3, 0, cols], start=(j == 0), stop=False)
                    pe.matmul(AO, oT[:, 0, j, :], split[:, 3, 1, cols], start=False, stop=False)
                    mm = pe.matmul(AO, oT[:, 1, j, :], split[:, 3, 0, cols], start=False, stop=(j == HP - 1))
                mm.then_inc(y_s, 1)

            x_turn(0, 0)
            q_proj(0)
            k_proj(0, 0)
            v_proj(0, 0)

            def body(t, u, i, first, last):
                pe.wait_ge(qa, t + 1)
                pe.wait_ge(ka, t + 1)
                pe.wait_ge(kd, t + 1)
                for h in range(H):
                    mm = pe.matmul(SC[:, h, :], qbd[:, h, :], kT[:, h, :], start=True, stop=True)
                    if h % HP == HP - 1:
                        mm.then_inc(sc_s, 1)
                if not last:
                    pe.wait_ge(va, t + 1)
                    x_turn(t + 1, 1 - u)
                pe.wait_ge(f_ld[u], 16 * (i + 1))
                if not (isinstance(t, int) and t < 2):
                    pe.wait_ge(x2_s, t - 1)
                for q in range(NB):
                    out = GA[:, q * 16 * H:(q + 1) * 16 * H]
                    pe.matmul(out, w["ones"][:, :], w["brows"][:, 2 * H * DK:], start=True, stop=False)
                    mm = pe.matmul(out, fts[:, u, q * P:(q + 1) * P], w["kron"][:, :], start=False, stop=True)
                mm.then_inc(g_s, 1)
                if not last:
                    q_proj(t + 1)
                    k_proj(t + 1, 1 - u)
                if not first:
                    pe.wait_ge(gated, t + 1)
                    out_proj(t - 1)
                zf = z[:, :, :].rearrange("p h k -> p (h k)")
                for j in range(HP):
                    if j % (HP // 2) == 0:
                        pe.wait_ge(p_s, 2 * t + 1 + j // (HP // 2))
                    mm = pe.transpose(YT[:, j, :], zf[:, j * P:(j + 1) * P], w["ident"][:, :])
                mm.then_inc(pT_s, 1)
                if not last:
                    v_proj(t + 1, 1 - u)
                pe.wait_ge(pa, t + 1)
                pe.wait_ge(pd, t + 1)
                pe.wait_ge(va, t + 1)
                for h in range(H):
                    half = slice(h % 2 * DK, (h % 2 + 1) * DK)
                    mm = pe.matmul(YT[half, h // 2, :], v[:, h, :], pbd[:, h, :], start=True, stop=True)
                mm.then_inc(o_s, 1)

            run_pairs(pe, T, body)
            out_proj(T - 1)


def raw_weights(w, e):
    if e == E:
        return w["raw_shared"][:, 0, :]
    n = 2 * FB
    return w["shared"][:, e * n:(e + 1) * n, :].rearrange("p t n -> p (t n)")


def norm_block(nc, ctx, w, d, x2d, T):
    C = T // Q

    def sem(n):
        return ctx.enter_context(nc.semaphore(n))

    ld = [sem("n_x2_loaded0"), sem("n_x2_loaded1")]
    cst, stats, agg_s, var_s, rstd_s, xn_s = (sem(n) for n in (
        "n_constants", "n_stats", "n_means", "n_variance", "n_rstd", "n_normed"))
    xT_s, xe_s, xh_s, xl_s, pr_s, num_s, row_s = (sem(n) for n in (
        "n_turned", "n_turned_out", "n_high", "n_low", "n_scored", "n_logits_out", "n_rows_kept"))
    w_ld = sem("expert_weights_loaded")
    rows, x2, xnT = w["rows"], w["x2"], w["xnT"]
    with ExitStack() as c_:
        def sb(n, s, dt=F32):
            return c_.enter_context(nc.sbuf_tensor(n, s, dt))

        st6, mv = sb("n_bn", [P, 2, Q, 6]), sb("n_mv", [P, 2, Q, 2])
        var, rs, xT = sb("n_var", [P, 2, Q]), sb("n_rs", [P, 2, Q]), sb("n_xT", [P, 2, Q * P])
        xn = sb("n_xn", [P, 2, Q, P])
        gw = sb("gate_weights", [P, E])
        ps = c_.enter_context(nc.psum_tensor("n_psum", [P, 2, Q * P], F32))
        pr = c_.enter_context(nc.psum_tensor("n_scores_psum", [P, T * E], F32))
        block = c_.enter_context(nc.Block())

        @block.sync
        def _(sp):
            sp.dma_start(gw[:, :], d["gate_w"]).then_inc(cst, 16)

            def body(c, u, i, first, last):
                if not (isinstance(c, int) and c < 2):
                    sp.wait_ge(ld[u], 16 * i)
                sp.dma_start(x2[:, at(c, Q), :],
                             x2d[at(c, Q * P), :].rearrange("(q p) n -> p q n", p=P)).then_inc(ld[u], 16)

            run_pairs(sp, C, body)
            sp.dma_start(w["up_bias"][:, :, :], d["up_b"]).then_inc(w_ld, 16)
            sp.dma_start(w["down_bias"][:, :, :], d["down_b"].partition_broadcast(P)).then_inc(w_ld, 16)
            for e in range(E + 1):
                raw = raw_weights(w, e)
                sp.dma_start(raw[:, 0:FB * P], d["up"][e]).then_inc(w_ld, 16)
                sp.dma_start(raw[:, FB * P:].rearrange("p (j n) -> p j n", n=P),
                             d["down"][e].rearrange("(j p) n -> p j n", p=P)).then_inc(w_ld, 16)
            sp.wait_ge(w_ld, 16 * 2 * (E + 2))

        @block.vector
        def _(dve):
            def statistics(c, u, i):
                dve.wait_ge(ld[u], 16 * (i + 1))
                if not (isinstance(c, int) and c < 2):
                    dve.wait_ge(xn_s, c - 1)
                for q in range(Q):
                    ins = dve.bn_stats(st6[:, u, q, :], tile_of(x2, c, q))
                ins.then_inc(stats, 1)
                dve.wait_ge(stats, c + 1)
                hold(dve, w["held_dve"])
                for q in range(Q):
                    ins = dve.bn_aggr(mv[:, u, q, :], st6[:, u, q, :])
                ins.then_inc(agg_s, 1)

            def low(c, u):
                dve.wait_ge(xh_s, c + 1)
                cols = at(c, Q * P)
                dve.tensor_tensor(xnT[:, 1, cols], ps[:, u, :], xnT[:, 0, cols], ALU.subtract).then_inc(xl_s, 1)

            statistics(0, 0, 0)

            def body(c, u, i, first, last):
                if not last:
                    statistics(c + 1, 1 - u, i + u)
                dve.wait_ge(rstd_s, c + 1)
                if not (isinstance(c, int) and c < 2):
                    dve.wait_ge(xT_s, c - 1)
                    dve.wait_ge(row_s, c - 1)
                for q in range(Q):
                    ins = dve.tensor_scalar(xn[:, u, q, :], tile_of(x2, c, q), mv[:, u, q, 0:1], rs[:, u, q:q + 1],
                                            ALU.subtract, ALU.mult)
                ins.then_inc(xn_s, 1)
                if not first:
                    low(c - 1, 1 - u)

            run_pairs(dve, C, body)
            low(C - 1, 1)
            dve.wait_ge(pr_s, C)
            dve.tensor_copy(w["logits"].rearrange("p t e -> p (t e)"), pr[:, :]).then_inc(num_s, 1)
            dve.wait_ge(num_s, 1)

        @block.gpsimd
        def _(pool):
            def body(c, u, i, first, last):
                pool.wait_ge(agg_s, c + 1)
                if not (isinstance(c, int) and c < 2):
                    pool.wait_ge(xn_s, c - 1)
                hold(pool, w["held_pool"])
                pool.tensor_scalar(var[:, u, :], mv[:, u, :, 1], LN_EPS, None, ALU.add).then_inc(var_s, 1)
                pool.wait_ge(var_s, c + 1)
                pool.tensor_tensor(rs[:, u, :], var[:, u, :], w["minus_half"][:, 0:1].to_broadcast([P, Q]),
                                   ALU.pow).then_inc(rstd_s, 1)
                if not first:
                    keep_rows(c - 1, 1 - u)

            def keep_rows(c, u):
                pool.wait_ge(xn_s, c + 1)
                hold(pool, w["held_pool"])
                pool.tensor_copy(rows[:, at(c, Q), :], xn[:, u, :, :]).then_inc(row_s, 1)

            run_pairs(pool, C, body)
            keep_rows(C - 1, 1)
            pool.wait_ge(row_s, C)

        @block.scalar
        def _(act):
            def body(c, u, i, first, last):
                act.wait_ge(xT_s, c + 1)
                if not (isinstance(c, int) and c < 2):
                    act.wait_ge(pr_s, c - 1)
                act.activation(xT[:, u, :], ps[:, u, :], ACT.Copy).then_inc(xe_s, 1)
                act.activation(xnT[:, 0, at(c, Q * P)], ps[:, u, :], ACT.Copy).then_inc(xh_s, 1)

            run_pairs(act, C, body)

        @block.tensor
        def _(pe):
            def turn(c, u):
                pe.wait_ge(xn_s, c + 1)
                if not (isinstance(c, int) and c < 2):
                    pe.wait_ge(xl_s, c - 1)
                    pe.wait_ge(xe_s, c - 1)
                for q in range(Q):
                    mm = pe.transpose(ps[:, u, q * P:(q + 1) * P], xn[:, u, q, :], w["ident"][:, :])
                mm.then_inc(xT_s, 1)

            pe.wait_ge(cst, 16)
            turn(0, 0)

            def body(c, u, i, first, last):
                if not last:
                    turn(c + 1, 1 - u)
                pe.wait_ge(xe_s, c + 1)
                for q in range(Q):
                    cols = slice((c * Q + q) * E, (c * Q + q + 1) * E) if isinstance(c, int) else bass.ds(c * (Q * E) + q * E, E)
                    mm = pe.matmul(pr[:, cols], xT[:, u, q * P:(q + 1) * P], gw[:, :], start=True, stop=True)
                mm.then_inc(pr_s, 1)

            run_pairs(pe, C, body)


def dispatch_block(nc, ctx, w, d, gates, counts, T):
    CAP = (T + U) * P

    def sem(n):
        return ctx.enter_context(nc.semaphore(n))

    cst, step_s, sig_s, mask_s, rank_s, zero_s = (sem(n) for n in (
        "d_constants", "d_steps", "d_sigmoid", "d_mask", "d_ranked", "d_zeros"))
    high_s, low_s = sem("weights_high"), sem("weights_low")
    with ExitStack() as c:
        def sb(n, s, dt=F32):
            return c.enter_context(nc.sbuf_tensor(n, s, dt))

        gb, below = sb("gate_bias", [P, E]), sb("expert_number_less_8", [P, E])
        z, score, rest = sb("d_z", [P, T, E]), sb("d_score", [P, T, E]), sb("d_rest", [P, T, E])
        best, number = sb("d_best", [P, 2, T]), sb("d_number", [P, 2, T])
        same, hot = sb("d_same", [P, T, E]), sb("d_hot", [P, 2, T, E])
        total, mask = sb("d_total", [P, T]), sb("d_mask_sb", [P, T, E], BF16)
        zeros, through, pos, dest = sb("d_zero_row", [P, T]), sb("d_through", [P, T, E]), sb("d_pos", [P, T, E]), sb("d_dest", [P, 2, T])
        before = sb("d_tokens_before", [P, P], BF16)
        pq = c.enter_context(nc.psum_tensor("d_rank_psum", [P, 2, T * E], F32))
        block = c.enter_context(nc.Block())

        @block.sync
        def _(sp):
            sp.dma_start(gb[:, :], d["gate_b"].partition_broadcast(P)).then_inc(cst, 16)
            sp.dma_start(below[:, :], d["numbers"].partition_broadcast(P)).then_inc(cst, 16)

        @block.gpsimd
        def _(pool):
            pool.memset(before[:, :], 1.0).then_inc(zero_s, 1)
            pool.wait_ge(zero_s, 1)
            pool.affine_select(out=before[:, :], in_=before[:, :], compare_op=ALU.is_gt, fill=0.0,
                               base=0, pattern=[[1, P]], channel_multiplier=-1).then_inc(zero_s, 1)
            pool.memset(zeros[:, :], 0.0).then_inc(zero_s, 1)
            for e in range(E + 1):
                pool.wait_ge(high_s, e + 1)
                pool.tensor_tensor(w["experts"][:, 1, e, :], raw_weights(w, e), w["experts"][:, 0, e, :],
                                   ALU.subtract).then_inc(low_s, 1)
            pool.wait_ge(low_s, E + 1)

        @block.scalar
        def _(act):
            act.wait_ge(step_s, 1)
            act.activation(score[:, :, :], z[:, :, :], ACT.Sigmoid).then_inc(sig_s, 1)
            for e in range(E + 1):
                act.activation(w["experts"][:, 0, e, :], raw_weights(w, e), ACT.Copy).then_inc(high_s, 1)

        @block.vector
        def _(dve):
            n = 0

            def step(ins):
                nonlocal n
                ins.then_inc(step_s, 1)
                n += 1
                dve.wait_ge(step_s, n)

            def each(x):
                return x.unsqueeze(2).to_broadcast([P, T, E])

            def every(x):
                return x.unsqueeze(1).to_broadcast([P, T, E])

            dve.wait_ge(cst, 32)
            step(dve.tensor_tensor(z[:, :, :], w["logits"][:, :, :], every(gb[:, :]), ALU.add))
            dve.wait_ge(sig_s, 1)
            for k, left in enumerate((score, rest)):
                step(dve.tensor_reduce(best[:, k, :], left[:, :, :], X, ALU.max))
                step(dve.tensor_tensor(same[:, :, :], left[:, :, :], each(best[:, k, :]), ALU.is_equal))
                step(dve.tensor_tensor(same[:, :, :], same[:, :, :], every(below[:, :]), ALU.mult))
                step(dve.tensor_reduce(number[:, k, :], same[:, :, :], X, ALU.min))
                step(dve.tensor_tensor(hot[:, k, :, :], every(below[:, :]), each(number[:, k, :]), ALU.is_equal))
                if k == 0:
                    step(dve.scalar_tensor_tensor(rest[:, :, :], hot[:, 0, :, :], -4.0, score[:, :, :], ALU.mult, ALU.add))
            dve.tensor_tensor(mask[:, :, :], hot[:, 0, :, :], hot[:, 1, :, :], ALU.add).then_inc(mask_s, 1)
            step(dve.tensor_tensor(total[:, :], best[:, 0, :], best[:, 1, :], ALU.add))
            step(dve.tensor_scalar(total[:, :], total[:, :], 1e-6, None, ALU.add))
            step(dve.reciprocal(total[:, :], total[:, :]))
            for k in range(2):
                step(dve.tensor_tensor(gates[:, :, k], best[:, k, :], total[:, :], ALU.mult))
            dve.wait_ge(zero_s, 3)
            dve.wait_ge(rank_s, 1)
            ranks, sums = (pq[:, k, :].rearrange("p (t e) -> p t e", e=E) for k in range(2))
            for e in range(E):
                step(dve.tensor_tensor_scan(through[:, :, e], sums[:, :, e], zeros[:, :], float(e * CAP), ALU.add, ALU.add))
            step(dve.tensor_copy(counts[:, :], through[:, T - 1, :]))
            step(dve.tensor_tensor(through[:, :, :], through[:, :, :], sums, ALU.subtract))
            step(dve.tensor_tensor(pos[:, :, :], through[:, :, :], ranks, ALU.add))
            for k in range(2):
                step(dve.tensor_tensor(same[:, :, :], hot[:, k, :, :], pos[:, :, :], ALU.mult))
                step(dve.tensor_reduce(dest[:, k, :], same[:, :, :], X, ALU.add))
                step(dve.tensor_copy(w["dest"][:, k, :], dest[:, k, :]))

        @block.tensor
        def _(pe):
            pe.wait_ge(zero_s, 2)
            pe.wait_ge(mask_s, 1)
            flat = mask[:, :, :].rearrange("p t e -> p (t e)")
            pe.matmul(pq[:, 0, :], before[:, :], flat, start=True, stop=True)
            pe.matmul(pq[:, 1, :], w["ones"][:, :], flat, start=True, stop=True).then_inc(rank_s, 1)


def units(T):
    return 2 * T // U + E


def unit_rows(slots, rows):
    return slots[rows, :].rearrange("(p k) n -> p k n", k=U)


def routed_block(nc, ctx, w, d, slots, results, T):
    N = units(T)
    WAYS = 8
    CAP = (T + U) * P
    def sem(n):
        return ctx.enter_context(nc.semaphore(n))

    ld, y_st = [sem(f"e_rows_loaded{q}") for q in range(WAYS)], [sem(f"e_results_stored{q}") for q in range(WAYS)]
    xT_s, xh_s, xl_s, up_s, gl_s, hh_s, hl_s, dn_s, y_s = (sem(n) for n in (
        "e_turned", "e_high", "e_low", "e_up", "e_gelu", "e_hidden_high", "e_hidden_low", "e_down", "e_result"))
    id_s = sem("e_numbers_copied")
    with ExitStack() as c:
        def sb(n, s, dt=F32):
            return c.enter_context(nc.sbuf_tensor(n, s, dt))

        xr, xT = sb("e_rows", [P, WAYS, U, ROW]), sb("e_T", [P, 2, 2, U * P], BF16)
        hid, hidp = sb("e_hidden", [P, 2, FB, U * P]), sb("e_hidden_parts", [P, 4, 2, FB, U * P], BF16)
        y, idn = sb("e_y", [P, WAYS, U, P]), sb("e_numbers", [P, WAYS, U], I32)
        ps = c.enter_context(nc.psum_tensor("e_psum", [P, 2, BANK], F32))
        ph = c.enter_context(nc.psum_tensor("e_up_psum", [P, 2, FB, U * P], F32))
        pd = c.enter_context(nc.psum_tensor("e_down_psum", [P, 2, BANK], F32))
        block = c.enter_context(nc.Block())
        exp_i, start_i = w["unit_expert"], w["unit_start"]

        def per_unit(x, t):
            return x[:, t:t + 1] if isinstance(t, int) else x[:, bass.ds(t, 1)]

        @block.sync
        def _(sp):
            def load(t, q):
                r = sp.value_load(per_unit(start_i, t), min_val=0, max_val=E * CAP)
                sp.dma_start(xr[:, q, :, :], unit_rows(slots, bass.ds(r, U * P))).then_inc(ld[q], 16)

            for t in range(WAYS):
                load(t, t)

            def body(t, q, i, first, last):
                if not (isinstance(t, int) and t + WAYS >= N):
                    sp.wait_ge(xT_s, t + 1)
                    sp.wait_ge(id_s, t + 1)
                    load(t + WAYS, q)

            run_tiles(sp, N, WAYS, body)

        @block.vector
        def _(dve):
            def x_parts(t, q, i):
                u = q % 2
                dve.wait_ge(ld[q], 16 * (i + 1))
                if not (isinstance(t, int) and t < WAYS):
                    dve.wait_ge(y_st[q], 16 * U * i)
                dve.tensor_copy(idn[:, q, :], xr[:, q, :, P].bitcast(I32)).then_inc(id_s, 1)
                dve.wait_ge(xh_s, t + 1)
                dve.tensor_tensor(xT[:, u, 1, :], ps[:, u, 0:U * P], xT[:, u, 0, :], ALU.subtract).then_inc(xl_s, 1)

            def result(t, q, i):
                e = dve.value_load(per_unit(exp_i, t), min_val=0, max_val=E)
                dve.wait_ge(dn_s, t + 1)
                dve.tensor_tensor(y[:, q, :, :], pd[:, q % 2, 0:U * P].rearrange("p (k n) -> p k n", n=P),
                                  w["down_bias"][:, bass.ds(e, 1), :].to_broadcast([P, U, P]),
                                  ALU.add).then_inc(y_s, 1)

            x_parts(0, 0, 0)

            def body(t, q, i, first, last):
                u = q % 2
                if not last:
                    x_parts(t + 1, (q + 1) % WAYS, i + (q == WAYS - 1))
                dve.wait_ge(gl_s, t + 1)
                if not (isinstance(t, int) and t < 4):
                    dve.wait_ge(dn_s, t - 3)
                dve.tensor_copy(hidp[:, q % 4, 0, :, :], hid[:, u, :, :]).then_inc(hh_s, 1)
                dve.wait_ge(hh_s, t + 1)
                dve.tensor_tensor(hidp[:, q % 4, 1, :, :], hid[:, u, :, :], hidp[:, q % 4, 0, :, :], ALU.subtract).then_inc(hl_s, 1)
                if not (isinstance(t, int) and t < 2):
                    result(t - 2, (q - 2) % WAYS, i - (q < 2))

            run_tiles(dve, N, WAYS, body)
            result(N - 2, WAYS - 2, N // WAYS - 1)
            result(N - 1, WAYS - 1, N // WAYS - 1)

        @block.gpsimd
        def _(pool):
            def body(t, q, i, first, last):
                pool.wait_ge(y_s, t + 1)
                hold(pool, w["held_pool"])
                for k in range(U):
                    pool.indirect_dma_start(results, bass.IndirectOffsetOnAxis(idn[:, q, k:k + 1], 0), y[:, q, k, :], None,
                                            bounds_check=2 * T * P - 1, oob_is_err=False).then_inc(y_st[q], 16)

            run_tiles(pool, N, WAYS, body)
            for q in range(WAYS):
                pool.wait_ge(y_st[q], 16 * U * (N // WAYS))

        @block.scalar
        def _(act):
            def high_x(t, u):
                act.wait_ge(xT_s, t + 1)
                if not (isinstance(t, int) and t < 2):
                    act.wait_ge(up_s, t - 1)
                act.activation(xT[:, u, 0, :], ps[:, u, 0:U * P], ACT.Copy).then_inc(xh_s, 1)

            high_x(0, 0)

            def body(t, q, i, first, last):
                u = q % 2
                if not last:
                    high_x(t + 1, 1 - u)
                e = act.value_load(per_unit(exp_i, t), min_val=0, max_val=E)
                act.wait_ge(up_s, t + 1)
                if not (isinstance(t, int) and t < 2):
                    act.wait_ge(hl_s, t - 1)
                for j in range(FB):
                    ins = act.activation(hid[:, u, j, :], ph[:, u, j, :], ACT.Gelu,
                                         bias=w["up_bias"][:, bass.ds(e, 1), j:j + 1].rearrange("p e j -> p (e j)"))
                ins.then_inc(gl_s, 1)

            run_tiles(act, N, WAYS, body)

        @block.tensor
        def _(pe):
            def turn(t, q, i):
                u = q % 2
                pe.wait_ge(ld[q], 16 * (i + 1))
                if not (isinstance(t, int) and t < 2):
                    pe.wait_ge(xl_s, t - 1)
                for k in range(U):
                    mm = pe.transpose(ps[:, u, k * P:(k + 1) * P], xr[:, q, k, 0:P], w["ident"][:, :])
                mm.then_inc(xT_s, 1)

            def expert(t):
                return pe.value_load(per_unit(exp_i, t), min_val=0, max_val=E)

            def part(k, e, n, size):
                return w["experts"][:, k, bass.ds(e, 1), n:n + size].rearrange("p e n -> p (e n)")

            def up_proj(t, u, e):
                pe.wait_ge(xl_s, t + 1)
                if not (isinstance(t, int) and t < 2):
                    pe.wait_ge(gl_s, t - 1)
                for j in range(FB):
                    pe.matmul(ph[:, u, j, :], part(0, e, j * P, P), xT[:, u, 0, :], start=True, stop=False)
                    pe.matmul(ph[:, u, j, :], part(0, e, j * P, P), xT[:, u, 1, :], start=False, stop=False)
                    mm = pe.matmul(ph[:, u, j, :], part(1, e, j * P, P), xT[:, u, 0, :], start=False, stop=True)
                mm.then_inc(up_s, 1)

            def down_proj(t, q, e):
                u = q % 2
                pe.wait_ge(hl_s, t + 1)
                if not (isinstance(t, int) and t < 2):
                    pe.wait_ge(y_s, t - 1)
                for k in range(U):
                    toks, own = slice(k * P, (k + 1) * P), pd[:, u, k * P:(k + 1) * P]
                    for j in range(FB):
                        hi, lo = (part(n, e, (FB + j) * P, P) for n in range(2))
                        pe.matmul(own, hidp[:, q % 4, 0, j, toks], hi, start=(j == 0), stop=False)
                        pe.matmul(own, hidp[:, q % 4, 0, j, toks], lo, start=False, stop=False)
                        mm = pe.matmul(own, hidp[:, q % 4, 1, j, toks], hi, start=False, stop=(j == FB - 1))
                mm.then_inc(dn_s, 1)

            turn(0, 0, 0)

            def body(t, q, i, first, last):
                u = q % 2
                if not last:
                    turn(t + 1, (q + 1) % WAYS, i + (q == WAYS - 1))
                up_proj(t, u, expert(t))
                if not (isinstance(t, int) and t < 2):
                    down_proj(t - 2, (q - 2) % WAYS, expert(t - 2))

            run_tiles(pe, N, WAYS, body)
            down_proj(N - 2, WAYS - 2, expert(N - 2))
            down_proj(N - 1, WAYS - 1, expert(N - 1))


def shared_block(nc, ctx, w, d, slots, counts, T):
    C = T // Q

    def sem(n):
        return ctx.enter_context(nc.semaphore(n))

    sent = [sem("s_rows_sent0"), sem("s_rows_sent1")]
    up_s, gl_s, hh_s, hl_s, dn_s, out_s, num_s, row_s = (sem(n) for n in (
        "s_up", "s_gelu", "s_hidden_high", "s_hidden_low", "s_down", "s_out", "s_numbered", "s_rows_copied"))
    ids_s = sem("s_numbers_loaded")
    pad_s, padded, step_s, cst = sem("pads_made"), sem("pads_stored"), sem("table_steps"), sem("table_constants")
    CAP = (T + U) * P
    rows, xnT = w["rows"], w["xnT"]
    with ExitStack() as c_:
        def sb(n, s, dt=F32):
            return c_.enter_context(nc.sbuf_tensor(n, s, dt))

        hid, hidp = sb("s_hidden", [P, FB, Q * P]), sb("s_hidden_parts", [P, 2, 2, FB, Q * P], BF16)
        ids, index = sb("s_numbers", [P, T, 2]), sb("s_index", [P, 2, 2, Q], I32)
        row = sb("s_rows", [P, 2, Q, 2, ROW])
        N = units(T)
        pad = sb("pad_row", [P, ROW])
        row_of, used, ti = sb("table_row_of", [1, E]), sb("table_used", [1, E]), sb("table_int", [1, E], I32)
        rows_i, cum = sb("table_first_free", [1, E], I32), sb("table_units_through", [1, E])
        num, bases = sb("table_tile_numbers", [1, N]), sb("region_bases", [1, E])
        past, exp_f, start_f = sb("table_past", [1, N, E]), sb("table_expert", [1, N]), sb("table_start", [1, N])
        real = sb("table_real", [1, N])
        exp_i, start_i = w["unit_expert"], w["unit_start"]
        ph = c_.enter_context(nc.psum_tensor("s_up_psum", [P, FB, Q * P], F32))
        pd = c_.enter_context(nc.psum_tensor("s_down_psum", [P, 2, Q * P], F32))
        block = c_.enter_context(nc.Block())

        @block.sync
        def _(sp):
            sp.dma_start(ids[:, :, :], d["ids"]).then_inc(ids_s, 16)
            sp.dma_start(num[:, :], d["unit_numbers"].unsqueeze(0)).then_inc(cst, 16)
            sp.dma_start(bases[:, :], d["bases"].unsqueeze(0)).then_inc(cst, 16)
            sp.wait_ge(pad_s, 2)
            sp.wait_ge(step_s, 1)
            for e in range(E):
                r = sp.value_load(rows_i[0:1, e:e + 1], min_val=e * CAP, max_val=e * CAP + T * P)
                sp.dma_start(unit_rows(slots, bass.ds(r, U * P)), pad[:, :].unsqueeze(1).to_broadcast([P, U, ROW])).then_inc(padded, 16)
            sp.dma_start(unit_rows(slots, slice(E * CAP, E * CAP + U * P)), pad[:, :].unsqueeze(1).to_broadcast([P, U, ROW])).then_inc(padded, 16)
            sp.wait_ge(padded, 16 * (E + 1))

        @block.gpsimd
        def _(pool):
            def body(c, u, i, first, last):
                pool.wait_ge(num_s, 2 * (c + 1))
                pool.wait_ge(row_s, c + 1)
                hold(pool, w["held_pool"])
                for q in range(Q):
                    for k in range(2):
                        pool.indirect_dma_start(slots, bass.IndirectOffsetOnAxis(index[:, u, k, q:q + 1], 0),
                                                row[:, u, q, k, :], None).then_inc(sent[u], 16)

            run_pairs(pool, C, body)
            for u in range(2):
                pool.wait_ge(sent[u], 16 * Q * C)

        @block.scalar
        def _(act):
            def body(c, u, i, first, last):
                if not (isinstance(c, int) and c < 2):
                    act.wait_ge(sent[u], 16 * 2 * Q * i)
                for k in range(2):
                    ins = act.activation(row[:, u, :, k, 0:P], rows[:, at(c, Q), :], ACT.Copy)
                ins.then_inc(row_s, 1)
                for j in range(FB):
                    act.wait_ge(up_s, c * FB + j + 1)
                    if not first:
                        act.wait_ge(hl_s, (c - 1) * FB + j + 1)
                    act.activation(hid[:, j, :], ph[:, j, :], ACT.Gelu, bias=w["up_bias"][:, E, j:j + 1]).then_inc(gl_s, 1)

            run_pairs(act, C, body)

        @block.vector
        def _(dve):
            def result(c, u):
                dve.wait_ge(dn_s, c + 1)
                dve.tensor_tensor(w["shared"][:, at(c, Q), :], pd[:, u, :].rearrange("p (q n) -> p q n", n=P),
                                  w["down_bias"][:, E:E + 1, :].to_broadcast([P, Q, P]), ALU.add).then_inc(out_s, 1)

            n = 0

            def step(ins):
                nonlocal n
                ins.then_inc(step_s, 1)
                n += 1
                dve.wait_ge(step_s, n)

            dve.memset(pad[:, :], 0.0).then_inc(pad_s, 1)
            dve.wait_ge(pad_s, 1)
            dve.memset(pad[:, P:P + 1].bitcast(I32), NOWHERE).then_inc(pad_s, 1)
            dve.wait_ge(cst, 32)
            own = counts[0:1, :]
            step(dve.tensor_copy(rows_i[:, :], own))
            dve.wait_ge(ids_s, 16)

            def body(c, u, i, first, last):
                if not (isinstance(c, int) and c < 2):
                    dve.wait_ge(sent[u], 16 * 2 * Q * i)
                dve.tensor_copy(index[:, u, :, :], w["dest"][:, :, at(c, Q)]).then_inc(num_s, 1)
                dve.tensor_copy(row[:, u, :, :, P].bitcast(I32), ids[:, at(c, Q), :]).then_inc(num_s, 1)
                for j in range(FB):
                    dve.wait_ge(gl_s, c * FB + j + 1)
                    if j == 0 and not (isinstance(c, int) and c < 2):
                        dve.wait_ge(dn_s, c - 1)
                    dve.tensor_copy(hidp[:, u, 0, j, :], hid[:, j, :]).then_inc(hh_s, 1)
                    dve.wait_ge(hh_s, c * FB + j + 1)
                    dve.tensor_tensor(hidp[:, u, 1, j, :], hid[:, j, :], hidp[:, u, 0, j, :], ALU.subtract).then_inc(hl_s, 1)
                if not first:
                    result(c - 1, 1 - u)

            run_pairs(dve, C, body)
            result(C - 1, 1)
            step(dve.tensor_tensor(used[:, :], own, bases[:, :], ALU.subtract))
            step(dve.tensor_scalar(used[:, :], used[:, :], float(U * P - 1), None, ALU.add))
            step(dve.tensor_copy(ti[:, :], used[:, :]))
            step(dve.tensor_scalar(ti[:, :], ti[:, :], (U * P).bit_length() - 1, None, ALU.arith_shift_right))
            step(dve.tensor_copy(used[:, :], ti[:, :]))
            step(dve.tensor_scalar(row_of[:, :], used[:, :], 0.0, None, ALU.mult))
            step(dve.tensor_tensor_scan(cum[:, :], used[:, :], row_of[:, :], 0.0, ALU.add, ALU.add))
            step(dve.tensor_tensor(past[:, :, :], num[:, :].unsqueeze(2).to_broadcast([1, N, E]),
                                   cum[:, :].unsqueeze(1).to_broadcast([1, N, E]), ALU.is_ge))
            step(dve.tensor_reduce(exp_f[:, :], past[:, :, :], X, ALU.add))
            step(dve.tensor_tensor(past[:, :, :], past[:, :, :], used[:, :].unsqueeze(1).to_broadcast([1, N, E]), ALU.mult))
            step(dve.tensor_reduce(start_f[:, :], past[:, :, :], X, ALU.add))
            step(dve.tensor_tensor(start_f[:, :], num[:, :], start_f[:, :], ALU.subtract))
            step(dve.tensor_scalar(real[:, :], exp_f[:, :], float(E), float(U * P), ALU.is_lt, ALU.mult))
            step(dve.tensor_tensor(start_f[:, :], start_f[:, :], real[:, :], ALU.mult))
            step(dve.scalar_tensor_tensor(start_f[:, :], exp_f[:, :], float(CAP), start_f[:, :], ALU.mult, ALU.add))
            step(dve.tensor_copy(exp_i[:, :], exp_f[:, :]))
            step(dve.tensor_copy(start_i[:, :], start_f[:, :]))

        @block.tensor
        def _(pe):
            def down_proj(c, u):
                pe.wait_ge(hl_s, (c + 1) * FB)
                if not (isinstance(c, int) and c < 2):
                    pe.wait_ge(out_s, c - 1)
                for q in range(Q):
                    toks, own = slice(q * P, (q + 1) * P), pd[:, u, q * P:(q + 1) * P]
                    for j in range(FB):
                        cols = slice((FB + j) * P, (FB + j + 1) * P)
                        hi, lo = w["experts"][:, 0, E, cols], w["experts"][:, 1, E, cols]
                        pe.matmul(own, hidp[:, u, 0, j, toks], hi, start=(j == 0), stop=False)
                        pe.matmul(own, hidp[:, u, 0, j, toks], lo, start=False, stop=False)
                        mm = pe.matmul(own, hidp[:, u, 1, j, toks], hi, start=False, stop=(j == FB - 1))
                mm.then_inc(dn_s, 1)

            def body(c, u, i, first, last):
                toks = at(c, Q * P)
                for j in range(FB):
                    cols = slice(j * P, (j + 1) * P)
                    hi, lo = w["experts"][:, 0, E, cols], w["experts"][:, 1, E, cols]
                    if not first:
                        pe.wait_ge(gl_s, (c - 1) * FB + j + 1)
                    pe.matmul(ph[:, j, :], hi, xnT[:, 0, toks], start=True, stop=False)
                    pe.matmul(ph[:, j, :], hi, xnT[:, 1, toks], start=False, stop=False)
                    pe.matmul(ph[:, j, :], lo, xnT[:, 0, toks], start=False, stop=True).then_inc(up_s, 1)
                if not first:
                    down_proj(c - 1, 1 - u)

            run_pairs(pe, C, body)
            down_proj(C - 1, 1)


def combine_block(nc, ctx, w, d, results, gates, out, T):
    C = T // Q

    def sem(n):
        return ctx.enter_context(nc.semaphore(n))

    W = 4
    ld = [sem(f"c_results_loaded{v}") for v in range(W)]
    st = [sem(f"c_out_stored{v}") for v in range(W)]
    a_s, shared_s, b_s, top_s, inv_s, scaled, fin = (sem(n) for n in (
        "c_first", "c_shared_added", "c_second_added", "c_top_steps", "c_top_inverted", "c_scaled", "c_final"))
    with ExitStack() as c_:
        def sb(n, s, dt=F32):
            return c_.enter_context(nc.sbuf_tensor(n, s, dt))

        res, acc, part = sb("c_results", [P, W, Q, 2, P]), sb("c_acc", [P, 2, Q, P]), sb("c_part", [P, 2, Q, P])
        top, o = sb("c_top", [P, 2, Q]), sb("c_out", [P, W, Q, P])
        block = c_.enter_context(nc.Block())

        def tiles(x, c):
            return x[at(c, Q * P)]

        @block.sync
        def _(sp):
            def load(c, v):
                sp.dma_start(res[:, v, :, :, :], tiles(results.rearrange("(n k) d -> n k d", k=2), c)
                             .rearrange("(q p) k n -> p q k n", p=P)).then_inc(ld[v], 16)

            for c in range(W):
                load(c, c)

            def body(c, v, i, first, last):
                if not (isinstance(c, int) and c + W >= C):
                    sp.wait_ge(b_s, c + 1)
                    load(c + W, v)
                sp.wait_ge(fin, c + 1)
                sp.dma_start(tiles(out, c).rearrange("(q p) n -> p q n", p=P), o[:, v, :, :]).then_inc(st[v], 16)

            run_tiles(sp, C, W, body)
            for v in range(W):
                sp.wait_ge(st[v], 16 * (C // W))

        def gate(c, q, k):
            if isinstance(c, int):
                return gates[:, c * Q + q, k:k + 1]
            return gates[:, bass.ds(c * Q + q, 1), k:k + 1].rearrange("p t k -> p (t k)")

        @block.scalar
        def _(act):
            def scale_out(c, v, i):
                u = v % 2
                if not (isinstance(c, int) and c < W):
                    act.wait_ge(st[v], 16 * i)
                act.wait_ge(inv_s, c + 1)
                for q in range(Q):
                    ins = act.activation(o[:, v, q, :], acc[:, u, q, :], ACT.Copy, scale=top[:, u, q:q + 1])
                ins.then_inc(scaled, 1)

            def body(c, v, i, first, last):
                u = v % 2
                act.wait_ge(ld[v], 16 * (i + 1))
                if not (isinstance(c, int) and c < 2):
                    act.wait_ge(b_s, c - 1)
                for q in range(Q):
                    ins = act.activation(part[:, u, q, :], res[:, v, q, 0, :], ACT.Copy, scale=gate(c, q, 0))
                ins.then_inc(a_s, 1)
                if not first:
                    scale_out(c - 1, (v - 1) % W, i - (v == 0))

            run_tiles(act, C, W, body)
            scale_out(C - 1, W - 1, C // W - 1)

        @block.gpsimd
        def _(pool):
            def add_x2(c, v):
                pool.wait_ge(scaled, c + 1)
                pool.tensor_tensor(o[:, v, :, :], o[:, v, :, :], w["x2"][:, at(c, Q), :], ALU.add).then_inc(fin, 1)

            def body(c, v, i, first, last):
                u = v % 2
                pool.wait_ge(a_s, c + 1)
                pool.tensor_tensor(part[:, u, :, :], part[:, u, :, :], w["shared"][:, at(c, Q), :], ALU.add).then_inc(shared_s, 1)
                if not first:
                    add_x2(c - 1, (v - 1) % W)

            run_tiles(pool, C, W, body)
            add_x2(C - 1, W - 1)

        @block.vector
        def _(dve):
            def body(c, v, i, first, last):
                u = v % 2
                dve.wait_ge(shared_s, c + 1)
                if not (isinstance(c, int) and c < 2):
                    dve.wait_ge(scaled, c - 1)
                for q in range(Q):
                    ins = dve.scalar_tensor_tensor(acc[:, u, q, :], res[:, v, q, 1, :], gate(c, q, 1), part[:, u, q, :], ALU.mult, ALU.add)
                ins.then_inc(b_s, 1)
                dve.wait_ge(b_s, c + 1)
                dve.tensor_reduce(top[:, u, :], acc[:, u, :, :], X, ALU.max, apply_absolute_value=True).then_inc(top_s, 1)
                dve.wait_ge(top_s, 2 * c + 1)
                dve.tensor_scalar(top[:, u, :], top[:, u, :], 1e-5, None, ALU.add).then_inc(top_s, 1)
                dve.wait_ge(top_s, 2 * c + 2)
                dve.reciprocal(top[:, u, :], top[:, u, :]).then_inc(inv_s, 1)

            run_tiles(dve, C, W, body)


def build(nc, a, out, T):
    with ExitStack() as ctx:
        def keep(n, s, dt=F32, stack=ctx):
            return stack.enter_context(nc.sbuf_tensor(n, s, dt))

        def scratch(n, s, dt=F32):
            return nc.dram_tensor(n, s, dt).ap()

        ft, mtab = scratch("features_dram", [T, P, BANK]), scratch("key_table_dram", [2 * T, S * NB])
        x2d = scratch("x2_dram", [T * P, P])
        slots = scratch("slots_dram", [(E * (T + U) + U) * P, ROW])
        results = scratch("results_dram", [2 * T * P, P])
        w = {
            "ident": keep("identity_sb", [P, P]), "ones": keep("ones", [P, P], BF16),
            "minus_half": keep("minus_half", [P, 1]), "quarter": keep("quarter_turn", [P, 1]),
        }
        w["held_dve"], w["held_pool"] = (ctx.enter_context(nc.semaphore(n)) for n in ("held_dve", "held_pool"))
        gates, counts = keep("gates", [P, T, 2]), keep("rows_through", [P, E])
        with ExitStack() as attention:
            def keep_for_attention(n, s, dt=F32):
                return keep(n, s, dt, attention)

            w["kron"] = keep_for_attention("gate_weights_spread", [P, 16 * H])
            w["split"] = keep_for_attention("projection_parts", [P, 4, 2, H * DK], BF16)
            w["brows"] = keep_for_attention("bias_parts", [P, 2 * H * DK + 16 * H], BF16)
            w["ybias"] = keep_for_attention("out_bias", [P, P])
            w["qbd"] = keep_for_attention("q_block_diagonal", [P, H, P])
            w["pbd"] = keep_for_attention("probs_block_diagonal", [P, H, P])
            w["v"] = keep_for_attention("values", [P, H, DK])
            w["centres"] = keep_for_attention("centres", [P, T, 2])
            w["sizes"], w["inverse_sizes"] = keep_for_attention("box_sizes", [P, T, 2]), keep_for_attention("inverse_sizes", [P, T, 2])
            setup_block(nc, ctx, w, a, mtab, T)
            relations_block(nc, ctx, w, a, ft, mtab, T)
            attention_block(nc, ctx, w, a, ft, x2d, T)
        w["experts"] = keep("expert_parts", [P, 2, E + 1, 2 * FB * P], BF16)
        w["up_bias"], w["down_bias"] = keep("up_biases", [P, E + 1, FB]), keep("down_biases", [P, E + 1, P])
        w["unit_expert"], w["unit_start"] = keep("unit_expert", [1, units(T)], I32), keep("unit_start", [1, units(T)], I32)
        w["x2"], w["shared"] = keep("x2_sb", [P, T, P]), keep("shared_results", [P, T, P])
        with ExitStack() as dispatch:
            w["rows"] = keep("normed_rows", [P, T, P], F32, dispatch)
            w["xnT"] = keep("normed_turned", [P, 2, T * P], BF16, dispatch)
            w["dest"] = keep("rows_to_fill", [P, 2, T], I32, dispatch)
            with ExitStack() as choice:
                w["logits"] = keep("expert_logits", [P, T, E], F32, choice)
                w["raw_shared"] = keep("shared_expert_raw", [P, 1, 2 * FB * P], F32, choice)
                norm_block(nc, ctx, w, a, x2d, T)
                dispatch_block(nc, ctx, w, a, gates, counts, T)
            shared_block(nc, ctx, w, a, slots, counts, T)
        routed_block(nc, ctx, w, a, slots, results, T)
        combine_block(nc, ctx, w, a, results, gates, out, T)


def kernel(**inputs):
    import numpy as np
    import concourse.bacc as bacc
    from concourse.bass_utils import run_bass_kernel_spmd as run

    g = {k.replace("L0_xattn_", "").replace("L0_ffn_", "f_"): np.asarray(v) for k, v in inputs.items()}
    tokens = g["x"].shape[0] * g["x"].shape[1]
    kron = np.zeros((16, NF, 16, H), np.float32)
    for m in range(16):
        kron[m, :, m, :] = g["Wg"].T
    bf = np.concatenate
    lay = {
        "x": g["x"].reshape(tokens, P), "ctxT": g["ctx_1024"].reshape(tokens, P).T,
        "boxes": g["fside_BxSx4_0"].reshape(tokens, NB),
        "wq": g["Wq"].T, "wk": g["Wk"].T, "wv": g["Wv"].T,
        "wo": g["Wo"].T.reshape(HP, P, P).transpose(1, 0, 2).reshape(P, H * DK),
        "bv": g["bv"].reshape(HP, P).T, "bo": g["bo"],
        "bias_rows": bf([g["bq"], g["bk"], np.tile(g["bg"], 16)]),
        "kron": kron.reshape(P, 16 * H), "ident": np.eye(P, dtype=np.float32),
        "gate_w": g["f_gate_w"], "gate_b": g["f_bias"], "numbers": np.arange(E, dtype=np.float32) - E,
        "bases": np.arange(E, dtype=np.float32) * (tokens + U * P),
        "ids": (2 * (np.arange(tokens // P)[None, :, None] * P + np.arange(P)[:, None, None]) + np.arange(2)).astype(np.float32),
        "unit_numbers": np.arange(2 * tokens // P // U + E, dtype=np.float32),
        "up": bf([g["f_up_w"], g["f_sw_up"][None]]), "down": bf([g["f_down_w"], g["f_sw_down"][None]]),
        "up_b": bf([g["f_up_b"], g["f_sb_up"][None]]).reshape(E + 1, FB, P).transpose(2, 0, 1),
        "down_b": bf([g["f_down_b"], g["f_sb_down"][None]]),
    }
    nc = bacc.Bacc("TRN2", target_bir_lowering=False, num_devices=1)
    arrays, a = {}, {}
    for n, v in lay.items():
        arrays["in_" + n] = np.ascontiguousarray(v)
        a[n] = nc.dram_tensor("in_" + n, v.shape, F32, kind="ExternalInput").ap()
    out = nc.dram_tensor("out", (tokens, P), F32, kind="ExternalOutput").ap()
    build(nc, a, out, tokens // P)
    r = run(nc, [arrays], core_ids=[0])
    return r.results[0]["out"].reshape(g["x"].shape)
```
